# Optimizing a Trainium2 kernel written in Bass

```python
import numpy as np
import jax
import jax.numpy as jnp

def _softmax(x, axis=-1):
    return jax.nn.softmax(x, axis=axis)

def _gelu(x):
    return jax.nn.gelu(x, approximate=True)

def _silu(x):
    return jax.nn.silu(x)

def _sigmoid(x):
    return jax.nn.sigmoid(x)

def _layernorm(x, axis=-1, eps=1e-05):
    m = jnp.mean(x, axis=axis, keepdims=True)
    v = jnp.var(x, axis=axis, keepdims=True)
    return (x - m) / jnp.sqrt(v + eps)

def _scatter_add(tgt, idx, src, axis=0):
    return tgt.at[idx].add(src)

def _segment_sum(src, seg, n):
    return jax.ops.segment_sum(src, seg, n)
kernel_name = 'mk_xattn_ffn_d2_seqx_r8_896e18'

def setup_inputs(seed: int=0):
    np.random.seed(seed)
    _w = jnp.asarray

    def _rec_inputs():
        import jax
        import jax.numpy as jnp
        _rk = jax.random.key(seed)
        x = -0.0002928 + 1 * jax.random.normal(jax.random.fold_in(_rk, 1), (16, 128, 128), jnp.float32)
        _lenS = 128 - jax.random.randint(jax.random.fold_in(_rk, 7), (16,), 0, max(1, 128 // 4) + 1, jnp.int32)
        _lenS2 = 128 - jax.random.randint(jax.random.fold_in(_rk, 8), (16,), 0, max(1, 128 // 4) + 1, jnp.int32)
        _ctx_1024P = jax.random.normal(jax.random.fold_in(_rk, 11), (16, 16, 128), jnp.float32)
        _ctx_1024c = jax.random.dirichlet(jax.random.fold_in(_rk, 511), 0.3 * jnp.ones((16,), jnp.float32), (16, 128))
        _ctx_1024t = jnp.einsum('bsk,bkd->bsd', _ctx_1024c, _ctx_1024P)
        _ctx_1024t = _ctx_1024t * jax.lax.rsqrt(jnp.mean(jnp.square(_ctx_1024t)) + 1e-12) * 0.953939
        ctx_1024 = -1.39393e-06 + 0.999914 * (_ctx_1024t + 0.3 * jax.random.normal(jax.random.fold_in(_rk, 611), (16, 128, 128), jnp.float32))
        return (x, ctx_1024)
    x, ctx_1024 = _rec_inputs()

    def _L0_xattn_setup():
        import jax, jax.numpy as jnp
        import numpy as np
        H, DK, DV = (16, 64, 64)
        MEM = 128
        D_MODEL = 128
        OUT_DIM = 128
        key = jax.random.key(seed)
        ks = jax.random.split(key, 12)
        B, S = (2, 256)
        scale = 1.0 / np.sqrt(D_MODEL)
        inp = {'queries': jax.random.normal(ks[0], (B, S, D_MODEL), jnp.float32), 'keys': jax.random.normal(ks[1], (B, S, D_MODEL), jnp.float32), 'values': jax.random.normal(ks[2], (B, S, D_MODEL), jnp.float32), 'wq_w': jax.random.normal(ks[3], (D_MODEL, H * DK), jnp.float32) * scale, 'wq_b': jnp.zeros((H * DK,), jnp.float32), 'wk_w': jax.random.normal(ks[4], (D_MODEL, H * DK), jnp.float32) * scale, 'wk_b': jnp.zeros((H * DK,), jnp.float32), 'wv_w': jax.random.normal(ks[5], (D_MODEL, H * DV), jnp.float32) * scale, 'wv_b': jnp.zeros((H * DV,), jnp.float32), 'mk': jax.random.normal(ks[6], (1, MEM, H * DK), jnp.float32) * (0.1 / DK), 'mv': jax.random.normal(ks[7], (1, MEM, H * DV), jnp.float32) * (0.1 / MEM), 'wo_w': jax.random.normal(ks[8], (H * DV, OUT_DIM), jnp.float32) * (1.0 / np.sqrt(H * DV)), 'wo_b': jnp.zeros((OUT_DIM,), jnp.float32)}
        return inp
    _L0_xattn_all = _L0_xattn_setup()
    _L0_xattn_in = {k: v for k, v in _L0_xattn_all.items() if k in ('wq_w', 'wq_b', 'wk_w', 'wk_b', 'wv_w', 'wv_b', 'mk', 'mv', 'wo_w', 'wo_b')}
    del _L0_xattn_all

    def _L0_ffn_setup():
        import jax, jax.numpy as jnp
        import numpy as np
        B, S, H, F, G = (8, 256, 128, 512, 128)
        EPS = 1e-05

        def _dequant(q, scales, g):
            K, N = q.shape
            w = (q.astype(jnp.float32) - 128.0).reshape(K // g, g, N) * scales[:, None, :]
            return w.reshape(K, N)
        key = jax.random.key(seed)
        ks = jax.random.split(key, 8)
        x = jax.random.normal(ks[0], (B, S, H), dtype=jnp.float32)
        ln_gamma = jnp.ones((H,), jnp.float32)
        ln_beta = jnp.zeros((H,), jnp.float32)
        fc1_q = jax.random.randint(ks[1], (H, F), 0, 32, dtype=jnp.int32)
        fc2_q = jax.random.randint(ks[2], (F, H), 0, 32, dtype=jnp.int32)
        fc1_scales = jax.random.uniform(ks[3], (H // G, F), jnp.float32) * 0.02 + 0.001
        fc2_scales = jax.random.uniform(ks[4], (F // G, H), jnp.float32) * 0.02 + 0.001
        fc1_bias = jax.random.normal(ks[5], (F,), jnp.float32) * 0.02
        fc2_bias = jax.random.normal(ks[6], (H,), jnp.float32) * 0.02
        return {'x': x, 'ln_gamma': ln_gamma, 'ln_beta': ln_beta, 'fc1_q': fc1_q, 'fc1_scales': fc1_scales, 'fc1_bias': fc1_bias, 'fc2_q': fc2_q, 'fc2_scales': fc2_scales, 'fc2_bias': fc2_bias}
    _L0_ffn_all = _L0_ffn_setup()
    _L0_ffn_in = {k: v for k, v in _L0_ffn_all.items() if k in ('ln_gamma', 'ln_beta', 'fc1_q', 'fc1_scales', 'fc1_bias', 'fc2_q', 'fc2_scales', 'fc2_bias')}
    del _L0_ffn_all

    def _L1_xattn_setup():
        import jax, jax.numpy as jnp
        import numpy as np
        EMBED = 128
        ATTN = 128
        HEADS = 16
        HEAD_DIM = ATTN // HEADS
        key = jax.random.key(seed)
        ks = jax.random.split(key, 8)
        s = 1.0 / np.sqrt(EMBED)
        sa = 1.0 / np.sqrt(ATTN)
        return {'queries': jax.random.normal(ks[0], (4, 64, EMBED), jnp.float32), 'context': jax.random.normal(ks[1], (4, 256, EMBED), jnp.float32), 'Wq': jax.random.normal(ks[2], (EMBED, ATTN), jnp.float32) * s, 'bq': jnp.zeros((ATTN,), jnp.float32), 'Wkv': jax.random.normal(ks[3], (EMBED, 2 * ATTN), jnp.float32) * s, 'bkv': jnp.zeros((2 * ATTN,), jnp.float32), 'Wo': jax.random.normal(ks[4], (ATTN, EMBED), jnp.float32) * sa, 'bo': jnp.zeros((EMBED,), jnp.float32)}
    _L1_xattn_all = _L1_xattn_setup()
    _L1_xattn_in = {k: v for k, v in _L1_xattn_all.items() if k in ('Wq', 'bq', 'Wkv', 'bkv', 'Wo', 'bo')}
    del _L1_xattn_all

    def _L1_ffn_setup():
        import jax, jax.numpy as jnp
        import numpy as np
        B, S, H = (4, 256, 128)
        E, K = (8, 2)
        I_R, I_S = (4 * H, 8 * H)
        CAP_FACTOR = 1.25
        SCALE = 1.0
        key = jax.random.key(seed)
        ks = jax.random.split(key, 9)
        std = 0.02
        return {'x': jax.random.normal(ks[0], (B, S, H), jnp.float32), 'router_w': std * jax.random.normal(ks[1], (E, H), jnp.float32), 'rg': std * jax.random.normal(ks[2], (E, H, I_R), jnp.float32), 'ru': std * jax.random.normal(ks[3], (E, H, I_R), jnp.float32), 'rd': std * jax.random.normal(ks[4], (E, I_R, H), jnp.float32), 'sg': std * jax.random.normal(ks[5], (H, I_S), jnp.float32), 'su': std * jax.random.normal(ks[6], (H, I_S), jnp.float32), 'sd': std * jax.random.normal(ks[7], (I_S, H), jnp.float32)}
    _L1_ffn_all = _L1_ffn_setup()
    _L1_ffn_in = {k: v for k, v in _L1_ffn_all.items() if k in ('router_w', 'rg', 'ru', 'rd', 'sg', 'su', 'sd')}
    del _L1_ffn_all
    return {'x': x, 'ctx_1024': ctx_1024, 'L0_xattn_wq_w': _L0_xattn_in['wq_w'], 'L0_xattn_wq_b': _L0_xattn_in['wq_b'], 'L0_xattn_wk_w': _L0_xattn_in['wk_w'], 'L0_xattn_wk_b': _L0_xattn_in['wk_b'], 'L0_xattn_wv_w': _L0_xattn_in['wv_w'], 'L0_xattn_wv_b': _L0_xattn_in['wv_b'], 'L0_xattn_mk': _L0_xattn_in['mk'], 'L0_xattn_mv': _L0_xattn_in['mv'], 'L0_xattn_wo_w': _L0_xattn_in['wo_w'], 'L0_xattn_wo_b': _L0_xattn_in['wo_b'], 'L0_ffn_ln_gamma': _L0_ffn_in['ln_gamma'], 'L0_ffn_ln_beta': _L0_ffn_in['ln_beta'], 'L0_ffn_fc1_q': _L0_ffn_in['fc1_q'], 'L0_ffn_fc1_scales': _L0_ffn_in['fc1_scales'], 'L0_ffn_fc1_bias': _L0_ffn_in['fc1_bias'], 'L0_ffn_fc2_q': _L0_ffn_in['fc2_q'], 'L0_ffn_fc2_scales': _L0_ffn_in['fc2_scales'], 'L0_ffn_fc2_bias': _L0_ffn_in['fc2_bias'], 'L1_xattn_Wq': _L1_xattn_in['Wq'], 'L1_xattn_bq': _L1_xattn_in['bq'], 'L1_xattn_Wkv': _L1_xattn_in['Wkv'], 'L1_xattn_bkv': _L1_xattn_in['bkv'], 'L1_xattn_Wo': _L1_xattn_in['Wo'], 'L1_xattn_bo': _L1_xattn_in['bo'], 'L1_ffn_router_w': _L1_ffn_in['router_w'], 'L1_ffn_rg': _L1_ffn_in['rg'], 'L1_ffn_ru': _L1_ffn_in['ru'], 'L1_ffn_rd': _L1_ffn_in['rd'], 'L1_ffn_sg': _L1_ffn_in['sg'], 'L1_ffn_su': _L1_ffn_in['su'], 'L1_ffn_sd': _L1_ffn_in['sd']}

def reference(x, ctx_1024, L0_xattn_wq_w, L0_xattn_wq_b, L0_xattn_wk_w, L0_xattn_wk_b, L0_xattn_wv_w, L0_xattn_wv_b, L0_xattn_mk, L0_xattn_mv, L0_xattn_wo_w, L0_xattn_wo_b, L0_ffn_ln_gamma, L0_ffn_ln_beta, L0_ffn_fc1_q, L0_ffn_fc1_scales, L0_ffn_fc1_bias, L0_ffn_fc2_q, L0_ffn_fc2_scales, L0_ffn_fc2_bias, L1_xattn_Wq, L1_xattn_bq, L1_xattn_Wkv, L1_xattn_bkv, L1_xattn_Wo, L1_xattn_bo, L1_ffn_router_w, L1_ffn_rg, L1_ffn_ru, L1_ffn_rd, L1_ffn_sg, L1_ffn_su, L1_ffn_sd):
    import jax
    import jax.numpy as jnp

    def _L0_xattn_ref(queries, keys, values, wq_w, wq_b, wk_w, wk_b, wv_w, wv_b, mk, mv, wo_w, wo_b):
        import jax, jax.numpy as jnp
        import numpy as np
        H, DK, DV = (16, 64, 64)
        MEM = 128
        D_MODEL = 128
        OUT_DIM = 128
        B, S, _ = queries.shape
        q = (queries @ wq_w + wq_b).reshape(B, S, H, DK).transpose(0, 2, 1, 3)
        k_proj = keys @ wk_w + wk_b
        v_proj = values @ wv_w + wv_b
        k_ext = jnp.concatenate([k_proj, jnp.broadcast_to(mk, (B, MEM, H * DK))], axis=1)
        v_ext = jnp.concatenate([v_proj, jnp.broadcast_to(mv, (B, MEM, H * DV))], axis=1)
        T = S + MEM
        k = k_ext.reshape(B, T, H, DK).transpose(0, 2, 1, 3)
        v = v_ext.reshape(B, T, H, DV).transpose(0, 2, 1, 3)
        scores = jnp.einsum('bhsd,bhtd->bhst', q, k) / jnp.sqrt(jnp.float32(DK))
        attn = jax.nn.softmax(scores, axis=-1)
        out = jnp.einsum('bhst,bhtd->bhsd', attn, v)
        out = out.transpose(0, 2, 1, 3).reshape(B, S, H * DV)
        return out @ wo_w + wo_b

    def _L0_ffn_ref(x, ln_gamma, ln_beta, fc1_q, fc1_scales, fc1_bias, fc2_q, fc2_scales, fc2_bias):
        import jax, jax.numpy as jnp
        import numpy as np
        B, S, H, F, G = (8, 256, 128, 512, 128)
        EPS = 1e-05

        def _dequant(q, scales, g):
            K, N = q.shape
            w = (q.astype(jnp.float32) - 128.0).reshape(K // g, g, N) * scales[:, None, :]
            return w.reshape(K, N)
        residual = x
        mu = jnp.mean(x, axis=-1, keepdims=True)
        var = jnp.mean(jnp.square(x - mu), axis=-1, keepdims=True)
        h = (x - mu) * jax.lax.rsqrt(var + EPS) * ln_gamma + ln_beta
        hf = h.reshape(-1, H)
        w1 = _dequant(fc1_q, fc1_scales, G)
        y = hf @ w1 + fc1_bias
        y = jax.nn.silu(y)
        w2 = _dequant(fc2_q, fc2_scales, G)
        z = y @ w2 + fc2_bias
        return residual + 0.5 * z.reshape(residual.shape)

    def _L1_xattn_ref(queries, context, Wq, bq, Wkv, bkv, Wo, bo):
        import jax, jax.numpy as jnp
        import numpy as np
        EMBED = 128
        ATTN = 128
        HEADS = 16
        HEAD_DIM = ATTN // HEADS
        B, Lq, _ = queries.shape
        Lk = context.shape[1]
        q = queries @ Wq + bq
        kv = context @ Wkv + bkv
        k, v = jnp.split(kv, 2, axis=-1)
        q = q.reshape(B, Lq, HEADS, HEAD_DIM)
        k = k.reshape(B, Lk, HEADS, HEAD_DIM)
        v = v.reshape(B, Lk, HEADS, HEAD_DIM)
        scale = 1.0 / np.sqrt(HEAD_DIM)
        scores = jnp.einsum('bqhd,bkhd->bhqk', q, k) * scale
        attn = jax.nn.softmax(scores, axis=-1)
        x = jnp.einsum('bhqk,bkhd->bqhd', attn, v).reshape(B, Lq, ATTN)
        return x @ Wo + bo

    def _L1_ffn_ref(x, router_w, rg, ru, rd, sg, su, sd):
        import jax, jax.numpy as jnp
        import numpy as np
        B, S, H = (4, 256, 128)
        E, K = (8, 2)
        I_R, I_S = (4 * H, 8 * H)
        CAP_FACTOR = 1.25
        SCALE = 1.0
        b, s, h = x.shape
        T = b * s
        capacity = max(int(CAP_FACTOR * T / E), 1)
        xf = x.reshape(T, h)
        eps = jnp.finfo(x.dtype).eps
        xn = xf * jax.lax.rsqrt(jnp.mean(xf * xf, axis=-1, keepdims=True) + eps)
        logits = xn @ router_w.T
        probs = jax.nn.softmax(logits, axis=-1)
        topk_p, topk_i = jax.lax.top_k(probs, K)
        rw = topk_p / jnp.sum(topk_p, axis=-1, keepdims=True)
        one_hot = jax.nn.one_hot(topk_i, E, dtype=x.dtype)
        mask = one_hot.sum(1)
        wdense = (one_hot * rw[..., None]).sum(1)
        sel = mask.T.astype(bool)
        order = jnp.argsort(~sel, axis=1, stable=True)
        dispatch = order[:, :capacity]
        count = sel.sum(axis=1)
        valid = (jnp.arange(capacity)[None, :] < count[:, None]).astype(x.dtype)
        xg = xf[dispatch]
        gate = jax.nn.silu(jnp.einsum('ech,ehi->eci', xg, rg))
        up = jnp.einsum('ech,ehi->eci', xg, ru)
        eout = jnp.einsum('eci,eih->ech', gate * up, rd)
        w = jnp.take_along_axis(wdense.T, dispatch, axis=1)
        contrib = eout * (w * valid)[..., None]
        routed = jnp.zeros_like(xf).at[dispatch.reshape(-1)].add(contrib.reshape(-1, h))
        shared = jax.nn.silu(x @ sg) * (x @ su) @ sd
        return shared + SCALE * routed.reshape(b, s, h)
    x = x + _L0_xattn_ref(_layernorm(x, axis=-1), ctx_1024, ctx_1024, L0_xattn_wq_w, L0_xattn_wq_b, L0_xattn_wk_w, L0_xattn_wk_b, L0_xattn_wv_w, L0_xattn_wv_b, L0_xattn_mk, L0_xattn_mv, L0_xattn_wo_w, L0_xattn_wo_b)
    x = x + _L0_ffn_ref(_layernorm(x, axis=-1), L0_ffn_ln_gamma, L0_ffn_ln_beta, L0_ffn_fc1_q, L0_ffn_fc1_scales, L0_ffn_fc1_bias, L0_ffn_fc2_q, L0_ffn_fc2_scales, L0_ffn_fc2_bias)
    x = x + _L1_xattn_ref(_layernorm(x, axis=-1), ctx_1024, L1_xattn_Wq, L1_xattn_bq, L1_xattn_Wkv, L1_xattn_bkv, L1_xattn_Wo, L1_xattn_bo)
    x = x + _L1_ffn_ref(_layernorm(x, axis=-1), L1_ffn_router_w, L1_ffn_rg, L1_ffn_ru, L1_ffn_rd, L1_ffn_sg, L1_ffn_su, L1_ffn_sd)
    return x

_drawn_inputs = setup_inputs


def setup_inputs(seed=0):
    import zlib

    import numpy as np

    out = dict(_drawn_inputs(seed))
    spreads = {'L0_xattn_wq_b': (0.0, 0.519),
     'L0_xattn_wk_b': (0.0, 0.686),
     'L0_xattn_wv_b': (0.0, 0.1),
     'L0_xattn_wo_b': (0.0, 0.1),
     'L0_ffn_ln_gamma': (1.0, 0.2),
     'L0_ffn_ln_beta': (0.0, 0.1),
     'L1_xattn_bq': (0.0, 2.0),
     'L1_xattn_bkv': (0.0, 2.0),
     'L1_xattn_bo': (0.0, 2.0)}
    factors = {'L0_xattn_mk': 64.0,
     'L0_xattn_mv': 64.0,
     'L0_ffn_fc1_scales': 12.078,
     'L0_ffn_fc1_bias': 64.0,
     'L0_ffn_fc2_bias': 64.0,
     'L1_xattn_Wq': 8.0,
     'L1_xattn_Wkv': 8.0,
     'L1_xattn_Wo': 8.0,
     'L1_ffn_router_w': 64.0,
     'L1_ffn_rg': 64.0,
     'L1_ffn_ru': 64.0,
     'L1_ffn_rd': 64.0,
     'L1_ffn_sg': 64.0,
     'L1_ffn_su': 64.0,
     'L1_ffn_sd': 64.0}
    for name, (base, spread) in spreads.items():
        noise = np.random.default_rng([zlib.crc32(name.encode()), seed]).standard_normal(out[name].shape)
        drawn = base * np.exp(spread * noise) if base else spread * noise
        out[name] = jnp.asarray(drawn.astype(out[name].dtype))
    for name, factor in factors.items():
        out[name] = (out[name] * factor).astype(out[name].dtype)
    return out
```

```python
from contextlib import ExitStack

import concourse.bass as bass
from concourse import mybir

ALU = mybir.AluOpType
ACT = mybir.ActivationFunctionType
F32 = mybir.dt.float32
F32R = mybir.dt.float32r
I32 = mybir.dt.int32
U32 = mybir.dt.uint32
BF16 = mybir.dt.bfloat16
AX_X = mybir.AxisListType.X

P = 128


class Shared:
    pass


def at_least(engine, semaphore, value):
    if not (isinstance(value, int) and value <= 0):
        engine.wait_ge(semaphore, value)


class Chain:

    def __init__(self, engine, semaphore):
        self.engine, self.semaphore, self.count = engine, semaphore, 0
        self.turn, self.start, self.each = None, 0, 0

    def loop(self, turn, first, each):
        self.turn, self.start, self.each = turn, self.count - first * each, each
        self.count = 0

    def end(self, last):
        assert self.count == self.each, (self.count, self.each)
        self.count = self.start + last * self.each
        self.turn = None

    def add(self, instruction):
        instruction.then_inc(self.semaphore, 1)
        self.count += 1
        return self

    def wait(self):
        if self.turn is None:
            self.engine.wait_ge(self.semaphore, self.count)
        else:
            self.engine.wait_ge(self.semaphore, self.turn * self.each + (self.start + self.count))


def inverse_root(dve, chain, y, variance, eps, tmp):
    v, t = tmp[:, 0, :], tmp[:, 1, :]
    yi, ti = y.bitcast(I32), t.bitcast(I32)
    chain.add(dve.tensor_scalar(v, variance, eps, None, ALU.add)).wait()
    chain.add(dve.tensor_scalar(ti, v.bitcast(I32), 1, None, ALU.logical_shift_right)).wait()
    chain.add(dve.tensor_scalar(yi, ti, -1.0, float(0x5F3759DF), ALU.mult, ALU.add)).wait()
    for _ in range(3):
        chain.add(dve.tensor_tensor(t, y, y, ALU.mult)).wait()
        chain.add(dve.tensor_tensor(t, t, v, ALU.mult)).wait()
        chain.add(dve.tensor_scalar(t, t, -0.5, 1.5, ALU.mult, ALU.add)).wait()
        chain.add(dve.tensor_tensor(y, y, t, ALU.mult)).wait()


FILLS_BEFORE = ["xt", "q0", "k0", "q1", "k1", "q2", "k2", "q3", "k3", "v0", "v1", "v2", "wo", "ka", "kb"]
FILLS_ROUND = ["pv0", "v3", "xt", "at3", "pv1", "q0", "k0", "wo", "pv2", "v0", "at0", "pv3", "q1", "k1",
               "ka", "pv4", "v1", "at1", "pv5", "q2", "k2", "kb", "pv6", "v2", "at2", "pv7", "q3", "k3"]
FILLS_LAST = ["pv0", "v3", "at3", "pv1", "wo", "pv2", "at0", "pv3", "pv4", "at1", "pv5", "pv6", "at2", "pv7",
              "pv8", "at3'", "wo'"]
HALVED_BEFORE = ["xt", "q0", "k0", "q1", "k1", "q2", "k2", "q3", "k3", "ka", "kb"]
HALVED_ROUND = ["xt", "q0", "k0", "q1", "k1", "ka", "q2", "k2", "kb", "q3", "k3"]
FILLS_ABSENT_FIRST = 2


class Round:

    def __init__(self, pair, first=False, last=False):
        self.pair, self.first, self.last = pair, first, last

    def fill(self, name):
        start = len(FILLS_BEFORE) - FILLS_ABSENT_FIRST
        if isinstance(self.pair, int) and self.pair == -1:
            n = FILLS_BEFORE.index(name)
            return n % 2, n // 2
        if self.first:
            n = len(FILLS_BEFORE) + [f for f in FILLS_ROUND if f not in ("pv0", "at3")].index(name)
            return n % 2, n // 2
        n = start + (FILLS_LAST if self.last else FILLS_ROUND).index(name)
        return n % 2, self.pair * (len(FILLS_ROUND) // 2) + n // 2

    def halved(self, name):
        if isinstance(self.pair, int) and self.pair == -1:
            return HALVED_BEFORE.index(name) + 1
        return self.pair * len(HALVED_ROUND) + (len(HALVED_BEFORE) + HALVED_ROUND.index(name) + 1)

    def before(self):
        return Round(self.pair - 1)


def transformer(nc, T, out):
    x_in, ctx_in = T["x"], T["ctx_1024"]
    B, S, D = x_in.shape
    HD = T["L0_xattn_wq_w"].shape[1]
    MEM = T["L0_xattn_mk"].shape[1]
    H0, DK = 16, HD // 16
    MT = HD // P
    PAIRS = B // 2
    H1, DH = 16, D // 16
    G1 = H1 // 4
    VW, VW1 = DK + 1, DH + 1
    F0 = T["L0_ffn_fc1_q"].shape[1]
    SC0, SC1 = DK ** -0.5, DH ** -0.5
    assert S == P and D == P and MEM == P and MT == 8 and PAIRS == 8 and DK == 64

    with ExitStack() as lasting, ExitStack() as ctx:
        def sb(name, shape, dt=F32):
            return ctx.enter_context(nc.sbuf_tensor(name, shape, dt))

        def keep(name, shape, dt=F32):
            return lasting.enter_context(nc.sbuf_tensor(name, shape, dt))

        def sem(name):
            return ctx.enter_context(nc.semaphore(name))

        x = keep("x", [P, B, D])
        ident = keep("ident", [P, P])
        one = keep("one", [1, 1])
        stats = keep("stats", [P, B, 6])
        mean_var = keep("mean_var", [P, B, 2])
        rstd = keep("rstd", [P, B])
        root_tmp = keep("root_tmp", [P, 2, B])
        R_BQ, R_BK, R_F1 = 0, HD, 2 * HD
        R_GA = R_F1 + F0
        R_BE = R_GA + D
        R_QE = R_BE + D
        R_KE = R_QE + 4 * D
        R_MQ = R_KE + 4 * D
        R_MK = R_MQ + D
        R_ALL = R_MK + D
        assert R_ALL == 4096
        cols = keep("cols", [P, R_ALL // P])
        mcols = keep("mcols", [P, 2 * G1])
        C = lambda r: r // P
        w1f = keep("w1f", [P, 2, F0], F32R)
        w2f = keep("w2f", [P, F0 // P, D])
        b2_bc = keep("b2_bc", [P, D])
        wqe = keep("wqe", [P, 2, G1 * P], F32R)
        k1T = keep("k1T", [P, G1, B * S], F32R)
        v1 = keep("v1", [P, B, H1, VW1])
        wo1 = keep("wo1", [P, D])
        bo1_bc = keep("bo1_bc", [P, D])

        w_raw = sb("w_raw", [P, 3, HD])
        wq = sb("wq", [P, 2, HD], F32R)
        wk = sb("wk", [P, 2, HD], F32R)
        wv = sb("wv", [P, 2, HD], F32R)
        wo = sb("wo", [P, MT, D])
        bv_bc = sb("bv_bc", [P, HD])
        bo_bc = sb("bo_bc", [P, D])
        rows1 = sb("rows1", [1, 2 * D])
        wke = sb("wke", [P, 2, G1 * P], F32R)
        wv1 = sb("wv1", [P, 2, D], F32R)
        bv1_bc = sb("bv1_bc", [P, D])
        assert 2 * F0 == HD
        fq = w_raw[:, 0, :].bitcast(I32).rearrange("p (w n) -> p w n", w=2)
        fs = w_raw[:, 1, :].rearrange("p (w n) -> p w n", w=2)
        w_ffn = w_raw[:, 2, :].rearrange("p (w n) -> p w n", w=2)
        xs = sb("xs", [P, 2, D])
        cs = sb("cs", [P, 2, D])
        xt = sb("xt", [P, 2, 4, P], F32R)
        qT = sb("qT", [P, 2, MT, 2 * S], F32R)
        kT = sb("kT", [P, 2, MT, 3, S], F32R)
        v = sb("v", [P, 2, H0, VW])
        mv = sb("mv", [P, H0, VW])
        nmx = sb("nmx", [P, 2, 4])
        probs = sb("probs", [P, 4096])
        pr = probs[:, 0:2048].rearrange("p (u r i k) -> p u r i k", u=2, r=2, i=2)
        pT = probs[:, 2048:4096].rearrange("p (u r t s) -> p u r t s", u=2, r=2, t=4)
        rows = probs[0:1, :]
        rec = sb("rec", [P, 2, 4])
        at = sb("at", [P, 2, 2, 256])
        attended = sb("attended", [P, 2048])
        aT = attended[:].rearrange("p (m b t s) -> p m b t s", m=4, b=2, t=2)
        mk_raw = attended[:, 0:HD]
        w1_raw = attended[:, HD:HD + 3 * D]
        k1h = sb("k1h", [P, 2, 2, 256], F32R)

        psS = ctx.enter_context(nc.psum_tensor("psS", [P, 2, 2, 512], F32))
        psT = ctx.enter_context(nc.psum_tensor("psT", [P, 2, 512], F32))
        psM = ctx.enter_context(nc.psum_tensor("psM", [P, 2, 512], F32))

        x_loaded, c_loaded = [sem("x_loaded0"), sem("x_loaded1")], sem("c_loaded")
        wqkv_loaded = [sem(f"w{n}_loaded") for n in "qkv"]
        rows_loaded, consts_loaded, mem_loaded = sem("rows_loaded"), sem("consts_loaded"), sem("mem_loaded")
        consts_set = sem("consts_set")
        ffn_loaded = sem("ffn_loaded")
        rows_ready, cols_full, cols_ready = sem("rows_ready"), sem("cols_full"), sem("cols_ready")
        mk_full, mk_hi, mk_ready = sem("mk_full"), sem("mk_hi"), sem("mk_ready")
        w_hi, w_ready = sem("w_hi"), sem("w_ready")
        w1_ready = sem("w1_ready")
        xs_ready = sem("xs_ready")
        misc_full = [sem("misc_full0"), sem("misc_full1")]
        misc_done = [sem("misc_done0"), sem("misc_done1")]
        hi_ready = sem("hi_ready")
        scores_full, max_ready, probs_ready = sem("scores_full"), sem("max_ready"), sem("probs_ready")
        pT_full = sem("pT_full")
        pT_ready = [sem("pT_ready0"), sem("pT_ready1")]
        dve_chain, act_chain, pool_chain = sem("dve_chain"), sem("act_chain"), sem("pool_chain")

        N_ROWS_DMA, N_CONST_DMA = 7, 5
        blocks = ExitStack()
        block = blocks.enter_context(nc.Block())

        def row(ap):
            return ap.rearrange("(a d) -> a d", a=1)

        rounds = [Round(0, first=True), Round(None), Round(PAIRS - 1, last=True)]

        @block.sync
        def _(sp):
            for c in range(4):
                sp.dma_start(x[:, 4 * c:4 * c + 4, :], x_in[4 * c:4 * c + 4].rearrange("b s d -> s b d")).then_inc(x_loaded[c > 0], 16)
                if c == 0:
                    sp.dma_start(w_raw[:, 0, :], T["L0_xattn_wq_w"]).then_inc(wqkv_loaded[0], 16)
                    sp.dma_start(cs[:], ctx_in[0:2].rearrange("b s d -> s b d")).then_inc(c_loaded, 16)
                    sp.dma_start(w_raw[:, 1, :], T["L0_xattn_wk_w"]).then_inc(wqkv_loaded[1], 16)
            sp.dma_start(w_raw[:, 2, :], T["L0_xattn_wv_w"]).then_inc(wqkv_loaded[2], 16)

            def next_context(r):
                bank, n = r.fill("xt")
                sp.wait_ge(misc_full[bank], n + 1)
                sp.dma_start(cs[:], ctx_in[bass.ds((r.pair + 2) * 2, 2)].rearrange("b s d -> s b d")).then_inc(c_loaded, 16)

            next_context(Round(-1))
            sp.wait_ge(w_ready, 3)
            sp.dma_start(fq[:, 0, :], T["L0_ffn_fc1_q"]).then_inc(ffn_loaded, 16)
            sp.dma_start(fq[:, 1, :].rearrange("p (t d) -> p t d", d=D), T["L0_ffn_fc2_q"].rearrange("(t p) d -> p t d", p=P)).then_inc(ffn_loaded, 16)
            sp.dma_start(fs[:, 0, :], T["L0_ffn_fc1_scales"].partition_broadcast(P)).then_inc(ffn_loaded, 16)
            sp.dma_start(fs[:, 1, :], row(T["L0_ffn_fc2_scales"].rearrange("g d -> (g d)")).partition_broadcast(P)).then_inc(ffn_loaded, 16)
            next_context(rounds[0])
            with sp.Fori(1, PAIRS - 2) as pair:
                next_context(Round(pair))

        @block.gpsimd
        def _(pool):
            chain = Chain(pool, pool_chain)
            chain.add(pool.memset(ident[:], 0.0))
            pool.memset(one[:], 1.0).then_inc(consts_set, 1)
            chain.add(pool.memset(rows[:, R_MQ:R_ALL], 0.0))
            pool.memset(v[:, :, :, DK:VW], 1.0).then_inc(consts_set, 1)
            pool.memset(mv[:, :, DK:VW], 1.0).then_inc(consts_set, 1)
            pool.memset(v1[:, :, :, DH:VW1], 1.0).then_inc(consts_set, 1)
            chain.wait()
            pool.affine_select(out=ident[:], in_=ident[:], compare_op=ALU.not_equal, fill=1.0, base=0,
                               pattern=[[-1, P]], channel_multiplier=1).then_inc(consts_set, 1)
            parts = rows[:, R_MQ:R_ALL].rearrange("a (w j r d) -> a w j r d", w=2, j=4, r=4)
            pool.memset(parts[:, 0, :, 2, :], 1.0).then_inc(consts_set, 1)
            pool.memset(parts[:, 1, :, 1, :], 1.0).then_inc(consts_set, 1)

            pool.wait_ge(ffn_loaded, 16 * 6)
            for i in range(2):
                chain.add(pool.tensor_copy(w_ffn[:, i, :], fq[:, i, :]))
            chain.wait()
            for i in range(2):
                chain.add(pool.tensor_scalar(w_ffn[:, i, :], w_ffn[:, i, :], -128.0, None, ALU.add))
            chain.wait()
            chain.add(pool.tensor_tensor(w_ffn[:, 0, :], w_ffn[:, 0, :], fs[:, 0, :], ALU.mult))
            pool.tensor_tensor(w2f[:, :, :].rearrange("p t d -> p (t d)"), w_ffn[:, 1, :], fs[:, 1, :], ALU.mult)
            chain.wait()
            chain.add(pool.tensor_copy(w1f[:, 0, :], w_ffn[:, 0, :])).wait()
            pool.tensor_tensor(w1f[:, 1, :], w_ffn[:, 0, :], w1f[:, 0, :].bitcast(F32), ALU.subtract)

        N_CONSTS = 7

        @block.scalar
        def _(act):
            for r0, name, n in ((R_BQ, "L0_xattn_wq_b", HD), (R_BK, "L0_xattn_wk_b", HD), (R_F1, "L0_ffn_fc1_bias", F0),
                                (R_GA, "L0_ffn_ln_gamma", D), (R_BE, "L0_ffn_ln_beta", D)):
                act.dma_start(rows[:, r0:r0 + n], row(T[name])).then_inc(rows_loaded, 16)
            act.dma_start(rows1[:, 0:D], row(T["L1_xattn_bq"])).then_inc(rows_loaded, 16)
            act.dma_start(rows1[:, D:2 * D], row(T["L1_xattn_bkv"])[:, 0:D]).then_inc(rows_loaded, 16)
            act.dma_start(mk_raw[:], T["L0_xattn_mk"][0]).then_inc(mem_loaded, 16)
            act.dma_start(bv_bc[:], row(T["L0_xattn_wv_b"]).partition_broadcast(P)).then_inc(consts_loaded, 16)
            act.dma_start(bv1_bc[:], row(T["L1_xattn_bkv"])[:, D:2 * D].partition_broadcast(P)).then_inc(consts_loaded, 16)
            act.dma_start(bo_bc[:], row(T["L0_xattn_wo_b"]).partition_broadcast(P)).then_inc(consts_loaded, 16)
            act.dma_start(w1_raw[:, 0:D], T["L1_xattn_Wq"]).then_inc(mem_loaded, 16)
            act.dma_start(w1_raw[:, D:3 * D], T["L1_xattn_Wkv"]).then_inc(mem_loaded, 16)
            act.dma_start(mv[:, :, 0:DK], T["L0_xattn_mv"][0].rearrange("t (h d) -> t h d", d=DK)).then_inc(mem_loaded, 16)
            act.dma_start(wo[:], T["L0_xattn_wo_w"].rearrange("(t p) n -> p t n", p=P)).then_inc(consts_loaded, 16)
            act.dma_start(b2_bc[:], row(T["L0_ffn_fc2_bias"]).partition_broadcast(P)).then_inc(ffn_loaded, 16)
            act.dma_start(wo1[:], T["L1_xattn_Wo"]).then_inc(ffn_loaded, 16)
            act.dma_start(bo1_bc[:], row(T["L1_xattn_bo"]).partition_broadcast(P)).then_inc(consts_loaded, 16)
            for n, (w, scale) in enumerate(((wq, SC0), (wk, 1.0), (wv, 1.0))):
                act.wait_ge(wqkv_loaded[n], 16)
                act.activation(w[:, 0, :], w_raw[:, n, :], ACT.Copy, scale=scale).then_inc(w_hi, 1)

            def hi_of_fill(r, name, pair_mm=None):
                bank, n = r.fill(name)
                act.wait_ge(misc_full[bank], n + 1)
                ps = psM[:, bank, :]
                if name == "xt":
                    last = act.activation(xt[:, 0, :, :], ps.rearrange("p (t s) -> p t s", t=4), ACT.Copy)
                elif name[0] == "q":
                    for i in range(2):
                        m = 2 * int(name[1]) + i
                        last = act.activation(qT[:, 0, m, :], ps[:, 256 * i:256 * i + 256], ACT.Identity,
                                              bias=cols[:, C(R_BQ) + m:C(R_BQ) + m + 1])
                elif name in ("ka", "kb"):
                    for i in range(2):
                        t = 2 * (name == "kb") + i
                        last = act.activation(k1h[:, t // 2, i, :], ps[:, 256 * i:256 * i + 256], ACT.Identity,
                                              scale=cols[:, C(R_MK):C(R_MK) + 1], bias=mcols[:, G1 + t:G1 + t + 1])
                else:
                    for i in range(2):
                        m = 2 * int(name[1]) + i
                        last = act.activation(kT[:, 0, m, 0:2, :], ps[:, 256 * i:256 * i + 256].rearrange("p (b s) -> p b s", b=2),
                                              ACT.Identity, bias=cols[:, C(R_BK) + m:C(R_BK) + m + 1])
                last.then_inc(hi_ready, 1)

            def exps(quad, unit):
                act.wait_ge(max_ready, quad + 1)
                at_least(act, pT_full, quad * 2 - 2)
                for r in range(2):
                    for i in range(2):
                        last = act.activation(pr[:, unit, r, i, :], psS[:, unit, r, 256 * i:256 * i + 256], ACT.Exp,
                                              bias=nmx[:, unit, 2 * r + i:2 * r + i + 1])
                last.then_inc(probs_ready, 1)

            def copy_pT(r, g, quad):
                act.wait_ge(pT_full, quad * 2 + 2)
                if not (r.first and g < 2):
                    bank, n = r.fill(f"pv{g - 1}") if g >= 1 else r.before().fill("pv7")
                    act.wait_ge(misc_full[bank], n + 1)
                act.copy(pT[:, g % 2, 1, :, :], psT[:, 1, :].rearrange("p (t s) -> p t s", t=4)).then_inc(pT_ready[1], 1)

            def copy_aT(r, name, mm):
                bank, n = r.fill(name)
                act.wait_ge(misc_full[bank], n + 1)
                act.copy(aT[:, mm, :, :, :], psM[:, bank, :].rearrange("p (b t s) -> p b t s", b=2, t=2)).then_inc(misc_done[bank], 1)

            act.wait_ge(mk_full, 1)
            for i in range(2):
                last = act.activation(kT[:, 0, 4 * i:4 * i + 4, 2, :], psS[:, 1, i, :].rearrange("p (t s) -> p t s", t=4), ACT.Copy)
            last.then_inc(mk_hi, 1)
            act.wait_ge(cols_ready, 1)
            for name in HALVED_BEFORE:
                hi_of_fill(Round(-1), name)
            exps(0, 0)

            def attention_round(r):
                for g in range(8):
                    quad = r.pair * 8 + g
                    if g == 1 and not r.first:
                        copy_aT(r, "at3", 3)
                    if g in (3, 5, 7):
                        copy_aT(r, f"at{g // 2 - 1}", g // 2 - 1)
                    if g in (4, 6) and not r.last:
                        hi_of_fill(r, "ka" if g == 4 else "kb")
                    if not (r.last and g == 7):
                        exps(quad + 1, (g + 1) % 2)
                    copy_pT(r, g, quad)
                    if not r.last:
                        if g == 0:
                            hi_of_fill(r, "xt")
                        if g % 2:
                            hi_of_fill(r, f"q{g // 2}")
                            hi_of_fill(r, f"k{g // 2}")

            attention_round(rounds[0])
            with act.Fori(1, PAIRS - 1) as pair:
                attention_round(Round(pair))
            attention_round(rounds[2])
            copy_aT(rounds[2], "at3'", 3)

        @block.tensor
        def _(pe):
            pe.wait_ge(consts_set, N_CONSTS)
            pe.wait_ge(rows_ready, 1)
            for c in range(R_ALL // P):
                last = pe.matmul(psT[:, 0, c:c + 1], rows[:, c * P:(c + 1) * P], one[:], start=True, stop=True)
            last.then_inc(cols_full, 1)
            pe.wait_ge(mem_loaded, 64)
            for m in range(MT):
                last = pe.transpose(psS[:, 1, m // 4, (m % 4) * P:(m % 4 + 1) * P], mk_raw[:, m * P:(m + 1) * P], ident[:])
            last.then_inc(mk_full, 1)

            def opened(r, name):
                bank, n = r.fill(name)
                at_least(pe, misc_done[bank], n)
                return bank

            def evacuated(r, name):
                bank, n = r.fill(name)
                pe.wait_ge(misc_done[bank], n + 1)

            def product(dst, left, right):
                (lh, ll), (rh, rl) = left, right
                pe.matmul(dst, lh, rh, start=True, stop=False)
                pe.matmul(dst, lh, rl, start=False, stop=False)
                return pe.matmul(dst, ll, rh, start=False, stop=True)

            def halves(t, *index):
                return t[(slice(None), 0) + index], t[(slice(None), 1) + index]

            ALL = slice(None)

            def transpose_inputs(r, n):
                bank = opened(r, "xt")
                pe.wait_ge(xs_ready, n)
                pe.wait_ge(c_loaded, n * 16)
                for t in range(4):
                    last = pe.transpose(psM[:, bank, t * P:(t + 1) * P], (xs if t < 2 else cs)[:, t % 2, :], ident[:])
                last.then_inc(misc_full[bank], 1)

            def project_q_or_k(r, name):
                bank = opened(r, name)
                w, src = (wq, slice(0, 2)) if name[0] == "q" else (wk, slice(2, 4))
                for i in range(2):
                    m = 2 * int(name[1]) + i
                    last = product(psM[:, bank, 256 * i:256 * i + 256], halves(w, slice(m * P, (m + 1) * P)),
                                   halves(xt, src, ALL))
                last.then_inc(misc_full[bank], 1)

            def project_k1(r, name):
                bank = opened(r, name)
                for i in range(2):
                    t = 2 * (name == "kb") + i
                    last = product(psM[:, bank, 256 * i:256 * i + 256], halves(wke, slice(t * P, (t + 1) * P)),
                                   halves(xt, slice(2, 4), ALL))
                last.then_inc(misc_full[bank], 1)

            def project_v(r, mm):
                bank = opened(r, f"v{mm}")
                for b in range(2):
                    last = product(psM[:, bank, 256 * b:256 * b + 256], halves(xt, 2 + b, ALL),
                                   halves(wv, slice(256 * mm, 256 * mm + 256)))
                last.then_inc(misc_full[bank], 1)

            def project_out_and_v1(r, name, out_part, v1_part):
                bank = opened(r, name)
                if out_part:
                    for b in range(2):
                        for t in range(MT):
                            last = pe.matmul(psM[:, bank, b * P:(b + 1) * P], aT[:, t // 2, b, t % 2, :], wo[:, t, :],
                                             start=t == 0, stop=t == MT - 1)
                if v1_part:
                    for b in range(2):
                        last = product(psM[:, bank, 256 + b * P:256 + (b + 1) * P], halves(xt, 2 + b, ALL), halves(wv1, ALL))
                last.then_inc(misc_full[bank], 1)

            def scores(unit, mm, b, quad):
                at_least(pe, probs_ready, quad - 1)
                for i in range(2):
                    for r in range(2):
                        m, part = 2 * mm + i, slice(64 * r, 64 * r + 64)
                        keys = slice(0, 3, 2) if b == 0 else slice(1, 3)
                        last = product(psS[:, unit, r, 256 * i:256 * i + 256],
                                       (qT[part, 0, m, b * S:(b + 1) * S], qT[part, 1, m, b * S:(b + 1) * S]),
                                       (kT[part, 0, m, keys, :], kT[part, 1, m, keys, :]))
                last.then_inc(scores_full, 1)

            def transpose_probs(unit, quad):
                pe.wait_ge(probs_ready, quad + 1)
                for r in range(2):
                    at_least(pe, pT_ready[r], quad)
                    for i in range(2):
                        for kt in range(2):
                            c = 2 * i + kt
                            last = pe.transpose(psT[:, r, c * P:(c + 1) * P], pr[:, unit, r, i, kt * P:(kt + 1) * P], ident[:])
                    last.then_inc(pT_full, 1)

            def attend(r, g, quad):
                local = (g - 1) % 8
                unit, mm, b = local % 2, local // 2, local % 2
                bank = opened(r, f"pv{g}")
                for i in range(2):
                    pe.wait_ge(pT_ready[i], quad)
                for h in range(4):
                    i, part, head = h // 2, h % 2, 4 * mm + h
                    pe.matmul(psM[:, bank, h * VW:(h + 1) * VW], pT[:, unit, part, 2 * i, :], v[:, b, head, :], start=True, stop=False)
                    last = pe.matmul(psM[:, bank, h * VW:(h + 1) * VW], pT[:, unit, part, 2 * i + 1, :], mv[:, head, :],
                                     start=False, stop=True)
                last.then_inc(misc_full[bank], 1)

            def transpose_attended(r, name, mm):
                bank = opened(r, name)
                if name == "at3":
                    evacuated(r, "pv0")
                elif name == "at3'":
                    evacuated(r, "pv8")
                else:
                    evacuated(r, f"pv{2 * mm + 2}")
                for b in range(2):
                    for t in range(2):
                        c = 2 * b + t
                        last = pe.transpose(psM[:, bank, c * P:(c + 1) * P], at[:, mm % 2, b, t * P:(t + 1) * P], ident[:])
                last.then_inc(misc_full[bank], 1)

            before = Round(-1)
            transpose_inputs(before, 1)
            evacuated(before, "xt")
            pe.wait_ge(w_ready, 2)
            for mm in range(4):
                project_q_or_k(before, f"q{mm}")
                project_q_or_k(before, f"k{mm}")
            pe.wait_ge(w_ready, 3)
            for mm in range(3):
                project_v(before, mm)
            pe.wait_ge(w1_ready, 1)
            project_out_and_v1(before, "wo", False, True)
            project_k1(before, "ka")
            project_k1(before, "kb")
            pe.wait_ge(mk_ready, 1)
            evacuated(before, "q0")
            evacuated(before, "k0")
            scores(0, 0, 0, 0)
            pe.wait_ge(consts_loaded, 16 * N_CONST_DMA)

            def attention_round(r):
                prior = before if r.first else r.before()
                for g in range(8):
                    quad = r.pair * 8 + g
                    mm = g // 2
                    if not (r.last and g == 7):
                        nxt = (g + 1) % 8
                        if nxt % 2 == 0:
                            source = r if g == 7 else prior
                            evacuated(source, f"q{nxt // 2}")
                            evacuated(source, f"k{nxt // 2}")
                        scores(nxt % 2, nxt // 2, nxt % 2, quad + 1)
                    if g == 1 and not r.first:
                        transpose_attended(r, "at3", 3)
                    if g == 2:
                        if not r.first:
                            evacuated(r, "at3")
                        project_out_and_v1(r, "wo", not r.first, not r.last)
                    if g in (3, 5, 7):
                        transpose_attended(r, f"at{mm - 1}", mm - 1)
                    if g in (4, 6) and not r.last:
                        project_k1(r, "ka" if g == 4 else "kb")
                    transpose_probs(g % 2, quad)
                    if not (r.first and g == 0):
                        if g % 2:
                            if g == 7:
                                evacuated(r, "v3")
                            else:
                                evacuated(prior, f"v{mm}")
                        attend(r, g, quad)
                    if g == 0:
                        project_v(r, 3)
                        if not r.last:
                            transpose_inputs(r, r.pair + 2)
                    if not r.last and g % 2:
                        if g == 1:
                            evacuated(r, "xt")
                        project_q_or_k(r, f"q{mm}")
                        project_q_or_k(r, f"k{mm}")
                    if not r.last and g in (2, 4, 6):
                        project_v(r, mm - 1)

            attention_round(rounds[0])
            with pe.Fori(1, PAIRS - 1) as pair:
                attention_round(Round(pair))
            last_round = rounds[2]
            attention_round(last_round)
            attend(last_round, 8, 8 * PAIRS)
            transpose_attended(last_round, "at3'", 3)
            evacuated(last_round, "at3'")
            project_out_and_v1(last_round, "wo'", True, False)

        @block.vector
        def _(dve):
            chain = Chain(dve, dve_chain)

            def statistics(tiles):
                a, z = tiles
                for t in range(a, z):
                    chain.add(dve.bn_stats(stats[:, t, :], x[:, t, :]))
                chain.wait()
                for t in range(a, z):
                    chain.add(dve.bn_aggr(mean_var[:, t, :], stats[:, t, :]))
                chain.wait()
                inverse_root(dve, chain, rstd[:, a:z], mean_var[:, a:z, 1], 1e-5, root_tmp[:, :, 0:z - a])

            def normalise(pair):
                for i in range(2):
                    t = pair * 2 + i
                    if isinstance(t, int):
                        mean, scale, src = mean_var[:, t, 0:1], rstd[:, t:t + 1], x[:, t, :]
                    else:
                        mean, scale, src = mean_var[:, bass.ds(t, 1), 0], rstd[:, bass.ds(t, 1)], x[:, bass.ds(t, 1), :].rearrange("p a d -> p (a d)")
                    last = dve.tensor_scalar(xs[:, i, :], src, mean, scale, ALU.subtract, ALU.mult)
                last.then_inc(xs_ready, 1)

            dve.wait_ge(x_loaded[0], 16)
            statistics((0, 4))
            chain.wait()
            normalise(0)
            for n, (w, scale) in enumerate(((wq, SC0), (wk, 1.0), (wv, 1.0))):
                dve.wait_ge(w_hi, n + 1)
                dve.scalar_tensor_tensor(w[:, 1, :], w_raw[:, n, :], scale, w[:, 0, :].bitcast(F32), ALU.mult, ALU.subtract)\
                    .then_inc(w_ready, 1)
                if n == 0:
                    dve.wait_ge(rows_loaded, 16 * N_ROWS_DMA)
                    dve.tensor_scalar(rows[:, R_BQ:R_BQ + HD], rows[:, R_BQ:R_BQ + HD], SC0, None, ALU.mult)
                    for r0, r1, scale in ((R_QE, 0, SC1), (R_KE, D, 1.0)):
                        last = dve.tensor_scalar(rows[:, r0:r0 + 4 * D].rearrange("a (h r d) -> a h r d", h=H1, r=4),
                                                 rows1[:, r1:r1 + D].rearrange("a (h r d) -> a h r d", h=H1, r=1).to_broadcast([1, H1, 4, DH]),
                                                 scale, None, ALU.mult)
                    last.then_inc(rows_ready, 1)
            dve.wait_ge(cols_full, 1)
            chain.add(dve.tensor_copy(cols[:], psT[:, 0, 0:R_ALL // P]))
            chain.wait()
            dve.tensor_scalar(mcols[:, 0:G1], cols[:, C(R_QE):C(R_QE) + G1], cols[:, C(R_MQ):C(R_MQ) + 1], None, ALU.mult)
            dve.tensor_scalar(mcols[:, G1:2 * G1], cols[:, C(R_KE):C(R_KE) + G1], cols[:, C(R_MK):C(R_MK) + 1], None, ALU.mult)\
                .then_inc(cols_ready, 1)

            def hi_lo(w, src, scale=1.0):
                dve.tensor_scalar(w[0], src, scale, None, ALU.mult) if scale != 1.0 else dve.tensor_copy(w[0], src)

            dve.wait_ge(mk_hi, 1)
            for i in range(2):
                last = dve.tensor_tensor(kT[:, 1, 4 * i:4 * i + 4, 2, :], psS[:, 1, i, :].rearrange("p (t s) -> p t s", t=4),
                                         kT[:, 0, 4 * i:4 * i + 4, 2, :].bitcast(F32), ALU.subtract)
            last.then_inc(mk_ready, 1)

            def lo_of_fill(r, name, pair=None):
                bank, n = r.fill(name)
                dve.wait_ge(misc_full[bank], n + 1)
                dve.wait_ge(hi_ready, r.halved(name))
                ps = psM[:, bank, :]
                if name == "xt":
                    last = dve.tensor_tensor(xt[:, 1, :, :], ps.rearrange("p (t s) -> p t s", t=4), xt[:, 0, :, :].bitcast(F32), ALU.subtract)
                elif name[0] == "q":
                    for i in range(2):
                        m = 2 * int(name[1]) + i
                        last = dve.scalar_tensor_tensor(qT[:, 1, m, :], ps[:, 256 * i:256 * i + 256], cols[:, C(R_BQ) + m:C(R_BQ) + m + 1],
                                                        qT[:, 0, m, :].bitcast(F32), ALU.add, ALU.subtract)
                elif name in ("ka", "kb"):
                    for i in range(2):
                        t = 2 * (name == "kb") + i
                        to = (pair + 1) * 256
                        dst = k1T[:, t, to:to + 256] if isinstance(to, int) else k1T[:, t, bass.ds(to, 256)]
                        last = dve.scalar_tensor_tensor(dst, ps[:, 256 * i:256 * i + 256], cols[:, C(R_KE) + t:C(R_KE) + t + 1],
                                                        k1h[:, t // 2, i, :].bitcast(F32), ALU.add, ALU.subtract)
                else:
                    for i in range(2):
                        m = 2 * int(name[1]) + i
                        last = dve.scalar_tensor_tensor(kT[:, 1, m, 0:2, :], ps[:, 256 * i:256 * i + 256].rearrange("p (b s) -> p b s", b=2),
                                                        cols[:, C(R_BK) + m:C(R_BK) + m + 1],
                                                        kT[:, 0, m, 0:2, :].bitcast(F32), ALU.add, ALU.subtract)
                last.then_inc(misc_done[bank], 1)

            def keep_v(r, mm):
                bank, n = r.fill(f"v{mm}")
                dve.wait_ge(misc_full[bank], n + 1)
                dve.tensor_tensor(v[:, :, 4 * mm:4 * mm + 4, 0:DK], psM[:, bank, :].rearrange("p (b h d) -> p b h d", b=2, h=4),
                                  bv_bc[:, 256 * mm:256 * mm + 256].rearrange("p (b h d) -> p b h d", b=1, h=4).to_broadcast([P, 2, 4, DK]),
                                  ALU.add).then_inc(misc_done[bank], 1)

            def residual_and_v1(r, name, out_part, v1_part, pair):
                bank, n = r.fill(name)
                dve.wait_ge(misc_full[bank], n + 1)
                if out_part:
                    t = pair * 2 - 2
                    dst = x[:, t:t + 2, :] if isinstance(t, int) else x[:, bass.ds(t, 2), :]
                    last = dve.tensor_tensor(dst, dst, psM[:, bank, 0:256].rearrange("p (b d) -> p b d", b=2), ALU.add)
                    if v1_part:
                        chain.add(last)
                        chain.wait()
                    else:
                        last.then_inc(dve_chain, 1)
                        chain.count += 1
                        chain.wait()
                    last = dve.tensor_tensor(dst, dst, bo_bc[:].rearrange("p (b d) -> p b d", b=1).to_broadcast([P, 2, D]), ALU.add)
                if v1_part:
                    t = pair * 2 + 2
                    dst = v1[:, t:t + 2, :, 0:DH] if isinstance(t, int) else v1[:, bass.ds(t, 2), :, 0:DH]
                    last = dve.tensor_tensor(dst, psM[:, bank, 256:512].rearrange("p (b h d) -> p b h d", b=2, h=H1),
                                             bv1_bc[:].rearrange("p (b h d) -> p b h d", b=1, h=H1).to_broadcast([P, 2, H1, DH]), ALU.add)
                last.then_inc(misc_done[bank], 1)

            def row_max(quad, unit):
                dve.wait_ge(scores_full, quad + 1)
                dve.tensor_reduce(nmx[:, unit, :], psS[:, unit, :, :].rearrange("p r (i k) -> p (r i) k", i=2), AX_X, ALU.max,
                                  negate=True).then_inc(max_ready, 1)

            def copy_pT(quad, unit):
                dve.wait_ge(pT_full, quad * 2 + 1)
                dve.tensor_copy(pT[:, unit, 0, :, :], psT[:, 0, :].rearrange("p (t s) -> p t s", t=4)).then_inc(pT_ready[0], 1)

            def normalise_attended(r, g):
                local = (g - 1) % 8
                mm, b = local // 2, local % 2
                bank, n = r.fill(f"pv{g}")
                dve.wait_ge(misc_full[bank], n + 1)
                o = psM[:, bank, 0:4 * VW].rearrange("p (h d) -> p h d", h=4)
                chain.add(dve.reciprocal(rec[:, b, :], o[:, :, DK])).wait()
                dve.tensor_tensor(at[:, mm % 2, b, :].rearrange("p (h d) -> p h d", h=4), o[:, :, 0:DK],
                                  rec[:, b, :].rearrange("p (h d) -> p h d", d=1).to_broadcast([P, 4, DK]), ALU.mult).then_inc(misc_done[bank], 1)

            before = Round(-1)
            lo_of_fill(before, "xt")
            dve.wait_ge(x_loaded[1], 48)
            statistics((4, B))
            chain.wait()
            normalise(1)
            for mm in range(4):
                lo_of_fill(before, f"q{mm}")
                lo_of_fill(before, f"k{mm}")
                if mm == 0:
                    dve.wait_ge(mem_loaded, 64)
                    for w, c0, scale in ((wqe, 0, SC1), (wke, D, 1.0)):
                        dst = w[:, :, :].rearrange("p a (h r d) -> p a h r d", h=H1, r=4)
                        src = w1_raw[:, c0:c0 + D].rearrange("p (h r d) -> p h r d", h=H1, r=1).to_broadcast([P, H1, 4, DH])
                        chain.add(dve.tensor_scalar(dst[:, 0], src, scale, None, ALU.mult)).wait()
                        for rep in range(4):
                            dve.scalar_tensor_tensor(dst[:, 1, :, rep, :], src[:, :, rep, :], scale, dst[:, 0, :, rep, :].bitcast(F32),
                                                     ALU.mult, ALU.subtract)
                    chain.add(dve.tensor_copy(wv1[:, 0, :], w1_raw[:, 2 * D:3 * D])).wait()
                    dve.tensor_tensor(wv1[:, 1, :], w1_raw[:, 2 * D:3 * D], wv1[:, 0, :].bitcast(F32), ALU.subtract).then_inc(w1_ready, 1)
            dve.wait_ge(consts_loaded, 16 * N_CONST_DMA)
            for mm in range(3):
                keep_v(before, mm)
            residual_and_v1(before, "wo", False, True, -1)
            lo_of_fill(before, "ka", -1)
            lo_of_fill(before, "kb", -1)
            row_max(0, 0)

            def attention_round(r):
                for g in range(8):
                    quad = r.pair * 8 + g
                    if not (r.last and g == 7):
                        row_max(quad + 1, (g + 1) % 2)
                    if g == 2:
                        residual_and_v1(r, "wo", not r.first, not r.last, r.pair)
                    if g in (4, 6) and not r.last:
                        lo_of_fill(r, "ka" if g == 4 else "kb", r.pair)
                    copy_pT(quad, g % 2)
                    if not (r.first and g == 0):
                        normalise_attended(r, g)
                    if g == 0:
                        keep_v(r, 3)
                        if not r.last:
                            lo_of_fill(r, "xt")
                    if not r.last and g % 2:
                        lo_of_fill(r, f"q{g // 2}")
                        lo_of_fill(r, f"k{g // 2}")
                    if not r.last and g in (2, 4, 6):
                        keep_v(r, g // 2 - 1)
                    if g == 4 and not r.last and r is not LAST_BUT_ONE:
                        normalise(r.pair + 2)

            LAST_BUT_ONE = Round(PAIRS - 2)
            attention_round(rounds[0])
            with dve.Fori(1, PAIRS - 2) as pair:
                chain.loop(pair, 1, 9)
                attention_round(Round(pair))
                chain.end(PAIRS - 2)
            attention_round(LAST_BUT_ONE)
            attention_round(rounds[2])
            normalise_attended(rounds[2], 8)
            residual_and_v1(rounds[2], "wo'", True, False, PAIRS)

        blocks.close()
        ctx.close()
        m = Shared()
        m.x, m.ident, m.stats, m.mean_var, m.rstd = x, ident, stats, mean_var, rstd
        m.root_tmp, m.cols, m.mcols, m.f1_bias, m.gamma = root_tmp, cols, mcols, C(R_F1), C(R_GA)
        m.beta, m.bq1, m.mq, m.w1f, m.w2f = C(R_BE), C(R_QE), C(R_MQ), w1f, w2f
        m.b2_bc, m.wqe, m.k1T, m.v1, m.wo1 = b2_bc, wqe, k1T, v1, wo1
        m.bo1_bc = bo1_bc
        prepare_second_attention(nc, m, lasting)
        prepare_experts(nc, m, T, lasting)
        feed_forward(nc, m)
        second_attention(nc, m)
        mixture(nc, m, T, out)


def feed_forward(nc, m):
    B, D = m.x.shape[1], m.x.shape[2]
    CH, N = 4, 4 * P
    CHUNKS = B // CH
    FT = m.w2f.shape[1]
    with ExitStack() as ctx:
        sb = lambda name, shape, dt=F32: ctx.enter_context(nc.sbuf_tensor(name, shape, dt))
        sem = lambda name: ctx.enter_context(nc.semaphore(name))
        rstd2 = sb("rstd2", [P, B])
        n1 = sb("f_n1", [P, 2, CH, D])
        n2 = sb("f_n2", [P, CH, D])
        h = sb("f_h", [P, N])
        hT = sb("f_hT", [P, 2, N], F32R)
        y = sb("f_y", [P, FT, N])
        z = sb("f_z", [P, CH, D])
        b2h = sb("f_b2h", [P, D])
        psH = ctx.enter_context(nc.psum_tensor("psH", [P, N], F32))
        psY = ctx.enter_context(nc.psum_tensor("psY", [P, FT, N], F32))
        psZ = ctx.enter_context(nc.psum_tensor("psZ", [P, N], F32))
        n2_ready, h_full, h_copied, hT_ready = sem("f_n2_ready"), sem("f_h_full"), sem("f_h_copied"), sem("f_hT_ready")
        y_full, y_ready, z_full, z_read, chained = sem("f_y_full"), sem("f_y_ready"), sem("f_z_full"), sem("f_z_read"), sem("f_chained")
        with nc.Block() as block:
            m.load_experts(block)

            @block.tensor
            def _(pe):
                def transpose_in(c):
                    at_least(pe, h_copied, c)
                    pe.wait_ge(n2_ready, c + 1)
                    for t in range(CH):
                        last = pe.transpose(psH[:, t * P:(t + 1) * P], n2[:, t, :], m.ident[:])
                    last.then_inc(h_full, 1)

                def up(c):
                    pe.wait_ge(hT_ready, c + 1)
                    for f in range(FT):
                        at_least(pe, y_ready, (c - 1) * FT + f + 1)
                        lh, ll = m.w1f[:, 0, f * P:(f + 1) * P], m.w1f[:, 1, f * P:(f + 1) * P]
                        pe.matmul(psY[:, f, :], lh, hT[:, 0, :], start=True, stop=False)
                        pe.matmul(psY[:, f, :], lh, hT[:, 1, :], start=False, stop=False)
                        pe.matmul(psY[:, f, :], ll, hT[:, 0, :], start=False, stop=True).then_inc(y_full, 1)

                def down(c):
                    at_least(pe, z_read, c)
                    pe.wait_ge(y_ready, (c + 1) * FT)
                    for t in range(CH):
                        for f in range(FT):
                            last = pe.matmul(psZ[:, t * P:(t + 1) * P], y[:, f, t * P:(t + 1) * P], m.w2f[:, f, :],
                                             start=f == 0, stop=f == FT - 1)
                    last.then_inc(z_full, 1)

                transpose_in(0)
                up(0)
                transpose_in(1)
                down(0)
                with pe.Fori(1, CHUNKS - 1) as c:
                    up(c)
                    transpose_in(c + 1)
                    down(c)
                up(CHUNKS - 1)
                down(CHUNKS - 1)

            @block.scalar
            def _(act):
                def scale_h(c):
                    act.wait_ge(h_full, c + 1)
                    at_least(act, hT_ready, c)
                    act.activation(h[:], psH[:], ACT.Identity, scale=m.cols[:, m.gamma:m.gamma + 1],
                                   bias=m.cols[:, m.beta:m.beta + 1]).then_inc(h_copied, 1)

                def silu(c):
                    for f in range(FT):
                        act.wait_ge(y_full, c * FT + f + 1)
                        at_least(act, z_full, c)
                        act.activation(y[:, f, :], psY[:, f, :], ACT.Silu,
                                       bias=m.cols[:, m.f1_bias + f:m.f1_bias + f + 1]).then_inc(y_ready, 1)

                scale_h(0)
                with act.Fori(0, CHUNKS - 1) as c:
                    silu(c)
                    scale_h(c + 1)
                silu(CHUNKS - 1)

            @block.vector
            def _(dve):
                chain = Chain(dve, chained)

                def layer_norms(c, buffer):
                    for t in range(CH):
                        i = c * CH + t
                        chain.add(dve.tensor_scalar(n1[:, buffer, t, :], m.x[:, bass.ds(i, 1), :].rearrange("p a d -> p (a d)"),
                                                    m.mean_var[:, bass.ds(i, 1), 0], m.rstd[:, bass.ds(i, 1)], ALU.subtract, ALU.mult))
                    chain.wait()
                    at_least(dve, h_full, c)
                    for t in range(CH):
                        last = dve.tensor_scalar(n2[:, t, :], n1[:, buffer, t, :], rstd2[:, bass.ds(c * CH + t, 1)], None, ALU.mult)
                    last.then_inc(n2_ready, 1)

                def split_h(c):
                    dve.wait_ge(h_copied, c + 1)
                    at_least(dve, y_full, c * FT)
                    chain.add(dve.tensor_copy(hT[:, 0, :], h[:])).wait()
                    dve.tensor_tensor(hT[:, 1, :], h[:], hT[:, 0, :].bitcast(F32), ALU.subtract).then_inc(hT_ready, 1)

                def residual(c, buffer):
                    dve.wait_ge(z_full, c + 1)
                    dst = m.x[:, bass.ds(c * CH, CH), :]
                    ins = dve.scalar_tensor_tensor(z[:, :, :], psZ[:].rearrange("p (t d) -> p t d", t=CH), 0.5, n1[:, buffer, :, :],
                                                   ALU.mult, ALU.add)
                    ins.then_inc(z_read, 1)
                    chain.add(dve.tensor_tensor(dst, dst, b2h[:].rearrange("p (t d) -> p t d", t=1).to_broadcast([P, CH, D]), ALU.add))
                    chain.wait()
                    dve.wait_ge(z_read, c + 1)
                    chain.add(dve.tensor_tensor(dst, dst, z[:, :, :], ALU.add)).wait()
                    for t in range(CH):
                        last = dve.bn_stats(m.stats[:, bass.ds(c * CH + t, 1), :].rearrange("p a s -> p (a s)"),
                                            m.x[:, bass.ds(c * CH + t, 1), :].rearrange("p a d -> p (a d)"))
                    chain.add(last)

                chain.add(dve.tensor_scalar(b2h[:], m.b2_bc[:], 0.5, None, ALU.mult))
                for t in range(B):
                    chain.add(dve.bn_stats(m.stats[:, t, :], m.x[:, t, :]))
                chain.wait()
                for t in range(B):
                    chain.add(dve.bn_aggr(m.mean_var[:, t, :], m.stats[:, t, :]))
                chain.wait()
                inverse_root(dve, chain, m.rstd[:], m.mean_var[:, :, 1], 1e-5, m.root_tmp)
                chain.add(dve.tensor_tensor(m.mean_var[:, :, 1], m.mean_var[:, :, 1], m.rstd[:], ALU.mult)).wait()
                chain.add(dve.tensor_tensor(m.mean_var[:, :, 1], m.mean_var[:, :, 1], m.rstd[:], ALU.mult)).wait()
                inverse_root(dve, chain, rstd2[:], m.mean_var[:, :, 1], 1e-5, m.root_tmp)
                layer_norms(0, 0)
                split_h(0)
                layer_norms(1, 1)
                residual(0, 0)
                split_h(1)
                layer_norms(2, 0)
                residual(1, 1)
                split_h(2)
                layer_norms(3, 1)
                residual(2, 0)
                split_h(3)
                residual(3, 1)
                assert CHUNKS == 4


CHUNK_FILLS_BEFORE = ["xt0", "qa0", "qb0", "xt1"]
CHUNK_FILLS = ["qa", "qb", "at", "wo", "xt"]
CHUNK_FILLS_LAST = ["at", "wo", "at'", "wo'"]
UNITS = 8
AHEAD = 4


class Chunk:

    def __init__(self, pair, parity, turn, first=False, last=False):
        self.pair, self.parity, self.turn, self.first, self.last = pair, parity, turn, first, last
        self.loads_ahead = not last and not (isinstance(pair, int) and pair + 2 >= CHUNKS_2)

    def fill(self, name):
        if self.first:
            return len(CHUNK_FILLS_BEFORE) + [f for f in CHUNK_FILLS if f not in ("at", "wo")].index(name)
        if self.last:
            return self.pair * len(CHUNK_FILLS) + (len(CHUNK_FILLS_BEFORE) - 3 + CHUNK_FILLS_LAST.index(name))
        return self.pair * len(CHUNK_FILLS) + (len(CHUNK_FILLS_BEFORE) - 2 + CHUNK_FILLS.index(name))

    def halved(self, name):
        return self.pair * 3 + (["qa", "qb", "xt"].index(name) + 5)


CHUNKS_2 = 8


def prepare_second_attention(nc, m, lasting):
    keep = lambda name, shape, dt=F32: lasting.enter_context(nc.sbuf_tensor(name, shape, dt))
    H = 16
    m.ident_b = keep("ident_b", [P, P], BF16)
    m.select = keep("select", [3 * H, H, P], BF16)
    m.select_set = lasting.enter_context(nc.semaphore("select_set"))

    def build(pool):
        chain = Chain(pool, m.select_set)
        chain.add(pool.memset(m.select[:], 0.0)).wait()
        for part in range(3):
            chain.add(pool.affine_select(out=m.select[:], in_=m.select[:], compare_op=ALU.not_equal, fill=1.0, base=-part * H,
                                         pattern=[[-1, H], [0, P]], channel_multiplier=1)).wait()
        chain.add(pool.tensor_copy(m.ident_b[:], m.ident[:])).wait()

    m.build_select = build


def second_attention(nc, m):
    B, D = m.x.shape[1], m.x.shape[2]
    S = P
    H, DH = 16, D // 16
    VW = DH + 1
    G = H // 4
    PAIRS = B // 2
    assert PAIRS == CHUNKS_2
    with ExitStack() as ctx:
        sb = lambda name, shape, dt=F32: ctx.enter_context(nc.sbuf_tensor(name, shape, dt))
        sem = lambda name: ctx.enter_context(nc.semaphore(name))
        psum = lambda name, shape: ctx.enter_context(nc.psum_tensor(name, shape, F32))
        xs = sb("s_xs", [P, 2, D])
        xt = sb("s_xt", [P, 2, 2 * S], F32R)
        q1h = sb("s_q1h", [P, 2, 2, 256], F32R)
        q1T = sb("s_q1T", [P, 2, G, 256], F32R)
        kc = sb("s_kc", [P, 2, G, 256], F32R)
        nmx = sb("s_nmx", [P, 2, 4, G])
        rest = sb("s_rest", [P, 2, H])
        parts = sb("s_parts", [P, 3, H], BF16)
        shift = sb("s_shift", [3 * H, 2, S], BF16)
        pT = sb("s_pT", [P, 4, G * S])
        k_blocks = sb("s_k_blocks", [P, 2, G, 4, S], F32R)
        q_blocks = sb("s_q_blocks", [P, 2, G, 4, S], F32R)
        v_wide = sb("s_v_wide", [P, 2, 2, H, 32])
        oT = sb("s_oT", [P, 4 * S])
        rec = sb("s_rec", [P, 2, H])
        at = sb("s_at", [P, 2, 2, D])
        aT = sb("s_aT", [P, 2, S])
        psS, psE = psum("s_psS", [P, 2, 512]), psum("s_psE", [P, 2, 512])
        psO, psR = psum("s_psO", [P, 512]), psum("s_psR", [P, 512])
        psM, psN = psum("s_psM", [P, 512]), psum("s_psN", [3 * H, 512])
        xs_ready, misc_full, misc_done, hi_ready = sem("s_xs_ready"), sem("s_misc_full"), sem("s_misc_done"), sem("s_hi_ready")
        scores_full, max_ready, parts_ready = sem("s_scores_full"), sem("s_max_ready"), sem("s_parts_ready")
        shift_full, shift_ready, shifted_full, probs_ready = sem("s_shift_full"), sem("s_shift_ready"), sem("s_shifted_full"), sem("s_probs_ready")
        values_full, values_copied, rows_full = sem("s_values_full"), sem("s_values_copied"), sem("s_rows_full")
        values_read, chained, v_ready, blank = sem("s_values_read"), sem("s_chained"), sem("s_v_ready"), sem("s_blank")
        keys_in = [[sem(f"s_keys_in{parity}{b}") for b in range(2)] for parity in range(2)]
        queries_in = [sem(f"s_queries_in{b}") for b in range(2)]

        def chunks(engine, body, chain=None):
            body(Chunk(0, 0, 0, first=True))
            body(Chunk(1, 1, 0))
            with engine.Fori(1, PAIRS // 2 - 1) as two:
                if chain:
                    chain.loop(two, 1, CHAINED_2)
                body(Chunk(two * 2, 0, two))
                body(Chunk(two * 2 + 1, 1, two))
                if chain:
                    chain.end(PAIRS // 2 - 1)
            body(Chunk(PAIRS - 2, 0, PAIRS // 2 - 1))
            body(Chunk(PAIRS - 1, 1, PAIRS // 2 - 1, last=True))

        with nc.Block() as block:
            @block.sync
            def _(sp):
                def place_keys(parity, b, batch):
                    keys = bass.ds(batch * S, S)
                    sp.dma_start(kc[:, parity, :, b * S:(b + 1) * S].bitcast(F32), m.k1T[:, :, keys].bitcast(F32)).then_inc(keys_in[parity][b], 16)
                    for j in range(4):
                        rows = slice(32 * j, 32 * j + 3 * DH)
                        sp.dma_start(k_blocks[rows, b, :, j, :].bitcast(F32), m.k1T[rows, :, keys].bitcast(F32)).then_inc(keys_in[parity][b], 16)

                def place_queries(parity, b):
                    for j in range(4):
                        rows = slice(32 * j, 32 * j + 3 * DH)
                        sp.dma_start(q_blocks[rows, b, :, j, :].bitcast(F32), q1T[rows, parity, :, b * S:(b + 1) * S].bitcast(F32)).then_inc(queries_in[b], 16)

                sp.wait_ge(blank, 1)
                place_keys(0, 0, 0)
                place_keys(0, 1, 1)
                sp.wait_ge(misc_done, 3)
                sp.wait_ge(blank, 3)
                place_queries(0, 0)
                place_queries(0, 1)

                def chunk(c):
                    if c.last:
                        return
                    if c.first:
                        sp.wait_ge(scores_full, 4)
                    at_least(sp, shifted_full, c.pair * UNITS)
                    place_keys(1 - c.parity, 0, c.pair * 2 + 2)
                    sp.wait_ge(shifted_full, c.pair * UNITS + 4)
                    place_keys(1 - c.parity, 1, c.pair * 2 + 3)
                    sp.wait_ge(shifted_full, c.pair * UNITS + 6)
                    place_queries(1 - c.parity, 0)
                    sp.wait_ge(shifted_full, c.pair * UNITS + 8)
                    place_queries(1 - c.parity, 1)

                chunks(sp, chunk)

            @block.gpsimd
            def _(pool):
                def place_values(parity, b, batch, used):
                    at_least(pool, values_full, used)
                    pool.tensor_copy(v_wide[:, parity, b, :, 0:DH], m.v1[:, bass.ds(batch, 1), :, 0:DH].rearrange("p a h d -> p (a h) d")).then_inc(v_ready, 1)

                def chunk(c):
                    if not c.last:
                        for b in range(2):
                            place_values(1 - c.parity, b, c.pair * 2 + (2 + b), c.pair * UNITS + (4 * b - 4))

                pool.memset(k_blocks[:].bitcast(F32), 0.0).then_inc(blank, 1)
                pool.memset(v_wide[:], 1.0).then_inc(blank, 1)
                pool.memset(q_blocks[:].bitcast(F32), 0.0).then_inc(blank, 1)
                pool.wait_ge(blank, 2)
                place_values(0, 0, 0, 0)
                place_values(0, 1, 1, 0)
                chunks(pool, chunk)

            @block.tensor
            def _(pe):
                def opened(n):
                    at_least(pe, misc_done, n)

                def transpose_inputs(n, pair):
                    opened(n)
                    pe.wait_ge(xs_ready, pair + 1)
                    for t in range(2):
                        last = pe.transpose(psM[:, t * P:(t + 1) * P], xs[:, t, :], m.ident[:])
                    last.then_inc(misc_full, 1)

                def project_q(n, half):
                    opened(n)
                    for i in range(2):
                        t = 2 * half + i
                        lh, ll = m.wqe[:, 0, t * P:(t + 1) * P], m.wqe[:, 1, t * P:(t + 1) * P]
                        dst = psM[:, 256 * i:256 * i + 256]
                        pe.matmul(dst, lh, xt[:, 0, :], start=True, stop=False)
                        pe.matmul(dst, lh, xt[:, 1, :], start=False, stop=False)
                        last = pe.matmul(dst, ll, xt[:, 0, :], start=False, stop=True)
                    last.then_inc(misc_full, 1)

                def scores(unit, parity, b, t):
                    at_least(pe, max_ready, unit - 1)
                    pe.matmul(psS[:, t % 2, :], q1T[:, parity, t, b * S:(b + 1) * S],
                              k_blocks[:, b, t].rearrange("p j s -> p (j s)"), start=True, stop=True).then_inc(scores_full, 1)

                def transpose_maxima(batch):
                    at_least(pe, shift_ready, batch)
                    pe.wait_ge(parts_ready, batch + 1)
                    pe.matmul(psN[:, 0:S], parts[:, :, :].rearrange("p a h -> p (a h)"), m.ident_b[:],
                              start=True, stop=True).then_inc(shift_full, 1)

                def shifted_scores(c, u):
                    b, t = u // 4, u % 4
                    unit = c.pair * UNITS + u
                    at_least(pe, probs_ready, unit - 1)
                    if t == 0:
                        pe.wait_ge(queries_in[b], c.pair * 64 + 64)
                        pe.wait_ge(shift_ready, c.pair * 2 + (b + 1))
                    pe.matmul(psE[:, t % 2, :], kc[:, c.parity, t, b * S:(b + 1) * S],
                              q_blocks[:, b, t].rearrange("p j s -> p (j s)"), start=True, stop=False)
                    for j in range(4):
                        last = pe.matmul(psE[:, t % 2, j * S:(j + 1) * S], m.select[:, t * 4 + j, :], shift[:, b, :],
                                         start=False, stop=j == 3)
                    last.then_inc(shifted_full, 1)

                def attend(c, local):
                    u = (local - 1) % UNITS
                    b, t = u // 4, u % 4
                    batch = c.pair * 2 + (b if local else -1)
                    parity = c.parity if local else 1 - c.parity
                    pe.wait_ge(probs_ready, c.pair * UNITS + local)
                    if t == 0:
                        at_least(pe, values_copied, batch)
                        pe.wait_ge(v_ready, batch + 1)
                    for j in range(4):
                        last = pe.matmul(psO[32 * j:32 * j + 32, t * S:(t + 1) * S], v_wide[:, parity, b, t * 4 + j, :],
                                         pT[:, t, j * S:(j + 1) * S], start=True, stop=True)
                    last.then_inc(values_full, 1)

                def turn_values(batch):
                    pe.wait_ge(values_copied, batch + 1)
                    at_least(pe, values_read, batch)
                    for t in range(4):
                        last = pe.transpose(psR[:, t * S:(t + 1) * S], oT[:, t * S:(t + 1) * S], m.ident[:])
                    last.then_inc(rows_full, 1)

                def transpose_attended(c, name, batches, parity):
                    opened(c.fill(name))
                    at_least(pe, values_read, batches)
                    for b in range(2):
                        last = pe.transpose(psM[:, b * P:(b + 1) * P], at[:, parity, b, :], m.ident[:])
                    last.then_inc(misc_full, 1)

                def project_out(c, name):
                    opened(c.fill(name))
                    for b in range(2):
                        last = pe.matmul(psM[:, b * P:(b + 1) * P], aT[:, b, :], m.wo1[:], start=True, stop=True)
                    last.then_inc(misc_full, 1)

                transpose_inputs(0, 0)
                project_q(1, 0)
                project_q(2, 1)
                transpose_inputs(3, 1)
                pe.wait_ge(misc_done, 3)
                pe.wait_ge(keys_in[0][0], 80)
                for u in range(AHEAD):
                    scores(u, 0, 0, u)
                transpose_maxima(0)

                def chunk(c):
                    for u in range(UNITS):
                        b, j = u // 4, u % 4
                        shifted_scores(c, u)
                        ahead = not (c.last and b == 1)
                        if ahead:
                            if j == 0:
                                if b == 0:
                                    pe.wait_ge(keys_in[c.parity][1], c.turn * 80 + 80)
                                else:
                                    pe.wait_ge(keys_in[1 - c.parity][0], (c.turn + c.parity) * 80 + 80)
                                if b == 1:
                                    pe.wait_ge(misc_done, c.fill("qb") + 1)
                            for v in {0: (0, 1), 1: (2,), 2: (3,), 3: ()}[j]:
                                scores(c.pair * UNITS + (4 * b + 4 + v), c.parity if b == 0 else 1 - c.parity, 1 - b, v)
                        if not (c.first and u == 0):
                            attend(c, u)
                        if j == 1 and not (c.first and u == 1):
                            turn_values(c.pair * 2 + (b - 1))
                        if ahead and j == 3:
                            transpose_maxima(c.pair * 2 + (b + 1))
                        if u in (0, 1) and not c.last:
                            project_q(c.fill("qa" if u == 0 else "qb"), u)
                        if u == 3 and not c.first:
                            transpose_attended(c, "at", c.pair * 2, 1 - c.parity)
                        if u == 4 and not c.first:
                            project_out(c, "wo")
                        if u == 6 and c.loads_ahead:
                            transpose_inputs(c.fill("xt"), c.pair + 2)

                chunks(pe, chunk)
                end = Chunk(PAIRS - 1, 1, PAIRS // 2 - 1, last=True)
                attend(Chunk(PAIRS, 0, 0), 0)
                turn_values(B - 1)
                transpose_attended(end, "at'", B, 1)
                project_out(end, "wo'")

            @block.scalar
            def _(act):
                def hi_x(n):
                    act.wait_ge(misc_full, n + 1)
                    act.copy(xt[:, 0, :], psM[:, 0:256]).then_inc(hi_ready, 1)

                def hi_q(n, half):
                    act.wait_ge(misc_full, n + 1)
                    for i in range(2):
                        t = 2 * half + i
                        last = act.activation(q1h[:, half, i, :], psM[:, 256 * i:256 * i + 256], ACT.Identity,
                                              scale=m.cols[:, m.mq:m.mq + 1], bias=m.mcols[:, t:t + 1])
                    last.then_inc(hi_ready, 1)

                def copy_shift(batch, b):
                    act.wait_ge(shift_full, batch + 1)
                    at_least(act, shifted_full, batch * 4 - 4)
                    act.copy(shift[:, b, :], psN[:, 0:S]).then_inc(shift_ready, 1)

                def exps(unit, j):
                    act.wait_ge(shifted_full, unit + 1)
                    at_least(act, values_full, unit - 3)
                    act.activation(pT[:, j, :], psE[:, j % 2, :], ACT.Exp).then_inc(probs_ready, 1)

                def copy_values(batch):
                    act.wait_ge(values_full, batch * 4 + 4)
                    at_least(act, rows_full, batch)
                    act.copy(oT[:], psO[:]).then_inc(values_copied, 1)

                hi_x(0)
                hi_q(1, 0)
                hi_q(2, 1)
                hi_x(3)
                copy_shift(0, 0)

                def chunk(c):
                    for u in range(UNITS):
                        b, j = u // 4, u % 4
                        exps(c.pair * UNITS + u, j)
                        if j == 0 and not (c.first and u == 0):
                            copy_values(c.pair * 2 + (b - 1))
                        if j == 3 and not (c.last and b == 1):
                            copy_shift(c.pair * 2 + (b + 1), 1 - b)
                        if u in (0, 1) and not c.last:
                            hi_q(c.fill("qa" if u == 0 else "qb"), u)
                        if u == 6 and c.loads_ahead:
                            hi_x(c.fill("xt"))

                chunks(act, chunk)
                copy_values(B - 1)

            @block.vector
            def _(dve):
                chain = Chain(dve, chained)

                def normalise(pair):
                    for i in range(2):
                        t = pair * 2 + i
                        last = dve.tensor_scalar(xs[:, i, :], m.x[:, bass.ds(t, 1), :].rearrange("p a d -> p (a d)"),
                                                 m.mean_var[:, bass.ds(t, 1), 0], m.rstd[:, bass.ds(t, 1)], ALU.subtract, ALU.mult)
                    last.then_inc(xs_ready, 1)

                def lo_x(n, done):
                    dve.wait_ge(misc_full, n + 1)
                    dve.wait_ge(hi_ready, done)
                    dve.tensor_tensor(xt[:, 1, :], psM[:, 0:256], xt[:, 0, :].bitcast(F32), ALU.subtract).then_inc(misc_done, 1)

                def lo_q(n, half, parity, done):
                    dve.wait_ge(misc_full, n + 1)
                    dve.wait_ge(hi_ready, done)
                    for i in range(2):
                        t = 2 * half + i
                        last = dve.scalar_tensor_tensor(q1T[:, parity, t, :], psM[:, 256 * i:256 * i + 256],
                                                        m.cols[:, m.bq1 + t:m.bq1 + t + 1], q1h[:, half, i, :].bitcast(F32),
                                                        ALU.add, ALU.subtract)
                    last.then_inc(misc_done, 1)

                def row_max(unit, b, j):
                    dve.wait_ge(scores_full, unit + 1)
                    dve.tensor_reduce(nmx[:, b, j, :], psS[:, j % 2, :].rearrange("p (t k) -> p t k", t=G), AX_X, ALU.max,
                                      negate=True).then_inc(max_ready, 1)

                def split_maxima(batch, b):
                    dve.wait_ge(max_ready, batch * 4 + 4)
                    at_least(dve, shift_full, batch)
                    whole = nmx[:, b].rearrange("p t j -> p (t j)")
                    chain.add(dve.tensor_copy(parts[:, 0, :], whole)).wait()
                    chain.add(dve.tensor_tensor(rest[:, 0, :], whole, parts[:, 0, :], ALU.subtract)).wait()
                    chain.add(dve.tensor_copy(parts[:, 1, :], rest[:, 0, :])).wait()
                    dve.tensor_tensor(parts[:, 2, :], rest[:, 0, :], parts[:, 1, :], ALU.subtract).then_inc(parts_ready, 1)

                def normalise_attended(b, batches):
                    dve.wait_ge(rows_full, batches)
                    o = psR[:].rearrange("p (h d) -> p h d", h=H)
                    chain.add(dve.reciprocal(rec[:, b, :], o[:, :, DH])).wait()
                    return o

                def scale_attended(o, parity, b):
                    dve.tensor_tensor(at[:, parity, b, :].rearrange("p (h d) -> p h d", h=H), o[:, :, 0:DH],
                                      rec[:, b, :].rearrange("p (h d) -> p h d", d=1).to_broadcast([P, H, DH]), ALU.mult).then_inc(values_read, 1)

                def copy_attended(n):
                    dve.wait_ge(misc_full, n + 1)
                    dve.tensor_copy(aT[:, :, :], psM[:, 0:256].rearrange("p (b s) -> p b s", b=2)).then_inc(misc_done, 1)

                def residual(n, pair):
                    dve.wait_ge(misc_full, n + 1)
                    dst = m.x[:, bass.ds(pair * 2, 2), :]
                    dve.tensor_tensor(dst, dst, psM[:, 0:256].rearrange("p (b d) -> p b d", b=2), ALU.add).then_inc(misc_done, 1)
                    dve.wait_ge(misc_done, n + 1)
                    chain.add(dve.tensor_tensor(dst, dst, m.bo1_bc[:].rearrange("p (b d) -> p b d", b=1).to_broadcast([P, 2, D]), ALU.add))
                    chain.wait()
                    for t in range(2):
                        last = dve.bn_stats(m.stats[:, bass.ds(pair * 2 + t, 1), :].rearrange("p a s -> p (a s)"),
                                            m.x[:, bass.ds(pair * 2 + t, 1), :].rearrange("p a d -> p (a d)"))
                    chain.add(last)

                for t in range(B):
                    chain.add(dve.bn_aggr(m.mean_var[:, t, :], m.stats[:, t, :]))
                chain.wait()
                inverse_root(dve, chain, m.rstd[:], m.mean_var[:, :, 1], 1e-5, m.root_tmp)
                normalise(0)
                lo_x(0, 1)
                normalise(1)
                lo_q(1, 0, 0, 2)
                lo_q(2, 1, 0, 3)
                lo_x(3, 4)
                for u in range(AHEAD):
                    row_max(u, 0, u)
                split_maxima(0, 0)

                def chunk(c):
                    for u in range(UNITS):
                        b, j = u // 4, u % 4
                        ahead = not (c.last and b == 1)
                        first_max = c.pair * UNITS + (4 * b + 4)
                        if ahead and j < 3:
                            row_max(first_max + (0, 2, 3)[j], 1 - b, (0, 2, 3)[j])
                        if ahead and j == 0:
                            row_max(first_max + 1, 1 - b, 1)
                        if ahead and j == 2:
                            split_maxima(c.pair * 2 + (b + 1), 1 - b)
                        if u in (0, 1) and not c.last:
                            at_least(dve, shifted_full, c.pair * UNITS)
                            name = "qa" if u == 0 else "qb"
                            lo_q(c.fill(name), u, 1 - c.parity, c.halved(name))
                        if j == 2 and not (c.first and u == 2):
                            o = normalise_attended(1 - b, c.pair * 2 + b)
                            scale_attended(o, c.parity if b else 1 - c.parity, 1 - b)
                        if u == 3 and not c.first:
                            copy_attended(c.fill("at"))
                        if u == 4 and not c.first:
                            residual(c.fill("wo"), c.pair - 1)
                        if u == 4 and c.loads_ahead:
                            normalise(c.pair + 2)
                        if u == 6 and c.loads_ahead:
                            lo_x(c.fill("xt"), c.halved("xt"))

                chunks(dve, chunk, chain)
                end = Chunk(PAIRS - 1, 1, PAIRS // 2 - 1, last=True)
                o = normalise_attended(1, B)
                scale_attended(o, 1, 1)
                copy_attended(end.fill("at'"))
                residual(end.fill("wo'"), PAIRS - 1)


CHAINED_2 = 20


CAP_FACTOR, TOP = 1.25, 2
RING = 2


def prepare_experts(nc, m, T, lasting):
    D, E = P, T["L1_ffn_router_w"].shape[0]
    IR, IS = T["L1_ffn_rg"].shape[2], T["L1_ffn_sg"].shape[1]
    keep = lambda name, shape, dt=F32: lasting.enter_context(nc.sbuf_tensor(name, shape, dt))
    sem = lambda name: lasting.enter_context(nc.semaphore(name))
    m.E, m.IR, m.IS = E, IR, IS
    m.capacity = max(int(CAP_FACTOR * m.x.shape[1] * P / E), 1)
    m.slots = E * m.capacity
    m.router = keep("router", [E, D])
    m.sd = keep("sd", [P, IS // P, D])
    m.sgu = keep("sgu", [P, 2, 2, IS], F32R)
    m.sgu_raw = keep("sgu_raw", [P, 2, IS])
    m.rgu = keep("rgu", [P, RING, 2, 2, IR], F32R)
    m.rgu_raw = keep("rgu_raw", [P, RING, 2, IR])
    m.rd = keep("rd", [P, RING, IR // P, D])
    m.zeros = keep("zeros", [P, D])
    m.gathered = nc.dram_tensor("gathered", (m.slots, D), F32, kind="Internal").ap()
    m.expert_out = nc.dram_tensor("expert_out", (m.slots + 1, D), F32, kind="Internal").ap()
    m.shared_loaded, m.zeroed, m.zeros_set = sem("shared_loaded"), sem("zeroed"), sem("zeros_set")
    m.raw_loaded = [sem(f"raw_loaded{i}") for i in range(RING)]
    m.rd_loaded = [sem(f"rd_loaded{i}") for i in range(RING)]
    m.shared_split, m.expert_split, m.pool_chained = sem("shared_split"), sem("expert_split"), sem("pool_chained")

    def load_expert(sp, e, slot):
        index = lambda name: T[name][bass.ds(e, 1)].rearrange("a k n -> k (a n)")
        sp.dma_start(m.rgu_raw[:, slot, 0, :], index("L1_ffn_rg")).then_inc(m.raw_loaded[slot], 16)
        sp.dma_start(m.rgu_raw[:, slot, 1, :], index("L1_ffn_ru")).then_inc(m.raw_loaded[slot], 16)

    def load_down(sp, e, slot):
        sp.dma_start(m.rd[:, slot, :, :], T["L1_ffn_rd"][bass.ds(e, 1)].rearrange("a (t p) n -> p (a t) n", p=P)).then_inc(m.rd_loaded[slot], 16)

    def load_experts(block):
        @block.gpsimd
        def _(pool):
            pool.memset(m.zeros[:], 0.0).then_inc(m.zeros_set, 1)
            m.build_select(pool)
            split_experts(pool)

        @block.sync
        def _(sp):
            sp.dma_start(m.sgu_raw[:, 0, :], T["L1_ffn_sg"]).then_inc(m.shared_loaded, 16)
            sp.dma_start(m.sgu_raw[:, 1, :], T["L1_ffn_su"]).then_inc(m.shared_loaded, 16)
            sp.dma_start(m.sd[:], T["L1_ffn_sd"].rearrange("(t p) n -> p t n", p=P)).then_inc(m.shared_loaded, 16)
            sp.dma_start(m.router[:], T["L1_ffn_router_w"]).then_inc(m.shared_loaded, 16)
            for e in range(RING):
                load_expert(sp, e, e)
                load_down(sp, e, e)
            sp.wait_ge(m.zeros_set, 1)
            tiles = m.slots // P
            sp.dma_start(m.gathered.rearrange("(t p) d -> p t d", p=P),
                         m.zeros[:].rearrange("p (t d) -> p t d", t=1).to_broadcast([P, tiles, D])).then_inc(m.zeroed, 16)
            sp.dma_start(m.expert_out[m.slots:m.slots + 1, :], m.zeros[0:1, :]).then_inc(m.zeroed, 16)

    def split(pool, chain, dst, src):
        for i in range(2):
            chain.add(pool.tensor_copy(dst[:, i, 0, :], src[:, i, :]))
        chain.wait()
        pool.tensor_tensor(dst[:, 0, 1, :], src[:, 0, :], dst[:, 0, 0, :].bitcast(F32), ALU.subtract)
        return pool.tensor_tensor(dst[:, 1, 1, :], src[:, 1, :], dst[:, 1, 0, :].bitcast(F32), ALU.subtract)

    def split_experts(pool):
        chain = Chain(pool, m.pool_chained)
        pool.wait_ge(m.shared_loaded, 64)
        split(pool, chain, m.sgu, m.sgu_raw).then_inc(m.shared_split, 1)
        for e in range(RING):
            pool.wait_ge(m.raw_loaded[e], 32)
            split(pool, chain, m.rgu[:, e], m.rgu_raw[:, e]).then_inc(m.expert_split, 1)

    m.load_expert, m.load_down, m.load_experts, m.split, m.split_experts = load_expert, load_down, load_experts, split, split_experts


def mixture(nc, m, T, out):
    B, D = m.x.shape[1], m.x.shape[2]
    E, IR, IS, CAP, SLOTS = m.E, m.IR, m.IS, m.capacity, m.slots
    N = 256
    FS, FE = IS // P, IR // P
    ST = SLOTS // P
    assert SLOTS % P == 0 and CAP <= 512 and CAP % 2 == 0 and RING == 2 and TOP == 2
    SLOT_TILES = [(a, min(P, CAP - a)) for a in range(0, CAP, P)]
    with ExitStack() as ctx:
        sb = lambda name, shape, dt=F32: ctx.enter_context(nc.sbuf_tensor(name, shape, dt))
        sem = lambda name: ctx.enter_context(nc.semaphore(name))
        psum = lambda name, shape: ctx.enter_context(nc.psum_tensor(name, shape, F32))
        u = sb("m_u", [P, B, D])
        k1T = m.k1T[:, :, :].rearrange("p g n -> p (g n)")
        uT = k1T[:, 0:2 * B * P].rearrange("p (h n) -> p h n", h=2)
        xgT_hi = k1T[:, 2 * B * P:2 * B * P + SLOTS]
        xgT_lo = sb("m_xgT_lo", [P, SLOTS], F32R)
        xg = sb("m_xg", [P, ST, D])
        rwT = sb("m_rwT", [P, 2, E], F32R)
        rms = sb("m_rms", [P, B])
        iota = sb("m_iota", [P, E])
        ones, tri = sb("m_ones", [P, P]), sb("m_tri", [P, P])
        logits, top = sb("m_logits", [P, B, E]), sb("m_top", [P, B, 8])
        index = sb("m_index", [P, B, 8], U32)
        chosen = sb("m_chosen", [P, 2, B])
        one_hot = sb("m_one_hot", [P, 2, B, E])
        mask = sb("m_mask", [P, B, E])
        prefix = sb("m_prefix", [P, 2, B, E])
        place = sb("m_place", [P, 2, B, E])
        pos = sb("m_pos", [P, 2, B])
        valid = sb("m_valid", [P, 2, B])
        slot = sb("m_slot", [P, 2, B], U32)
        weight = sb("m_weight", [P, 2, B])
        gap = sb("m_gap", [P, 2, B])
        s = sb("m_s", [P, 2, 512])
        a = sb("m_a", [P, 2, FS, N])
        ae = a[:, :, :, :].rearrange("p b f n -> p b (f n)")[:, :, 0:FE * CAP].rearrange("p b (f n) -> p b f n", f=FE)
        eo = sb("m_eo", [P, 2, len(SLOT_TILES), D])
        picked = [sb("m_picked", [P, 2, B // 2, D]), u[:].rearrange("p (c t) d -> p c t d", c=2)]
        psG, psU, psD, psX = psum("m_psG", [P, 2, 512]), psum("m_psU", [P, 2, 512]), psum("m_psD", [P, 2, 512]), psum("m_psX", [P, 2, 512])
        consts, u_ready, x_full, x_done, hi_done = sem("m_consts"), sem("m_u_ready"), sem("m_x_full"), sem("m_x_done"), sem("m_hi_done")
        gap_ready, gap_exp, mask_ready, slot_ready = sem("m_gap_ready"), sem("m_gap_exp"), sem("m_mask_ready"), sem("m_slot_ready")
        scattered, xg_loaded, w_hi = sem("m_scattered"), sem("m_xg_loaded"), sem("m_w_hi")
        gu_full, s_ready, a_ready, down_full, down_read = sem("m_gu_full"), sem("m_s_ready"), sem("m_a_ready"), sem("m_down_full"), sem("m_down_read")
        eo_stored, picked_in, combined, stored = [sem("m_eo_stored0"), sem("m_eo_stored1")], [sem(f"m_picked{i}") for i in range(4)], sem("m_combined"), sem("m_stored")
        chained = sem("m_chained")
        SH_ROUNDS = B * P // N // 4
        EX_ROUNDS = E // 2

        class Section:
            def __init__(self, kind, i, part=0, last=False):
                self.kind, self.i, self.part, self.last = kind, i, part, last
                self.first = kind == "shared" and part == 0 and isinstance(i, int) and i == 0
                self.tiles = FE if kind == "expert" else FS
                if kind == "expert":
                    self.tile0 = i * (2 * FE) + SH_ROUNDS * 2 * FS
                    self.job0 = i * 2 + SH_ROUNDS * 2
                else:
                    self.tile0 = i * (2 * FS) + part * (SH_ROUNDS * 2 * FS + EX_ROUNDS * 2 * FE)
                    self.job0 = i * 2 + part * (SH_ROUNDS * 2 + EX_ROUNDS * 2)
                self.item0 = i * 2 + (part * SH_ROUNDS * 2 if kind == "shared" else 0)

        def sections(engine, body, before_experts=None):
            for i in range(SH_ROUNDS):
                body(Section("shared", i))
            if before_experts:
                before_experts()
            body(Section("expert", 0))
            with engine.Fori(1, EX_ROUNDS - 1) as i:
                body(Section("expert", i))
            body(Section("expert", EX_ROUNDS - 1, last=True))
            for i in range(SH_ROUNDS):
                body(Section("shared", i, 1, last=i == SH_ROUNDS - 1))

        X_ROUTER, X_UT, X_LOGITS, X_PLACE, X_XGT = 0, 1, 5, 6, 7
        XG_FILLS = ST // 4
        COMBINE_AT = (2, 6, 12)
        ROUTER_COUNT = 6
        with nc.Block() as block:
            @block.sync
            def _(sp):
                for b in range(2):
                    m.load_expert(sp, 2 + b, b)
                sp.wait_ge(scattered, 16 * 2 * B)
                sp.dma_start(xg[:], m.gathered.rearrange("(t p) d -> p t d", p=P)).then_inc(xg_loaded, 16)

                def expert_round(i):
                    if not (isinstance(i, int) and i + 2 >= EX_ROUNDS):
                        for b in range(2):
                            sp.wait_ge(m.expert_split, i * 2 + (b + 3))
                            m.load_expert(sp, (i + 2) * 2 + b, b)
                    if not (isinstance(i, int) and i + 1 >= EX_ROUNDS):
                        for b in range(2):
                            sp.wait_ge(down_full, i * 2 + (SH_ROUNDS * 2 + b + 1))
                            m.load_down(sp, (i + 1) * 2 + b, b)
                    for b in range(2):
                        sp.wait_ge(down_read, i * 2 + (SH_ROUNDS * 2 + b + 1))
                        whole, (at, rows) = len(SLOT_TILES) - 1, SLOT_TILES[-1]
                        sp.dma_start(m.expert_out[bass.ds((i * 2 + b) * CAP, at)].rearrange("(t p) d -> p t d", p=P),
                                     eo[:, b, 0:whole, :]).then_inc(eo_stored[b], 16)
                        sp.dma_start(m.expert_out[bass.ds((i * 2 + b) * CAP + at, rows)],
                                     eo[0:rows, b, whole, :]).then_inc(eo_stored[b], 16)

                with sp.Fori(0, EX_ROUNDS - 2) as i:
                    expert_round(i)
                for i in range(EX_ROUNDS - 2, EX_ROUNDS):
                    expert_round(i)
                for g in range(4):
                    sp.wait_ge(combined, g + 1)
                    sp.dma_start(out[4 * g:4 * g + 4].rearrange("b s d -> s b d"), m.x[:, 4 * g:4 * g + 4, :]).then_inc(stored, 16)
                sp.wait_ge(stored, 64)

            @block.gpsimd
            def _(pool):
                pool.memset(ones[:], 1.0).then_inc(consts, 1)
                for e in range(E):
                    last = pool.memset(iota[:, e:e + 1], float(e))
                last.then_inc(consts, 1)
                pool.wait_ge(consts, 1)
                pool.affine_select(out=tri[:], in_=ones[:], compare_op=ALU.is_gt, fill=0.0, base=0,
                                   pattern=[[1, P]], channel_multiplier=-1).then_inc(consts, 1)
                pool.wait_ge(slot_ready, 1)
                pool.wait_ge(m.zeroed, 32)
                for t in range(B):
                    for c in range(TOP):
                        pool.indirect_dma_start(m.gathered, bass.IndirectOffsetOnAxis(ap=slot[:, c, t:t + 1], axis=0),
                                                u[:, t, :], None, bounds_check=SLOTS - 1, oob_is_err=False).then_inc(scattered, 16)
                for b in range(2):
                    pool.wait_ge(eo_stored[b], 32 * EX_ROUNDS)
                for t in range(B):
                    for c in range(TOP):
                        pool.indirect_dma_start(picked[t // 8][:, c, t % 8, :], None, m.expert_out,
                                                bass.IndirectOffsetOnAxis(ap=slot[:, c, t:t + 1], axis=0)).then_inc(picked_in[t // 4], 16)

            @block.tensor
            def _(pe):
                def product(dst, lh, ll, rh, rl):
                    pe.matmul(dst, lh, rh, start=True, stop=False)
                    pe.matmul(dst, lh, rl, start=False, stop=False)
                    return pe.matmul(dst, ll, rh, start=False, stop=True)

                pe.transpose(psX[:, 0, 0:E], m.router[:], m.ident[0:E, 0:E]).then_inc(x_full, 1)
                for f in range(4):
                    n = X_UT + f
                    at_least(pe, x_done, n - 1)
                    pe.wait_ge(u_ready, f + 1)
                    for t in range(4):
                        last = pe.transpose(psX[:, n % 2, t * P:(t + 1) * P], u[:, 4 * f + t, :], m.ident[:])
                    last.then_inc(x_full, 1)
                pe.wait_ge(x_done, X_LOGITS)
                for t in range(B):
                    part = slice(t * P, (t + 1) * P)
                    at = t * 2 * E
                    pe.matmul(psX[:, X_LOGITS % 2, at:at + 2 * E], uT[:, 0, part], rwT[:, :, :].rearrange("p h e -> p (h e)"),
                              start=True, stop=False)
                    last = pe.matmul(psX[:, X_LOGITS % 2, at:at + E], uT[:, 1, part], rwT[:, 0, :], start=False, stop=True)
                last.then_inc(x_full, 1)
                def count_chosen():
                    pe.wait_ge(mask_ready, 1)
                    pe.wait_ge(consts, 3)
                    chosen_in = mask[:, :, :].rearrange("p b e -> p (b e)")
                    pe.matmul(psX[:, X_PLACE % 2, 0:B * E], tri[:], chosen_in, start=True, stop=True)
                    pe.matmul(psX[:, X_PLACE % 2, B * E:2 * B * E], ones[:], chosen_in, start=True, stop=True).then_inc(x_full, 1)

                def jobs(sec):
                    n = N if sec.kind == "shared" else CAP
                    for b in range(2):
                        if sec.kind == "expert":
                            pe.wait_ge(m.expert_split, sec.item0 + b + 1)
                        for f in range(sec.tiles):
                            k = b * sec.tiles + f
                            tile = sec.tile0 + k
                            at_least(pe, a_ready, tile - 1)
                            w = m.sgu if sec.kind == "shared" else m.rgu[:, b]
                            cols = slice(f * P, (f + 1) * P)
                            at = bass.ds((sec.item0 + b) * n, n)
                            rh, rl = (uT[:, 0, at], uT[:, 1, at]) if sec.kind == "shared" else (xgT_hi[:, at], xgT_lo[:, at])
                            product(psG[:, k % 2, 0:n], w[:, 0, 0, cols], w[:, 0, 1, cols], rh, rl)
                            product(psU[:, k % 2, 0:n], w[:, 1, 0, cols], w[:, 1, 1, cols], rh, rl).then_inc(gu_full, 1)
                            if sec.first and k == ROUTER_COUNT:
                                count_chosen()
                    for b in range(2):
                        pe.wait_ge(a_ready, sec.tile0 + (b + 1) * sec.tiles)
                        at_least(pe, down_read, sec.job0 + (b - 1))
                        if sec.kind == "expert":
                            pe.wait_ge(m.rd_loaded[b], sec.i * 16 + 16)
                        tiles = SLOT_TILES if sec.kind == "expert" else [(c, P) for c in range(0, N, P)]
                        w, act = (m.rd[:, b], ae) if sec.kind == "expert" else (m.sd, a)
                        for c, (at, rows) in enumerate(tiles):
                            for f in range(sec.tiles):
                                last = pe.matmul(psD[0:rows, b, c * P:(c + 1) * P], act[:, b, f, at:at + rows], w[:, f, :],
                                                 start=f == 0, stop=f == sec.tiles - 1)
                        last.then_inc(down_full, 1)

                def transpose_slots():
                    pe.wait_ge(xg_loaded, 16)
                    for f in range(XG_FILLS):
                        n = X_XGT + f
                        pe.wait_ge(x_done, n - 1)
                        for t in range(4):
                            last = pe.transpose(psX[:, n % 2, t * P:(t + 1) * P], xg[:, 4 * f + t, :], m.ident[:])
                        last.then_inc(x_full, 1)
                    pe.wait_ge(x_done, X_XGT + XG_FILLS)

                pe.wait_ge(m.shared_split, 1)
                sections(pe, jobs, transpose_slots)

            @block.scalar
            def _(act):
                def hi(n, dst):
                    act.wait_ge(x_full, n + 1)
                    act.copy(dst, psX[:, n % 2, :]).then_inc(hi_done, 1)

                for f in range(4):
                    hi(X_UT + f, uT[:, 0, f * 512:(f + 1) * 512])

                def jobs(sec):
                    n = N if sec.kind == "shared" else CAP
                    for b in range(2):
                        for f in range(sec.tiles):
                            k = b * sec.tiles + f
                            act.wait_ge(gu_full, sec.tile0 + k + 1)
                            act.activation(s[:, k % 2, 0:n], psG[:, k % 2, 0:n], ACT.Silu).then_inc(s_ready, 1)
                    if sec.kind == "expert" and not sec.last:
                        for b in range(2):
                            act.wait_ge(m.raw_loaded[b], sec.i * 32 + 64)
                            act.copy(m.rgu[:, b, :, 0, :], m.rgu_raw[:, b]).then_inc(w_hi, 1)
                    if sec.kind == "expert":
                        for b in range(2):
                            job = sec.job0 + b
                            act.wait_ge(down_full, job + 1)
                            at_least(act, eo_stored[b], sec.i * 32)
                            whole = len(SLOT_TILES) - 1
                            act.copy(eo[:, b, 0:whole, :], psD[:, b, 0:whole * P].rearrange("p (t d) -> p t d", t=whole))
                            rows = SLOT_TILES[-1][1]
                            ins = act.copy(eo[0:rows, b, whole, :], psD[0:rows, b, whole * P:(whole + 1) * P])
                            ins.then_inc(down_read, 1)

                def slots():
                    act.wait_ge(gap_ready, 1)
                    act.activation(gap[:, 1, :], gap[:, 0, :], ACT.Exp).then_inc(gap_exp, 1)
                    for f in range(XG_FILLS):
                        hi(X_XGT + f, xgT_hi[:, f * 512:(f + 1) * 512])

                sections(act, jobs, slots)

            @block.vector
            def _(dve):
                chain = Chain(dve, chained)
                C = lambda ins: chain.add(ins).wait()
                for t in range(B):
                    chain.add(dve.bn_aggr(m.mean_var[:, t, :], m.stats[:, t, :]))
                chain.wait()
                inverse_root(dve, chain, m.rstd[:], m.mean_var[:, :, 1], 1e-5, m.root_tmp)
                for t in range(B):
                    last = dve.tensor_scalar(u[:, t, :], m.x[:, t, :], m.mean_var[:, t, 0:1], m.rstd[:, t:t + 1], ALU.subtract, ALU.mult)
                    if t % 4 == 3:
                        last.then_inc(u_ready, 1)
                dve.wait_ge(x_full, 1)
                C(dve.tensor_copy(rwT[:, 0, :], psX[:, 0, 0:E]))
                dve.tensor_tensor(rwT[:, 1, :], psX[:, 0, 0:E], rwT[:, 0, :].bitcast(F32), ALU.subtract).then_inc(x_done, 1)

                def lo(n, done, dst, hi):
                    dve.wait_ge(hi_done, done)
                    dve.tensor_tensor(dst, psX[:, n % 2, :], hi.bitcast(F32), ALU.subtract).then_inc(x_done, 1)

                for f in range(4):
                    part = slice(f * 512, (f + 1) * 512)
                    lo(X_UT + f, f + 1, uT[:, 1, part], uT[:, 0, part])
                def logits_and_top():
                    C(dve.tensor_tensor(m.mean_var[:, :, 1], m.mean_var[:, :, 1], m.rstd[:], ALU.mult))
                    C(dve.tensor_tensor(m.mean_var[:, :, 1], m.mean_var[:, :, 1], m.rstd[:], ALU.mult))
                    inverse_root(dve, chain, rms[:], m.mean_var[:, :, 1], 1.1920929e-07, m.root_tmp)
                    dve.wait_ge(x_full, X_LOGITS + 1)
                    parts = psX[:, X_LOGITS % 2, :].rearrange("p (b h e) -> p b h e", h=2, e=E)
                    C(dve.tensor_copy(logits[:, :, :], parts[:, 0:B, 0, :]))
                    dve.tensor_tensor(logits[:, :, :], parts[:, 0:B, 1, :], logits[:, :, :], ALU.add).then_inc(x_done, 1)
                    dve.wait_ge(x_done, X_LOGITS + 1)
                    C(dve.tensor_tensor(logits[:, :, :], logits[:, :, :], rms[:].rearrange("p (b e) -> p b e", e=1).to_broadcast([P, B, E]), ALU.mult))
                    for t in range(B):
                        chain.add(dve.max(top[:, t, :], logits[:, t, :]))
                    chain.wait()

                def top_two():
                    for t in range(B):
                        chain.add(dve.max_index(index[:, t, :], top[:, t, :], logits[:, t, :]))
                    dve.tensor_tensor(gap[:, 0, :], top[:, :, 1], top[:, :, 0], ALU.subtract).then_inc(gap_ready, 1)
                    chain.wait()
                    for c in range(TOP):
                        chain.add(dve.tensor_copy(chosen[:, c, :], index[:, :, c]))
                    chain.wait()

                def choose():
                    dve.wait_ge(consts, 2)
                    for c in range(TOP):
                        chain.add(dve.tensor_tensor(one_hot[:, c], iota[:].rearrange("p (b e) -> p b e", b=1).to_broadcast([P, B, E]),
                                                    chosen[:, c, :].rearrange("p (b e) -> p b e", e=1).to_broadcast([P, B, E]), ALU.is_equal))
                    chain.wait()
                    dve.tensor_tensor(mask[:, :, :], one_hot[:, 0], one_hot[:, 1], ALU.add).then_inc(mask_ready, 1)

                placed = psX[:, X_PLACE % 2, :]

                def counts_of_batches():
                    dve.wait_ge(x_full, X_PLACE + 1)
                    total = placed[:, B * E:2 * B * E].rearrange("p (b e) -> p b e", e=E)
                    chain.add(dve.memset(prefix[:, 0, 0:1, :], 0.0))
                    C(dve.tensor_copy(prefix[:, 0, 1:B, :], total[:, 0:B - 1, :]))
                    now, step = 0, 1
                    while step < B:
                        chain.add(dve.tensor_copy(prefix[:, 1 - now, 0:step, :], prefix[:, now, 0:step, :]))
                        C(dve.tensor_tensor(prefix[:, 1 - now, step:B, :], prefix[:, now, step:B, :], prefix[:, now, 0:B - step, :], ALU.add))
                        now, step = 1 - now, step * 2
                    return now

                def places(now):
                    within = placed[:, 0:B * E].rearrange("p (b e) -> p b e", e=E)
                    ins = dve.tensor_tensor(prefix[:, 1 - now], within, prefix[:, now], ALU.add)
                    ins.then_inc(x_done, 1)
                    dve.wait_ge(x_done, X_PLACE + 1)
                    for c in range(TOP):
                        chain.add(dve.tensor_tensor(place[:, c], one_hot[:, c], prefix[:, 1 - now], ALU.mult))
                    chain.wait()
                    C(dve.tensor_reduce(pos[:], place[:, :, :, :], AX_X, ALU.add))

                def slots_of_tokens():
                    chain.add(dve.tensor_scalar(valid[:], pos[:], float(CAP), None, ALU.is_lt))
                    C(dve.scalar_tensor_tensor(pos[:], chosen[:], float(CAP), pos[:], ALU.mult, ALU.add))
                    C(dve.scalar_tensor_tensor(pos[:], pos[:], float(-SLOTS), valid[:], ALU.add, ALU.mult))
                    dve.tensor_scalar(slot[:], pos[:], float(SLOTS), None, ALU.add).then_inc(slot_ready, 1)

                def weights():
                    dve.wait_ge(gap_exp, 1)
                    C(dve.tensor_scalar(weight[:, 0, :], gap[:, 1, :], 1.0, None, ALU.add))
                    C(dve.reciprocal(weight[:, 0, :], weight[:, 0, :]))
                    C(dve.tensor_tensor(weight[:, 1, :], gap[:, 1, :], weight[:, 0, :], ALU.mult))

                def combine(t, c):
                    return dve.scalar_tensor_tensor(m.x[:, t, :], picked[t // 8][:, c, t % 8, :], weight[:, c, t:t + 1],
                                                    m.x[:, t, :], ALU.mult, ALU.add)

                def combine_group(g):
                    dve.wait_ge(picked_in[g], 16 * TOP * 4)
                    dve.wait_ge(down_read, EX_ROUNDS * 2 + (8 if g == 3 else 6))
                    for c in range(TOP):
                        for t in range(4 * g, 4 * g + 4):
                            last = combine(t, c)
                            if c == 0:
                                chain.add(last)
                        if c == 0:
                            chain.wait()
                    last.then_inc(combined, 1)

                def jobs(sec):
                    n = N if sec.kind == "shared" else CAP
                    for b in range(2):
                        for f in range(sec.tiles):
                            k = b * sec.tiles + f
                            if sec.first and k == 0:
                                logits_and_top()
                            if sec.first and k == 2:
                                top_two()
                            if sec.first and k == 4:
                                choose()
                            if sec.first and k == ROUTER_COUNT + 2:
                                now = counts_of_batches()
                            if sec.first and k == ROUTER_COUNT + 4:
                                places(now)
                                slots_of_tokens()
                            if sec.kind == "shared" and sec.part == 1 and sec.last and k in COMBINE_AT:
                                g = COMBINE_AT.index(k)
                                combine_group(g)
                            dve.wait_ge(s_ready, sec.tile0 + k + 1)
                            if f == 0:
                                at_least(dve, down_full, sec.job0 + (b - 1))
                            dst = a[:, b, f, :] if sec.kind == "shared" else ae[:, b, f, :]
                            dve.tensor_tensor(dst, s[:, k % 2, 0:n], psU[:, k % 2, 0:n], ALU.mult).then_inc(a_ready, 1)
                    if sec.kind == "expert" and not sec.last:
                        for b in range(2):
                            dve.wait_ge(w_hi, sec.i * 2 + b + 1)
                            dve.tensor_tensor(m.rgu[:, b, :, 1, :], m.rgu_raw[:, b], m.rgu[:, b, :, 0, :].bitcast(F32),
                                              ALU.subtract).then_inc(m.expert_split, 1)
                    if sec.kind == "shared":
                        for b in range(2):
                            dve.wait_ge(down_full, sec.job0 + b + 1)
                            dst = m.x[:, bass.ds((sec.item0 + b) * (N // P), N // P), :]
                            dve.tensor_tensor(dst, dst, psD[:, b, 0:N].rearrange("p (t d) -> p t d", t=N // P), ALU.add).then_inc(down_read, 1)

                def slots():
                    weights()
                    for f in range(XG_FILLS):
                        part = slice(f * 512, (f + 1) * 512)
                        lo(X_XGT + f, 4 + f + 1, xgT_lo[:, part], xgT_hi[:, part])

                sections(dve, jobs, slots)
                combine_group(3)



_INS = ["x", "ctx_1024", "L0_xattn_wq_w", "L0_xattn_wq_b", "L0_xattn_wk_w", "L0_xattn_wk_b", "L0_xattn_wv_w",
        "L0_xattn_wv_b", "L0_xattn_mk", "L0_xattn_mv", "L0_xattn_wo_w", "L0_xattn_wo_b", "L0_ffn_ln_gamma",
        "L0_ffn_ln_beta", "L0_ffn_fc1_q", "L0_ffn_fc1_scales", "L0_ffn_fc1_bias", "L0_ffn_fc2_q", "L0_ffn_fc2_scales",
        "L0_ffn_fc2_bias", "L1_xattn_Wq", "L1_xattn_bq", "L1_xattn_Wkv", "L1_xattn_bkv", "L1_xattn_Wo", "L1_xattn_bo",
        "L1_ffn_router_w", "L1_ffn_rg", "L1_ffn_ru", "L1_ffn_rd", "L1_ffn_sg", "L1_ffn_su", "L1_ffn_sd"]


def kernel(**inputs):
    import numpy as np
    import concourse.bacc as bacc
    from concourse.bass_utils import run_bass_kernel_spmd

    nc = bacc.Bacc("TRN2", target_bir_lowering=False, num_devices=1)
    arrays, tensors = {}, {}
    for name in _INS:
        a = np.ascontiguousarray(inputs[name])
        arrays[f"in_{name}"] = a
        tensors[name] = nc.dram_tensor(f"in_{name}", a.shape, mybir.dt.from_np(a.dtype), kind="ExternalInput").ap()
    out = nc.dram_tensor("out", inputs["x"].shape, F32, kind="ExternalOutput").ap()
    transformer(nc, tensors, out)
    return run_bass_kernel_spmd(nc, [arrays], core_ids=[0]).results[0]["out"]
```

```python
from contextlib import ExitStack

import concourse.bass as bass
from concourse import mybir

ALU = mybir.AluOpType
ACT = mybir.ActivationFunctionType
F32 = mybir.dt.float32
F32R = mybir.dt.float32r
I32 = mybir.dt.int32
U32 = mybir.dt.uint32
BF16 = mybir.dt.bfloat16
AX_X = mybir.AxisListType.X

P = 128


class Shared:
    pass


def at_least(engine, semaphore, value):
    if not (isinstance(value, int) and value <= 0):
        engine.wait_ge(semaphore, value)


class Chain:

    def __init__(self, engine, semaphore):
        self.engine, self.semaphore, self.count = engine, semaphore, 0
        self.turn, self.start, self.each = None, 0, 0

    def loop(self, turn, first, each):
        self.turn, self.start, self.each = turn, self.count - first * each, each
        self.count = 0

    def end(self, last):
        assert self.count == self.each, (self.count, self.each)
        self.count = self.start + last * self.each
        self.turn = None

    def add(self, instruction):
        instruction.then_inc(self.semaphore, 1)
        self.count += 1
        return self

    def wait(self):
        if self.turn is None:
            self.engine.wait_ge(self.semaphore, self.count)
        else:
            self.engine.wait_ge(self.semaphore, self.turn * self.each + (self.start + self.count))


def root_guess(dve, chain, y, variance, eps, tmp):
    v, t = tmp[:, 0, :], tmp[:, 1, :]
    yi, ti = y.bitcast(I32), t.bitcast(I32)
    chain.add(dve.tensor_scalar(v, variance, eps, None, ALU.add)).wait()
    chain.add(dve.tensor_scalar(ti, v.bitcast(I32), 1, None, ALU.logical_shift_right)).wait()
    chain.add(dve.tensor_scalar(yi, ti, -1.0, float(0x5F3759DF), ALU.mult, ALU.add)).wait()


def root_step(dve, chain, y, tmp):
    v, t = tmp[:, 0, :], tmp[:, 1, :]
    chain.add(dve.tensor_tensor(t, y, y, ALU.mult)).wait()
    chain.add(dve.tensor_tensor(t, t, v, ALU.mult)).wait()
    chain.add(dve.tensor_scalar(t, t, -0.5, 1.5, ALU.mult, ALU.add)).wait()
    chain.add(dve.tensor_tensor(y, y, t, ALU.mult)).wait()


def inverse_root(dve, chain, y, variance, eps, tmp):
    root_guess(dve, chain, y, variance, eps, tmp)
    for _ in range(3):
        root_step(dve, chain, y, tmp)


class RowStatistics:

    def __init__(self, dve, chain, m, a, z):
        self.dve, self.chain, self.m, self.a, self.z = dve, chain, m, a, z
        self.tmp = m.root_tmp[:, :, a:z]

    def moments(self, a, z):
        for t in range(a, z):
            self.chain.add(self.dve.bn_stats(self.m.stats[:, t, :], self.m.x[:, t, :]))
        self.chain.wait()

    def aggregate(self):
        for t in range(self.a, self.z):
            self.chain.add(self.dve.bn_aggr(self.m.mean_var[:, t, :], self.m.stats[:, t, :]))
        self.chain.wait()

    def guess(self):
        root_guess(self.dve, self.chain, self.m.rstd[:, self.a:self.z], self.m.mean_var[:, self.a:self.z, 1], LN_EPS, self.tmp)

    def step(self):
        root_step(self.dve, self.chain, self.m.rstd[:, self.a:self.z], self.tmp)

    def turn_to_second(self):
        variance, rstd = self.m.mean_var[:, self.a:self.z, 1], self.m.rstd[:, self.a:self.z]
        for _ in range(2):
            self.chain.add(self.dve.tensor_tensor(variance, variance, rstd, ALU.mult)).wait()
        root_guess(self.dve, self.chain, self.m.rstd2[:, self.a:self.z], variance, LN_EPS, self.tmp)

    def second_step(self):
        root_step(self.dve, self.chain, self.m.rstd2[:, self.a:self.z], self.tmp)

    def finish(self):
        self.aggregate()
        self.guess()
        for _ in range(3):
            self.step()


LN_EPS = 1e-5
CHAINED_1 = 9
STACKING = 4 * 16
WARM_UP = 44
EARLY = 12


FILLS_BEFORE = ["xt", "q0", "k0", "v0", "q1", "k1", "v1", "wo", "q2", "k2", "v2", "ka", "q3", "k3", "kb"]
FILLS_ROUND = ["pv0", "v3", "xt", "at3", "pv1", "q0", "k0", "wo", "pv2", "v0", "at0", "pv3", "q1", "k1",
               "ka", "pv4", "v1", "at1", "pv5", "q2", "k2", "kb", "pv6", "v2", "at2", "pv7", "q3", "k3"]
FILLS_LAST = ["pv0", "v3", "at3", "pv1", "wo", "pv2", "at0", "pv3", "pv4", "at1", "pv5", "pv6", "at2", "pv7",
              "pv8", "at3'", "wo'"]
HALVED_BEFORE = ["xt", "q0", "k0", "q1", "k1", "q2", "k2", "ka", "q3", "k3", "kb"]
HALVED_ROUND = ["xt", "q0", "k0", "q1", "k1", "ka", "q2", "k2", "kb", "q3", "k3"]
FILLS_ABSENT_FIRST = 2


class Round:

    def __init__(self, pair, first=False, last=False):
        self.pair, self.first, self.last = pair, first, last

    def fill(self, name):
        start = len(FILLS_BEFORE) - FILLS_ABSENT_FIRST
        if isinstance(self.pair, int) and self.pair == -1:
            n = FILLS_BEFORE.index(name)
            return n % 2, n // 2
        if self.first:
            n = len(FILLS_BEFORE) + [f for f in FILLS_ROUND if f not in ("pv0", "at3")].index(name)
            return n % 2, n // 2
        n = start + (FILLS_LAST if self.last else FILLS_ROUND).index(name)
        return n % 2, self.pair * (len(FILLS_ROUND) // 2) + n // 2

    def halved(self, name):
        if isinstance(self.pair, int) and self.pair == -1:
            return HALVED_BEFORE.index(name) + 1
        return self.pair * len(HALVED_ROUND) + (len(HALVED_BEFORE) + HALVED_ROUND.index(name) + 1)

    def before(self):
        return Round(self.pair - 1)


def transformer(nc, T, out):
    x_in, ctx_in = T["x"], T["ctx_1024"]
    B, S, D = x_in.shape
    HD = T["L0_xattn_wq_w"].shape[1]
    MEM = T["L0_xattn_mk"].shape[1]
    H0, DK = 16, HD // 16
    MT = HD // P
    PAIRS = B // 2
    H1, DH = 16, D // 16
    G1 = H1 // 4
    VW, VW1 = DK + 1, DH + 1
    F0 = T["L0_ffn_fc1_q"].shape[1]
    SC0, SC1 = DK ** -0.5, DH ** -0.5
    assert S == P and D == P and MEM == P and MT == 8 and PAIRS == 8 and DK == 64

    with ExitStack() as lasting, ExitStack() as ctx:
        def sb(name, shape, dt=F32):
            return ctx.enter_context(nc.sbuf_tensor(name, shape, dt))

        def keep(name, shape, dt=F32):
            return lasting.enter_context(nc.sbuf_tensor(name, shape, dt))

        def sem(name):
            return ctx.enter_context(nc.semaphore(name))

        x = keep("x", [P, B, D])
        ident = keep("ident", [P, P])
        stats = keep("stats", [P, B, 6])
        mean_var = keep("mean_var", [P, B, 2])
        rstd = keep("rstd", [P, B])
        rstd2 = keep("rstd2", [P, B])
        root_tmp = keep("root_tmp", [P, 2, B])
        m = Shared()
        m.x, m.stats, m.mean_var, m.rstd, m.rstd2, m.root_tmp = x, stats, mean_var, rstd, rstd2, root_tmp
        R_QE, R_KE, R_MQ, R_MK = 0, 32, 64, 96
        R_BQ = R_QE + G1
        R_BK = R_BQ + MT
        R_F1 = R_BK + MT
        R_GA = R_F1 + F0 // P
        R_BE = R_GA + 1
        assert R_BE < R_KE
        cols = keep("cols", [P, P])
        mcols = keep("mcols", [P, 2 * G1])
        w1f = keep("w1f", [P, 2, F0], F32R)
        w2f = keep("w2f", [P, F0 // P, D])
        b2_bc = keep("b2_bc", [P, D])
        wqe = keep("wqe", [P, 2, G1 * P], F32R)
        k1T = keep("k1T", [P, G1, B * S], F32R)
        v1 = keep("v1", [P, B, H1, VW1])
        wo1 = keep("wo1", [P, D])
        bo1_bc = keep("bo1_bc", [P, D])

        wq = sb("wq", [P, 2, HD], F32R)
        wk = sb("wk", [P, 2, HD], F32R)
        wv = sb("wv", [P, 2, HD], F32R)
        wo = sb("wo", [P, MT, D])
        bv_bc = sb("bv_bc", [P, HD])
        bo_bc = sb("bo_bc", [P, D])
        rows1 = sb("rows1", [R_KE + G1, D // G1])
        wke = sb("wke", [P, 2, G1 * P], F32R)
        wv1 = sb("wv1", [P, 2, D], F32R)
        bv1_bc = sb("bv1_bc", [P, D])
        assert 2 * F0 == HD and F0 == 512 and G1 == 4
        fq = k1T[:, 3, 4 * 2 * S:4 * 2 * S + HD].bitcast(I32).rearrange("p (w n) -> p w n", w=2)
        w_ffn = fq.bitcast(F32)
        fs = [k1T[:, w, 5 * 2 * S:5 * 2 * S + F0].bitcast(F32) for w in range(2)]
        xs = sb("xs", [P, 2, D])
        cs = sb("cs", [P, 2, D])
        xt = sb("xt", [P, 2, 4, P], F32R)
        q_stack = sb("q_stack", [P, MT, 2, 2 * S], F32R)
        k_stack = sb("k_stack", [P, MT, 2, 3, S], F32R)
        q_hi, q_lo, k_hi = sb("q_hi", [P, 2, 2 * S], F32R), sb("q_lo", [P, 2, 2 * S], F32R), sb("k_hi", [P, 2, 2 * S], F32R)
        k_lo = sb("k_lo", [P, MT, 3, S], F32R)
        OWN = [slice(0, DK), slice(DK, 2 * DK)]
        v = sb("v", [P, 2, H0, VW])
        mv = sb("mv", [P, H0, VW])
        nmx = sb("nmx", [P, 2, 4])
        probs = sb("probs", [P, 4096])
        w_raw = probs[:, 4096 - 3 * HD:4096].rearrange("p (w n) -> p w n", w=3)
        pr = probs[:, 0:2048].rearrange("p (u r i k) -> p u r i k", u=2, r=2, i=2)
        pT = probs[:, 2048:4096].rearrange("p (u r t s) -> p u r t s", u=2, r=2, t=4)
        rows = probs[:, 0:P]
        rec = sb("rec", [P, 2, 4])
        at = sb("at", [P, 2, 2, 256])
        attended = sb("attended", [P, 2048])
        aT = attended[:].rearrange("p (m b t s) -> p m b t s", m=4, b=2, t=2)
        mk_raw = attended[:, 0:HD]
        w1_raw = attended[:, HD:HD + 3 * D]
        k1h = sb("k1h", [P, 2, 256], F32R)

        psS = ctx.enter_context(nc.psum_tensor("psS", [P, 2, 2, 512], F32))
        psT = ctx.enter_context(nc.psum_tensor("psT", [P, 2, 512], F32))
        psM = ctx.enter_context(nc.psum_tensor("psM", [P, 2, 512], F32))

        x_loaded, c_loaded = [sem("x_loaded0"), sem("x_loaded1")], sem("c_loaded")
        wqkv_loaded = [sem(f"w{n}_loaded") for n in "qkv"]
        rows_loaded, consts_loaded, mk_loaded, w1_loaded = sem("rows_loaded"), sem("consts_loaded"), sem("mk_loaded"), sem("w1_loaded")
        consts_set, table_blank = sem("consts_set"), sem("table_blank")
        ffn_loaded, later_loaded, ffn_set = sem("ffn_loaded"), sem("later_loaded"), sem("ffn_set")
        rows_ready, cols_full, cols_ready = sem("rows_ready"), sem("cols_full"), sem("cols_ready")
        mk_full, mk_hi, mk_ready, mk_stacked = sem("mk_full"), sem("mk_hi"), sem("mk_ready"), sem("mk_stacked")
        stacked = {name: [sem(f"{name}_stacked{mm}") for mm in range(4)] for name in "qk"}
        w_hi, w_ready = sem("w_hi"), sem("w_ready")
        w1_ready = sem("w1_ready")
        xs_ready = sem("xs_ready")
        misc_full = [sem("misc_full0"), sem("misc_full1")]
        misc_done = [sem("misc_done0"), sem("misc_done1")]
        hi_ready = sem("hi_ready")
        scores_full, max_ready, probs_ready = sem("scores_full"), sem("max_ready"), sem("probs_ready")
        pT_full = sem("pT_full")
        pT_ready = [sem("pT_ready0"), sem("pT_ready1")]
        dve_chain, act_chain, pool_chain = sem("dve_chain"), sem("act_chain"), sem("pool_chain")

        N_ROWS_DMA, N_CONST_DMA = 7, 6
        blocks = ExitStack()
        block = blocks.enter_context(nc.Block())

        def row(ap):
            return ap.rearrange("(a d) -> a d", a=1)

        rounds = [Round(0, first=True), Round(None), Round(PAIRS - 1, last=True)]

        @block.sync
        def _(sp):
            def load_x(c):
                sp.dma_start(x[:, 4 * c:4 * c + 4, :], x_in[4 * c:4 * c + 4].rearrange("b s d -> s b d")).then_inc(x_loaded[c > 0], 16)

            load_x(0)
            sp.dma_start(w_raw[:, 0, :], T["L0_xattn_wq_w"]).then_inc(wqkv_loaded[0], 16)
            sp.dma_start(cs[:], ctx_in[0:2].rearrange("b s d -> s b d")).then_inc(c_loaded, 16)
            sp.wait_ge(table_blank, 1)
            for r0, name, n in ((R_BQ, "L0_xattn_wq_b", MT), (R_BK, "L0_xattn_wk_b", MT), (R_F1, "L0_ffn_fc1_bias", F0 // P),
                                (R_GA, "L0_ffn_ln_gamma", 1), (R_BE, "L0_ffn_ln_beta", 1)):
                sp.dma_start(rows[r0:r0 + n, :], T[name].rearrange("(r p) -> r p", p=P)).then_inc(rows_loaded, 16)
            for r0, name in ((R_QE, "L1_xattn_bq"), (R_KE, "L1_xattn_bkv")):
                sp.dma_start(rows1[r0:r0 + G1, :], T[name][0:D].rearrange("(r p) -> r p", r=G1)).then_inc(rows_loaded, 16)
            sp.dma_start(w_raw[:, 2, :], T["L0_xattn_wv_w"]).then_inc(wqkv_loaded[2], 16)
            for c in range(1, 4):
                load_x(c)

            def next_context(r):
                bank, n = r.fill("xt")
                sp.wait_ge(misc_full[bank], n + 1)
                sp.dma_start(cs[:], ctx_in[bass.ds((r.pair + 2) * 2, 2)].rearrange("b s d -> s b d")).then_inc(c_loaded, 16)

            def move_rows(dst, src, swapped, semaphore):
                for h in range(2):
                    sp.dma_start(dst(OWN[1 - h] if swapped else OWN[h], h).bitcast(F32), src(OWN[h], h).bitcast(F32)).then_inc(semaphore, 16)

            def stack(r, first=False):
                for mm in range(4):
                    if first and mm == 2:
                        sp.wait_ge(mk_ready, 1)
                        move_rows(lambda rows, h: k_stack[rows, :, h, 2, :], lambda rows, h: k_stack[rows, :, h, 2, :], True, mk_stacked)
                    two = slice(2 * mm, 2 * mm + 2)
                    bank, n = r.fill(f"q{mm}")
                    sp.wait_ge(misc_done[bank], n + 1)
                    move_rows(lambda rows, h: q_stack[rows, two, h, :], lambda rows, h: q_hi[rows, :, :], False, stacked["q"][mm])
                    move_rows(lambda rows, h: q_stack[rows, two, h, :], lambda rows, h: q_lo[rows, :, :], True, stacked["q"][mm])
                    bank, n = r.fill(f"k{mm}")
                    sp.wait_ge(misc_done[bank], n + 1)
                    for swapped in (False, True):
                        move_rows(lambda rows, h: k_stack[rows, two, h, 0:2, :],
                                  lambda rows, h: k_hi[rows, :, :].rearrange("p m (b s) -> p m b s", b=2), swapped, stacked["k"][mm])

            next_context(Round(-1))
            stack(Round(-1), first=True)
            sp.dma_start(fq[:, 0, :], T["L0_ffn_fc1_q"]).then_inc(ffn_loaded, 16)
            sp.dma_start(fq[:, 1, :].rearrange("p (t d) -> p t d", d=D),
                         T["L0_ffn_fc2_q"].rearrange("(t p) d -> p t d", p=P)).then_inc(ffn_loaded, 16)
            sp.dma_start(fs[0], T["L0_ffn_fc1_scales"].partition_broadcast(P)).then_inc(ffn_loaded, 16)
            sp.dma_start(fs[1], row(T["L0_ffn_fc2_scales"].rearrange("g d -> (g d)")).partition_broadcast(P)).then_inc(ffn_loaded, 16)
            next_context(rounds[0])
            stack(rounds[0])
            with sp.Fori(1, PAIRS - 2) as pair:
                next_context(Round(pair))
                stack(Round(pair))
            stack(Round(PAIRS - 2))

        @block.gpsimd
        def _(pool):
            chain = Chain(pool, pool_chain)
            chain.add(pool.memset(ident[:], 0.0))
            pool.memset(rows[:], 0.0).then_inc(table_blank, 1)
            pool.memset(v[:, :, :, DK:VW], 1.0).then_inc(consts_set, 1)
            pool.memset(mv[:, :, DK:VW], 1.0).then_inc(consts_set, 1)
            pool.memset(v1[:, :, :, DH:VW1], 1.0).then_inc(consts_set, 1)
            chain.wait()
            pool.affine_select(out=ident[:], in_=ident[:], compare_op=ALU.not_equal, fill=1.0, base=0,
                               pattern=[[-1, P]], channel_multiplier=1).then_inc(consts_set, 1)
            pool.wait_ge(table_blank, 1)
            for n, (r0, rep) in enumerate(((R_MQ, 2), (R_MK, 1))):
                pool.wait_ge(consts_set, 4 + n)
                parts = rows[r0:r0 + 1, :].rearrange("a (j r d) -> a j r d", j=4, r=4)
                pool.memset(parts[:, :, rep, :], 1.0).then_inc(consts_set, 1)
            pool.wait_ge(wqkv_loaded[1], 16)
            pool.dma_start(bv_bc[:], row(T["L0_xattn_wv_b"]).partition_broadcast(P)).then_inc(consts_loaded, 16)
            pool.dma_start(bv1_bc[:], row(T["L1_xattn_bkv"])[:, D:2 * D].partition_broadcast(P)).then_inc(consts_loaded, 16)
            pool.dma_start(mv[:, :, 0:DK], T["L0_xattn_mv"][0].rearrange("t (h d) -> t h d", d=DK)).then_inc(consts_loaded, 16)
            pool.dma_start(bo_bc[:], row(T["L0_xattn_wo_b"]).partition_broadcast(P)).then_inc(consts_loaded, 16)
            pool.dma_start(wo[:], T["L0_xattn_wo_w"].rearrange("(t p) n -> p t n", p=P)).then_inc(consts_loaded, 16)
            pool.dma_start(bo1_bc[:], row(T["L1_xattn_bo"]).partition_broadcast(P)).then_inc(consts_loaded, 16)
            pool.dma_start(b2_bc[:], row(T["L0_ffn_fc2_bias"]).partition_broadcast(P)).then_inc(later_loaded, 16)
            pool.dma_start(wo1[:], T["L1_xattn_Wo"]).then_inc(later_loaded, 16)

            pool.wait_ge(later_loaded, 16 * 2)
            pool.wait_ge(ffn_loaded, 16 * 4)
            for i in range(2):
                chain.add(pool.tensor_copy(w_ffn[:, i, :], fq[:, i, :]))
            chain.wait()
            for i in range(2):
                chain.add(pool.tensor_scalar(w_ffn[:, i, :], w_ffn[:, i, :], -128.0, None, ALU.add))
            chain.wait()
            chain.add(pool.tensor_tensor(w_ffn[:, 0, :], w_ffn[:, 0, :], fs[0], ALU.mult))
            pool.tensor_tensor(w2f[:, :, :].rearrange("p t d -> p (t d)"), w_ffn[:, 1, :], fs[1], ALU.mult)
            chain.wait()
            chain.add(pool.tensor_copy(w1f[:, 0, :], w_ffn[:, 0, :])).wait()
            pool.tensor_tensor(w1f[:, 1, :], w_ffn[:, 0, :], w1f[:, 0, :].bitcast(F32), ALU.subtract).then_inc(ffn_set, 1)

        N_CONSTS = 6

        @block.scalar
        def _(act):
            act.dma_start(w_raw[:, 1, :], T["L0_xattn_wk_w"]).then_inc(wqkv_loaded[1], 16)
            act.dma_start(mk_raw[:], T["L0_xattn_mk"][0]).then_inc(mk_loaded, 16)
            act.dma_start(w1_raw[:, 0:D], T["L1_xattn_Wq"]).then_inc(w1_loaded, 16)
            act.dma_start(w1_raw[:, D:3 * D], T["L1_xattn_Wkv"]).then_inc(w1_loaded, 16)
            def hi_of_weights(n):
                w, scale = ((wq, SC0), (wk, 1.0), (wv, 1.0))[n]
                act.wait_ge(wqkv_loaded[n], 16)
                act.activation(w[:, 0, :], w_raw[:, n, :], ACT.Copy, scale=scale).then_inc(w_hi, 1)

            hi_of_weights(0)
            hi_of_weights(1)

            def moved(r, q_or_k, mm):
                if mm:
                    act.wait_ge(stacked[q_or_k][mm - 1], r.pair * STACKING + 2 * STACKING)
                else:
                    at_least(act, stacked[q_or_k][3], r.pair * STACKING + STACKING)

            def hi_of_fill(r, name):
                bank, n = r.fill(name)
                act.wait_ge(misc_full[bank], n + 1)
                ps = psM[:, bank, :]
                if name == "xt":
                    last = act.activation(xt[:, 0, :, :], ps.rearrange("p (t s) -> p t s", t=4), ACT.Copy)
                elif name[0] == "q":
                    mm = int(name[1])
                    moved(r, name[0], mm)
                    for i in range(2):
                        m = 2 * mm + i
                        last = act.activation(q_hi[:, i, :], ps[:, 256 * i:256 * i + 256], ACT.Identity,
                                              bias=cols[:, R_BQ + m:R_BQ + m + 1])
                elif name in ("ka", "kb"):
                    if name == "kb" or not (isinstance(r.pair, int) and r.pair == -1):
                        used, count = r.fill("ka") if name == "kb" else r.before().fill("kb")
                        act.wait_ge(misc_done[used], count + 1)
                    for i in range(2):
                        t = 2 * (name == "kb") + i
                        last = act.activation(k1h[:, i, :], ps[:, 256 * i:256 * i + 256], ACT.Identity,
                                              scale=cols[:, R_MK:R_MK + 1], bias=mcols[:, G1 + t:G1 + t + 1])
                else:
                    moved(r, name[0], int(name[1]))
                    for i in range(2):
                        m = 2 * int(name[1]) + i
                        last = act.activation(k_hi[:, i, :], ps[:, 256 * i:256 * i + 256], ACT.Identity,
                                              bias=cols[:, R_BK + m:R_BK + m + 1])
                last.then_inc(hi_ready, 1)

            def exps(quad, unit):
                act.wait_ge(max_ready, quad + 1)
                at_least(act, pT_full, quad * 2 - 2)
                for r in range(2):
                    for i in range(2):
                        last = act.activation(pr[:, unit, r, i, :], psS[:, unit, r, 256 * i:256 * i + 256], ACT.Exp,
                                              bias=nmx[:, unit, 2 * r + i:2 * r + i + 1])
                last.then_inc(probs_ready, 1)

            def copy_pT(r, g, quad):
                act.wait_ge(pT_full, quad * 2 + 2)
                if not (r.first and g < 2):
                    bank, n = r.fill(f"pv{g - 1}") if g >= 1 else r.before().fill("pv7")
                    act.wait_ge(misc_full[bank], n + 1)
                act.copy(pT[:, g % 2, 1, :, :], psT[:, 1, :].rearrange("p (t s) -> p t s", t=4)).then_inc(pT_ready[1], 1)

            def copy_aT(r, name, mm):
                bank, n = r.fill(name)
                act.wait_ge(misc_full[bank], n + 1)
                act.copy(aT[:, mm, :, :, :], psM[:, bank, :].rearrange("p (b t s) -> p b t s", b=2, t=2)).then_inc(misc_done[bank], 1)

            for name in HALVED_BEFORE:
                if name == "q0":
                    hi_of_weights(2)
                    act.wait_ge(cols_ready, 1)
                if name == "q1":
                    act.wait_ge(mk_full, 1)
                    for i in range(2):
                        for h, own in enumerate(OWN):
                            last = act.activation(k_stack[own, 4 * i:4 * i + 4, h, 2, :],
                                                  psS[own, 1, i, :].rearrange("p (t s) -> p t s", t=4), ACT.Copy)
                    last.then_inc(mk_hi, 1)
                hi_of_fill(Round(-1), name)
            exps(0, 0)

            def attention_round(r):
                for g in range(8):
                    quad = r.pair * 8 + g
                    if g == 1 and not r.first:
                        copy_aT(r, "at3", 3)
                    if g in (3, 5, 7):
                        copy_aT(r, f"at{g // 2 - 1}", g // 2 - 1)
                    if g in (4, 6) and not r.last:
                        hi_of_fill(r, "ka" if g == 4 else "kb")
                    if not (r.last and g == 7):
                        exps(quad + 1, (g + 1) % 2)
                    copy_pT(r, g, quad)
                    if not r.last:
                        if g == 0:
                            hi_of_fill(r, "xt")
                        if g % 2:
                            hi_of_fill(r, f"q{g // 2}")
                            hi_of_fill(r, f"k{g // 2}")

            attention_round(rounds[0])
            with act.Fori(1, PAIRS - 1) as pair:
                attention_round(Round(pair))
            attention_round(rounds[2])
            copy_aT(rounds[2], "at3'", 3)

        @block.tensor
        def _(pe):
            pe.wait_ge(consts_set, N_CONSTS)
            for _ in range(WARM_UP):
                pe.transpose(psT[:, 1, 0:P], ident[:], ident[:])
            pe.wait_ge(rows_ready, 1)
            pe.transpose(psT[:, 0, 0:P], rows[:], ident[:]).then_inc(cols_full, 1)

            def opened(r, name):
                bank, n = r.fill(name)
                at_least(pe, misc_done[bank], n)
                return bank

            def evacuated(r, name):
                bank, n = r.fill(name)
                pe.wait_ge(misc_done[bank], n + 1)

            def product(dst, left, right):
                (lh, ll), (rh, rl) = left, right
                pe.matmul(dst, lh, rh, start=True, stop=False)
                pe.matmul(dst, lh, rl, start=False, stop=False)
                return pe.matmul(dst, ll, rh, start=False, stop=True)

            def halves(t, *index):
                return t[(slice(None), 0) + index], t[(slice(None), 1) + index]

            ALL = slice(None)

            def transpose_inputs(r, n):
                bank = opened(r, "xt")
                pe.wait_ge(xs_ready, n)
                pe.wait_ge(c_loaded, n * 16)
                for t in range(4):
                    last = pe.transpose(psM[:, bank, t * P:(t + 1) * P], (xs if t < 2 else cs)[:, t % 2, :], ident[:])
                last.then_inc(misc_full[bank], 1)

            def project_q_or_k(r, name):
                bank = opened(r, name)
                w, src = (wq, slice(0, 2)) if name[0] == "q" else (wk, slice(2, 4))
                for i in range(2):
                    m = 2 * int(name[1]) + i
                    last = product(psM[:, bank, 256 * i:256 * i + 256], halves(w, slice(m * P, (m + 1) * P)),
                                   halves(xt, src, ALL))
                last.then_inc(misc_full[bank], 1)

            def project_k1(r, name):
                bank = opened(r, name)
                for i in range(2):
                    t = 2 * (name == "kb") + i
                    last = product(psM[:, bank, 256 * i:256 * i + 256], halves(wke, slice(t * P, (t + 1) * P)),
                                   halves(xt, slice(2, 4), ALL))
                last.then_inc(misc_full[bank], 1)

            def project_v(r, mm):
                bank = opened(r, f"v{mm}")
                for b in range(2):
                    last = product(psM[:, bank, 256 * b:256 * b + 256], halves(xt, 2 + b, ALL),
                                   halves(wv, slice(256 * mm, 256 * mm + 256)))
                last.then_inc(misc_full[bank], 1)

            def project_out_and_v1(r, name, out_part, v1_part):
                bank = opened(r, name)
                if out_part:
                    for b in range(2):
                        for t in range(MT):
                            last = pe.matmul(psM[:, bank, b * P:(b + 1) * P], aT[:, t // 2, b, t % 2, :], wo[:, t, :],
                                             start=t == 0, stop=t == MT - 1)
                if v1_part:
                    for b in range(2):
                        last = product(psM[:, bank, 256 + b * P:256 + (b + 1) * P], halves(xt, 2 + b, ALL), halves(wv1, ALL))
                last.then_inc(misc_full[bank], 1)

            def scores(unit, mm, b, quad):
                at_least(pe, probs_ready, quad - 1)
                for i in range(2):
                    for r in range(2):
                        m, dst, queries = 2 * mm + i, psS[:, unit, r, 256 * i:256 * i + 256], slice(b * S, (b + 1) * S)
                        keys = slice(0, 3, 2) if b == 0 else slice(1, 3)
                        pe.matmul(dst, q_stack[:, m, r, queries], k_stack[:, m, r, keys, :], start=True, stop=False)
                        last = pe.matmul(dst, q_stack[OWN[r], m, r, queries], k_lo[OWN[r], m, keys, :], start=False, stop=True)
                last.then_inc(scores_full, 1)

            def transpose_probs(unit, quad):
                pe.wait_ge(probs_ready, quad + 1)
                for r in range(2):
                    at_least(pe, pT_ready[r], quad)
                    for i in range(2):
                        for kt in range(2):
                            c = 2 * i + kt
                            last = pe.transpose(psT[:, r, c * P:(c + 1) * P], pr[:, unit, r, i, kt * P:(kt + 1) * P], ident[:])
                    last.then_inc(pT_full, 1)

            def attend(r, g, quad):
                local = (g - 1) % 8
                unit, mm, b = local % 2, local // 2, local % 2
                bank = opened(r, f"pv{g}")
                for i in range(2):
                    pe.wait_ge(pT_ready[i], quad)
                for h in range(4):
                    i, part, head = h // 2, h % 2, 4 * mm + h
                    pe.matmul(psM[:, bank, h * VW:(h + 1) * VW], pT[:, unit, part, 2 * i, :], v[:, b, head, :], start=True, stop=False)
                    last = pe.matmul(psM[:, bank, h * VW:(h + 1) * VW], pT[:, unit, part, 2 * i + 1, :], mv[:, head, :],
                                     start=False, stop=True)
                last.then_inc(misc_full[bank], 1)

            def transpose_attended(r, name, mm):
                bank = opened(r, name)
                if name == "at3":
                    evacuated(r, "pv0")
                elif name == "at3'":
                    evacuated(r, "pv8")
                else:
                    evacuated(r, f"pv{2 * mm + 2}")
                for b in range(2):
                    for t in range(2):
                        c = 2 * b + t
                        last = pe.transpose(psM[:, bank, c * P:(c + 1) * P], at[:, mm % 2, b, t * P:(t + 1) * P], ident[:])
                last.then_inc(misc_full[bank], 1)

            before = Round(-1)
            transpose_inputs(before, 1)
            evacuated(before, "xt")
            pe.wait_ge(w_ready, 2)
            for mm in range(4):
                project_q_or_k(before, f"q{mm}")
                project_q_or_k(before, f"k{mm}")
                if mm < 3:
                    pe.wait_ge(w_ready, 3)
                    project_v(before, mm)
                if mm == 0:
                    pe.wait_ge(mk_loaded, 16)
                    for m in range(MT):
                        last = pe.transpose(psS[:, 1, m // 4, (m % 4) * P:(m % 4 + 1) * P], mk_raw[:, m * P:(m + 1) * P], ident[:])
                    last.then_inc(mk_full, 1)
                elif mm == 1:
                    pe.wait_ge(w1_ready, 1)
                    project_out_and_v1(before, "wo", False, True)
                else:
                    project_k1(before, "ka" if mm == 2 else "kb")
            pe.wait_ge(mk_ready, 1)
            pe.wait_ge(mk_stacked, 32)
            for name in "qk":
                pe.wait_ge(stacked[name][0], STACKING)
            scores(0, 0, 0, 0)
            pe.wait_ge(consts_loaded, 16 * N_CONST_DMA)

            def attention_round(r):
                prior = before if r.first else r.before()
                for g in range(8):
                    quad = r.pair * 8 + g
                    mm = g // 2
                    if not (r.last and g == 7):
                        nxt = (g + 1) % 8
                        if nxt % 2 == 0:
                            for name in "qk":
                                pe.wait_ge(stacked[name][nxt // 2], r.pair * STACKING + (2 * STACKING if g == 7 else STACKING))
                        scores(nxt % 2, nxt // 2, nxt % 2, quad + 1)
                    if g == 1 and not r.first:
                        transpose_attended(r, "at3", 3)
                    if g == 2:
                        if not r.first:
                            evacuated(r, "at3")
                        project_out_and_v1(r, "wo", not r.first, not r.last)
                    if g in (3, 5, 7):
                        transpose_attended(r, f"at{mm - 1}", mm - 1)
                    if g in (4, 6) and not r.last:
                        project_k1(r, "ka" if g == 4 else "kb")
                    transpose_probs(g % 2, quad)
                    if not (r.first and g == 0):
                        if g % 2:
                            if g == 7:
                                evacuated(r, "v3")
                            else:
                                evacuated(prior, f"v{mm}")
                        attend(r, g, quad)
                    if g == 0:
                        project_v(r, 3)
                        if not r.last:
                            transpose_inputs(r, r.pair + 2)
                    if not r.last and g % 2:
                        if g == 1:
                            evacuated(r, "xt")
                        project_q_or_k(r, f"q{mm}")
                        project_q_or_k(r, f"k{mm}")
                    if not r.last and g in (2, 4, 6):
                        project_v(r, mm - 1)

            attention_round(rounds[0])
            with pe.Fori(1, PAIRS - 1) as pair:
                attention_round(Round(pair))
            last_round = rounds[2]
            attention_round(last_round)
            attend(last_round, 8, 8 * PAIRS)
            transpose_attended(last_round, "at3'", 3)
            evacuated(last_round, "at3'")
            project_out_and_v1(last_round, "wo'", True, False)

        @block.vector
        def _(dve):
            chain = Chain(dve, dve_chain)

            def normalise(pair):
                for i in range(2):
                    t = pair * 2 + i
                    if isinstance(t, int):
                        mean, scale, src = mean_var[:, t, 0:1], rstd[:, t:t + 1], x[:, t, :]
                    else:
                        mean, scale, src = mean_var[:, bass.ds(t, 1), 0], rstd[:, bass.ds(t, 1)], x[:, bass.ds(t, 1), :].rearrange("p a d -> p (a d)")
                    last = dve.tensor_scalar(xs[:, i, :], src, mean, scale, ALU.subtract, ALU.mult)
                last.then_inc(xs_ready, 1)

            dve.wait_ge(x_loaded[0], 16)
            first = RowStatistics(dve, chain, m, 0, 4)
            first.moments(0, 4)
            first.finish()
            normalise(0)
            def lo_of_weights(n):
                w, scale = ((wq, SC0), (wk, 1.0), (wv, 1.0))[n]
                dve.wait_ge(w_hi, n + 1)
                dve.scalar_tensor_tensor(w[:, 1, :], w_raw[:, n, :], scale, w[:, 0, :].bitcast(F32), ALU.mult, ALU.subtract)\
                    .then_inc(w_ready, 1)

            lo_of_weights(0)
            lo_of_weights(1)
            dve.wait_ge(rows_loaded, 16 * N_ROWS_DMA)
            for r0, scale in ((R_QE, SC1), (R_KE, 1.0)):
                last = dve.tensor_scalar(rows[r0:r0 + G1, :].rearrange("a (h r d) -> a h r d", r=4, d=DH),
                                         rows1[r0:r0 + G1, :].rearrange("a (h r d) -> a h r d", r=1, d=DH).to_broadcast([G1, H1 // G1, 4, DH]),
                                         scale, None, ALU.mult)
            last.then_inc(rows_ready, 1)
            dve.wait_ge(cols_full, 1)
            chain.add(dve.tensor_copy(cols[:], psT[:, 0, 0:P]))
            chain.wait()
            dve.tensor_scalar(cols[:, R_BQ:R_BQ + MT], cols[:, R_BQ:R_BQ + MT], SC0, None, ALU.mult)
            dve.tensor_scalar(mcols[:, 0:G1], cols[:, R_QE:R_QE + G1], cols[:, R_MQ:R_MQ + 1], None, ALU.mult)
            dve.tensor_scalar(mcols[:, G1:2 * G1], cols[:, R_KE:R_KE + G1], cols[:, R_MK:R_MK + 1], None, ALU.mult)\
                .then_inc(cols_ready, 1)

            def lo_of_fill(r, name, pair=None):
                bank, n = r.fill(name)
                dve.wait_ge(misc_full[bank], n + 1)
                dve.wait_ge(hi_ready, r.halved(name))
                ps = psM[:, bank, :]
                if name == "xt":
                    last = dve.tensor_tensor(xt[:, 1, :, :], ps.rearrange("p (t s) -> p t s", t=4), xt[:, 0, :, :].bitcast(F32), ALU.subtract)
                elif name[0] == "q":
                    for i in range(2):
                        m = 2 * int(name[1]) + i
                        last = dve.scalar_tensor_tensor(q_lo[:, i, :], ps[:, 256 * i:256 * i + 256], cols[:, R_BQ + m:R_BQ + m + 1],
                                                        q_hi[:, i, :].bitcast(F32), ALU.add, ALU.subtract)
                elif name in ("ka", "kb"):
                    for i in range(2):
                        t = 2 * (name == "kb") + i
                        to = (pair + 1) * 256
                        dst = k1T[:, t, to:to + 256] if isinstance(to, int) else k1T[:, t, bass.ds(to, 256)]
                        last = dve.scalar_tensor_tensor(dst, ps[:, 256 * i:256 * i + 256], cols[:, R_KE + t:R_KE + t + 1],
                                                        k1h[:, i, :].bitcast(F32), ALU.add, ALU.subtract)
                else:
                    for i in range(2):
                        m = 2 * int(name[1]) + i
                        last = dve.scalar_tensor_tensor(k_lo[:, m, 0:2, :].rearrange("p b s -> p (b s)"), ps[:, 256 * i:256 * i + 256],
                                                        cols[:, R_BK + m:R_BK + m + 1], k_hi[:, i, :].bitcast(F32), ALU.add, ALU.subtract)
                last.then_inc(misc_done[bank], 1)

            def keep_v(r, mm):
                bank, n = r.fill(f"v{mm}")
                dve.wait_ge(misc_full[bank], n + 1)
                dve.tensor_tensor(v[:, :, 4 * mm:4 * mm + 4, 0:DK], psM[:, bank, :].rearrange("p (b h d) -> p b h d", b=2, h=4),
                                  bv_bc[:, 256 * mm:256 * mm + 256].rearrange("p (b h d) -> p b h d", b=1, h=4).to_broadcast([P, 2, 4, DK]),
                                  ALU.add).then_inc(misc_done[bank], 1)

            def residual_and_v1(r, name, out_part, v1_part, pair):
                bank, n = r.fill(name)
                dve.wait_ge(misc_full[bank], n + 1)
                if out_part:
                    t = pair * 2 - 2
                    dst = x[:, t:t + 2, :] if isinstance(t, int) else x[:, bass.ds(t, 2), :]
                    last = dve.tensor_tensor(dst, dst, psM[:, bank, 0:256].rearrange("p (b d) -> p b d", b=2), ALU.add)
                    if v1_part:
                        chain.add(last)
                        chain.wait()
                    else:
                        last.then_inc(dve_chain, 1)
                        chain.count += 1
                        chain.wait()
                    last = dve.tensor_tensor(dst, dst, bo_bc[:].rearrange("p (b d) -> p b d", b=1).to_broadcast([P, 2, D]), ALU.add)
                if v1_part:
                    t = pair * 2 + 2
                    dst = v1[:, t:t + 2, :, 0:DH] if isinstance(t, int) else v1[:, bass.ds(t, 2), :, 0:DH]
                    last = dve.tensor_tensor(dst, psM[:, bank, 256:512].rearrange("p (b h d) -> p b h d", b=2, h=H1),
                                             bv1_bc[:].rearrange("p (b h d) -> p b h d", b=1, h=H1).to_broadcast([P, 2, H1, DH]), ALU.add)
                last.then_inc(misc_done[bank], 1)

            def row_max(quad, unit):
                dve.wait_ge(scores_full, quad + 1)
                dve.tensor_reduce(nmx[:, unit, :], psS[:, unit, :, :].rearrange("p r (i k) -> p (r i) k", i=2), AX_X, ALU.max,
                                  negate=True).then_inc(max_ready, 1)

            def copy_pT(quad, unit):
                dve.wait_ge(pT_full, quad * 2 + 1)
                dve.tensor_copy(pT[:, unit, 0, :, :], psT[:, 0, :].rearrange("p (t s) -> p t s", t=4)).then_inc(pT_ready[0], 1)

            def normalise_attended(r, g):
                local = (g - 1) % 8
                mm, b = local // 2, local % 2
                bank, n = r.fill(f"pv{g}")
                dve.wait_ge(misc_full[bank], n + 1)
                o = psM[:, bank, 0:4 * VW].rearrange("p (h d) -> p h d", h=4)
                chain.add(dve.reciprocal(rec[:, b, :], o[:, :, DK])).wait()
                dve.tensor_tensor(at[:, mm % 2, b, :].rearrange("p (h d) -> p h d", h=4), o[:, :, 0:DK],
                                  rec[:, b, :].rearrange("p (h d) -> p h d", d=1).to_broadcast([P, 4, DK]), ALU.mult).then_inc(misc_done[bank], 1)

            before = Round(-1)
            lo_of_fill(before, "xt")
            normalise(1)
            lo_of_weights(2)
            for mm in range(4):
                lo_of_fill(before, f"q{mm}")
                lo_of_fill(before, f"k{mm}")
                if mm < 3:
                    dve.wait_ge(consts_loaded, 16 * N_CONST_DMA)
                    keep_v(before, mm)
                if mm == 0:
                    dve.wait_ge(w1_loaded, 32)
                    for w, c0, scale in ((wqe, 0, SC1), (wke, D, 1.0)):
                        dst = w[:, :, :].rearrange("p a (h r d) -> p a h r d", h=H1, r=4)
                        src = w1_raw[:, c0:c0 + D].rearrange("p (h r d) -> p h r d", h=H1, r=1).to_broadcast([P, H1, 4, DH])
                        chain.add(dve.tensor_scalar(dst[:, 0], src, scale, None, ALU.mult)).wait()
                        for rep in range(4):
                            dve.scalar_tensor_tensor(dst[:, 1, :, rep, :], src[:, :, rep, :], scale, dst[:, 0, :, rep, :].bitcast(F32),
                                                     ALU.mult, ALU.subtract)
                    chain.add(dve.tensor_copy(wv1[:, 0, :], w1_raw[:, 2 * D:3 * D])).wait()
                    dve.tensor_tensor(wv1[:, 1, :], w1_raw[:, 2 * D:3 * D], wv1[:, 0, :].bitcast(F32), ALU.subtract).then_inc(w1_ready, 1)
                    dve.wait_ge(mk_hi, 1)
                    for i in range(2):
                        for h, own in enumerate(OWN):
                            last = dve.tensor_tensor(k_lo[own, 4 * i:4 * i + 4, 2, :], psS[own, 1, i, :].rearrange("p (t s) -> p t s", t=4),
                                                     k_stack[own, 4 * i:4 * i + 4, h, 2, :].bitcast(F32), ALU.subtract)
                    last.then_inc(mk_ready, 1)
                elif mm == 1:
                    residual_and_v1(before, "wo", False, True, -1)
                else:
                    lo_of_fill(before, "ka" if mm == 2 else "kb", -1)
            row_max(0, 0)

            def attention_round(r):
                for g in range(8):
                    quad = r.pair * 8 + g
                    if not (r.last and g == 7):
                        row_max(quad + 1, (g + 1) % 2)
                    if g == 2:
                        residual_and_v1(r, "wo", not r.first, not r.last, r.pair)
                    copy_pT(quad, g % 2)
                    if g in (4, 6) and not r.last:
                        lo_of_fill(r, "ka" if g == 4 else "kb", r.pair)
                    if r.first:
                        if g == 0:
                            dve.wait_ge(x_loaded[1], 48)
                            rest.moments(4, 10)
                        elif g == 1:
                            rest.moments(10, B)
                        elif g == 2:
                            rest.aggregate()
                            rest.guess()
                        elif g == 3:
                            rest.step()
                            rest.step()
                        elif g == 4:
                            rest.step()
                    if r.last:
                        if g == 2:
                            early.moments(0, EARLY // 2)
                        elif g == 3:
                            early.moments(EARLY // 2, EARLY)
                            early.aggregate()
                        elif g == 4:
                            early.guess()
                            early.step()
                        elif g == 5:
                            early.step()
                            early.step()
                        elif g == 6:
                            early.turn_to_second()
                            early.second_step()
                        elif g == 7:
                            early.second_step()
                            early.second_step()
                    if not (r.first and g == 0):
                        normalise_attended(r, g)
                    if g == 0:
                        keep_v(r, 3)
                        if not r.last:
                            lo_of_fill(r, "xt")
                    if not r.last and g % 2:
                        lo_of_fill(r, f"q{g // 2}")
                        lo_of_fill(r, f"k{g // 2}")
                    if not r.last and g in (2, 4, 6):
                        keep_v(r, g // 2 - 1)
                    if g == 4 and not r.last and r is not LAST_BUT_ONE:
                        normalise(r.pair + 2)

            rest, early = RowStatistics(dve, chain, m, 4, B), RowStatistics(dve, chain, m, 0, EARLY)
            LAST_BUT_ONE = Round(PAIRS - 2)
            attention_round(rounds[0])
            dve.wait_ge(ffn_set, 1)
            with dve.Fori(1, PAIRS - 2) as pair:
                chain.loop(pair, 1, CHAINED_1)
                attention_round(Round(pair))
                chain.end(PAIRS - 2)
            attention_round(LAST_BUT_ONE)
            attention_round(rounds[2])
            normalise_attended(rounds[2], 8)
            residual_and_v1(rounds[2], "wo'", True, False, PAIRS)

        blocks.close()
        ctx.close()
        m.ident, m.cols, m.mcols, m.f1_bias, m.gamma = ident, cols, mcols, R_F1, R_GA
        m.beta, m.bq1, m.mq, m.w1f, m.w2f = R_BE, R_QE, R_MQ, w1f, w2f
        m.b2_bc, m.wqe, m.k1T, m.v1, m.wo1 = b2_bc, wqe, k1T, v1, wo1
        m.bo1_bc = bo1_bc
        prepare_second_attention(nc, m, lasting)
        prepare_experts(nc, m, T, lasting)
        feed_forward(nc, m)
        second_attention(nc, m)
        mixture(nc, m, T, out)


def feed_forward(nc, m):
    B, D = m.x.shape[1], m.x.shape[2]
    CH, N = 4, 4 * P
    CHUNKS = B // CH
    FT = m.w2f.shape[1]
    with ExitStack() as ctx:
        sb = lambda name, shape, dt=F32: ctx.enter_context(nc.sbuf_tensor(name, shape, dt))
        sem = lambda name: ctx.enter_context(nc.semaphore(name))
        n1 = sb("f_n1", [P, CHUNKS, CH, D])
        n2 = sb("f_n2", [P, CH, D])
        h = sb("f_h", [P, N])
        hT = sb("f_hT", [P, 2, N], F32R)
        y = sb("f_y", [P, FT, N])
        z = sb("f_z", [P, CH, D])
        b2h = sb("f_b2h", [P, D])
        psH = ctx.enter_context(nc.psum_tensor("psH", [P, N], F32))
        psY = ctx.enter_context(nc.psum_tensor("psY", [P, FT, N], F32))
        psZ = ctx.enter_context(nc.psum_tensor("psZ", [P, N], F32))
        n2_ready, h_full, h_copied, hT_ready = sem("f_n2_ready"), sem("f_h_full"), sem("f_h_copied"), sem("f_hT_ready")
        y_full, y_ready, z_full, z_read, chained = sem("f_y_full"), sem("f_y_ready"), sem("f_z_full"), sem("f_z_read"), sem("f_chained")
        with nc.Block() as block:
            m.load_experts(block)

            @block.tensor
            def _(pe):
                def transpose_in(c):
                    at_least(pe, h_copied, c)
                    pe.wait_ge(n2_ready, c + 1)
                    for t in range(CH):
                        last = pe.transpose(psH[:, t * P:(t + 1) * P], n2[:, t, :], m.ident[:])
                    last.then_inc(h_full, 1)

                def up(c):
                    pe.wait_ge(hT_ready, c + 1)
                    for f in range(FT):
                        at_least(pe, y_ready, (c - 1) * FT + f + 1)
                        lh, ll = m.w1f[:, 0, f * P:(f + 1) * P], m.w1f[:, 1, f * P:(f + 1) * P]
                        pe.matmul(psY[:, f, :], lh, hT[:, 0, :], start=True, stop=False)
                        pe.matmul(psY[:, f, :], lh, hT[:, 1, :], start=False, stop=False)
                        pe.matmul(psY[:, f, :], ll, hT[:, 0, :], start=False, stop=True).then_inc(y_full, 1)

                def down(c):
                    at_least(pe, z_read, c)
                    pe.wait_ge(y_ready, (c + 1) * FT)
                    for t in range(CH):
                        for f in range(FT):
                            last = pe.matmul(psZ[:, t * P:(t + 1) * P], y[:, f, t * P:(t + 1) * P], m.w2f[:, f, :],
                                             start=f == 0, stop=f == FT - 1)
                    last.then_inc(z_full, 1)

                transpose_in(0)
                up(0)
                transpose_in(1)
                up(1)
                for c in range(CHUNKS - 2):
                    transpose_in(c + 2)
                    down(c)
                    up(c + 2)
                down(CHUNKS - 2)
                down(CHUNKS - 1)

            @block.scalar
            def _(act):
                def scale_h(c):
                    act.wait_ge(h_full, c + 1)
                    at_least(act, hT_ready, c)
                    act.activation(h[:], psH[:], ACT.Identity, scale=m.cols[:, m.gamma:m.gamma + 1],
                                   bias=m.cols[:, m.beta:m.beta + 1]).then_inc(h_copied, 1)

                def silu(c):
                    for f in range(FT):
                        act.wait_ge(y_full, c * FT + f + 1)
                        at_least(act, z_full, c)
                        act.activation(y[:, f, :], psY[:, f, :], ACT.Silu,
                                       bias=m.cols[:, m.f1_bias + f:m.f1_bias + f + 1]).then_inc(y_ready, 1)

                scale_h(0)
                scale_h(1)
                for c in range(CHUNKS - 2):
                    silu(c)
                    scale_h(c + 2)
                silu(CHUNKS - 2)
                silu(CHUNKS - 1)

            @block.vector
            def _(dve):
                chain = Chain(dve, chained)

                def layer_norms(c):
                    for t in range(CH):
                        i = c * CH + t
                        chain.add(dve.tensor_scalar(n1[:, c, t, :], m.x[:, bass.ds(i, 1), :].rearrange("p a d -> p (a d)"),
                                                    m.mean_var[:, bass.ds(i, 1), 0], m.rstd[:, bass.ds(i, 1)], ALU.subtract, ALU.mult))
                    chain.wait()
                    at_least(dve, h_full, c)
                    for t in range(CH):
                        last = dve.tensor_scalar(n2[:, t, :], n1[:, c, t, :], m.rstd2[:, bass.ds(c * CH + t, 1)], None, ALU.mult)
                    last.then_inc(n2_ready, 1)

                def split_h(c):
                    dve.wait_ge(h_copied, c + 1)
                    at_least(dve, y_full, c * FT)
                    chain.add(dve.tensor_copy(hT[:, 0, :], h[:])).wait()
                    dve.tensor_tensor(hT[:, 1, :], h[:], hT[:, 0, :].bitcast(F32), ALU.subtract).then_inc(hT_ready, 1)

                def residual(c):
                    dve.wait_ge(z_full, c + 1)
                    dst = m.x[:, bass.ds(c * CH, CH), :]
                    ins = dve.scalar_tensor_tensor(z[:, :, :], psZ[:].rearrange("p (t d) -> p t d", t=CH), 0.5, n1[:, c, :, :],
                                                   ALU.mult, ALU.add)
                    ins.then_inc(z_read, 1)
                    chain.add(dve.tensor_tensor(dst, dst, b2h[:].rearrange("p (t d) -> p t d", t=1).to_broadcast([P, CH, D]), ALU.add))
                    chain.wait()
                    dve.wait_ge(z_read, c + 1)
                    chain.add(dve.tensor_tensor(dst, dst, z[:, :, :], ALU.add)).wait()
                    for t in range(CH):
                        last = dve.bn_stats(m.stats[:, bass.ds(c * CH + t, 1), :].rearrange("p a s -> p (a s)"),
                                            m.x[:, bass.ds(c * CH + t, 1), :].rearrange("p a d -> p (a d)"))
                    chain.add(last)

                chain.add(dve.tensor_scalar(b2h[:], m.b2_bc[:], 0.5, None, ALU.mult))
                late, next_early = RowStatistics(dve, chain, m, EARLY, B), RowStatistics(dve, chain, m, 0, 2 * CH)
                layer_norms(0)
                split_h(0)
                layer_norms(1)
                late.moments(EARLY, B)
                late.finish()
                split_h(1)
                layer_norms(2)
                late.turn_to_second()
                late.second_step()
                split_h(2)
                late.second_step()
                late.second_step()
                layer_norms(3)
                residual(0)
                split_h(3)
                residual(1)
                chain.wait()
                next_early.finish()
                residual(2)
                residual(3)
                assert CHUNKS == 4


CHUNK_FILLS_BEFORE = ["xt0", "qa0", "qb0", "xt1"]
CHUNK_FILLS = ["qa", "qb", "at", "wo", "xt"]
CHUNK_FILLS_LAST = ["at", "wo", "at'", "wo'"]
UNITS = 8
AHEAD = 4


class Chunk:

    def __init__(self, pair, parity, turn, first=False, last=False):
        self.pair, self.parity, self.turn, self.first, self.last = pair, parity, turn, first, last
        self.loads_ahead = not last and not (isinstance(pair, int) and pair + 2 >= CHUNKS_2)

    def fill(self, name):
        if self.first:
            return len(CHUNK_FILLS_BEFORE) + [f for f in CHUNK_FILLS if f not in ("at", "wo")].index(name)
        if self.last:
            return self.pair * len(CHUNK_FILLS) + (len(CHUNK_FILLS_BEFORE) - 3 + CHUNK_FILLS_LAST.index(name))
        return self.pair * len(CHUNK_FILLS) + (len(CHUNK_FILLS_BEFORE) - 2 + CHUNK_FILLS.index(name))

    def halved(self, name):
        return self.pair * 3 + (["qa", "qb", "xt"].index(name) + 5)


CHUNKS_2 = 8


def prepare_second_attention(nc, m, lasting):
    keep = lambda name, shape, dt=F32: lasting.enter_context(nc.sbuf_tensor(name, shape, dt))
    H = 16
    m.ident_b = keep("ident_b", [P, P], BF16)
    m.select = keep("select", [3 * H, H, P], BF16)
    m.select_set = lasting.enter_context(nc.semaphore("select_set"))

    def build(pool):
        chain = Chain(pool, m.select_set)
        chain.add(pool.memset(m.select[:], 0.0)).wait()
        for part in range(3):
            chain.add(pool.affine_select(out=m.select[:], in_=m.select[:], compare_op=ALU.not_equal, fill=1.0, base=-part * H,
                                         pattern=[[-1, H], [0, P]], channel_multiplier=1)).wait()
        chain.add(pool.tensor_copy(m.ident_b[:], m.ident[:])).wait()

    m.build_select = build


def second_attention(nc, m):
    B, D = m.x.shape[1], m.x.shape[2]
    S = P
    H, DH = 16, D // 16
    VW = DH + 1
    G = H // 4
    PAIRS = B // 2
    assert PAIRS == CHUNKS_2
    with ExitStack() as ctx:
        sb = lambda name, shape, dt=F32: ctx.enter_context(nc.sbuf_tensor(name, shape, dt))
        sem = lambda name: ctx.enter_context(nc.semaphore(name))
        psum = lambda name, shape: ctx.enter_context(nc.psum_tensor(name, shape, F32))
        xs = sb("s_xs", [P, 2, D])
        xt = sb("s_xt", [P, 2, 2 * S], F32R)
        q1h = sb("s_q1h", [P, 2, 2, 256], F32R)
        q1T = sb("s_q1T", [P, 2, G, 256], F32R)
        kc = sb("s_kc", [P, 2, G, 256], F32R)
        nmx = sb("s_nmx", [P, 2, 4, G])
        rest = sb("s_rest", [P, 2, H])
        parts = sb("s_parts", [P, 3, H], BF16)
        shift = sb("s_shift", [3 * H, 2, S], BF16)
        pT = sb("s_pT", [P, 4, G * S])
        k_blocks = sb("s_k_blocks", [P, 2, G, 4, S], F32R)
        q_blocks = sb("s_q_blocks", [P, 2, G, 4, S], F32R)
        v_wide = sb("s_v_wide", [P, 2, 2, H, 32])
        oT = sb("s_oT", [P, 4 * S])
        rec = sb("s_rec", [P, 2, H])
        at = sb("s_at", [P, 2, 2, D])
        aT = sb("s_aT", [P, 2, S])
        psS, psE = psum("s_psS", [P, 2, 512]), psum("s_psE", [P, 2, 512])
        psO, psR = psum("s_psO", [P, 512]), psum("s_psR", [P, 512])
        psM, psN = psum("s_psM", [P, 512]), psum("s_psN", [3 * H, 512])
        xs_ready, misc_full, misc_done, hi_ready = sem("s_xs_ready"), sem("s_misc_full"), sem("s_misc_done"), sem("s_hi_ready")
        scores_full, max_ready, parts_ready = sem("s_scores_full"), sem("s_max_ready"), sem("s_parts_ready")
        shift_full, shift_ready, shifted_full, probs_ready = sem("s_shift_full"), sem("s_shift_ready"), sem("s_shifted_full"), sem("s_probs_ready")
        values_full, values_copied, rows_full = sem("s_values_full"), sem("s_values_copied"), sem("s_rows_full")
        values_read, chained, v_ready, blank = sem("s_values_read"), sem("s_chained"), sem("s_v_ready"), sem("s_blank")
        keys_in = [[sem(f"s_keys_in{parity}{b}") for b in range(2)] for parity in range(2)]
        queries_in = [sem(f"s_queries_in{b}") for b in range(2)]

        def chunks(engine, body, chain=None):
            body(Chunk(0, 0, 0, first=True))
            body(Chunk(1, 1, 0))
            with engine.Fori(1, PAIRS // 2 - 1) as two:
                if chain:
                    chain.loop(two, 1, CHAINED_2)
                body(Chunk(two * 2, 0, two))
                body(Chunk(two * 2 + 1, 1, two))
                if chain:
                    chain.end(PAIRS // 2 - 1)
            body(Chunk(PAIRS - 2, 0, PAIRS // 2 - 1))
            body(Chunk(PAIRS - 1, 1, PAIRS // 2 - 1, last=True))

        with nc.Block() as block:
            @block.sync
            def _(sp):
                def place_keys(parity, b, batch):
                    keys = bass.ds(batch * S, S)
                    sp.dma_start(kc[:, parity, :, b * S:(b + 1) * S].bitcast(F32), m.k1T[:, :, keys].bitcast(F32)).then_inc(keys_in[parity][b], 16)
                    for j in range(4):
                        rows = slice(32 * j, 32 * j + 3 * DH)
                        sp.dma_start(k_blocks[rows, b, :, j, :].bitcast(F32), m.k1T[rows, :, keys].bitcast(F32)).then_inc(keys_in[parity][b], 16)

                def place_queries(parity, b):
                    for j in range(4):
                        rows = slice(32 * j, 32 * j + 3 * DH)
                        sp.dma_start(q_blocks[rows, b, :, j, :].bitcast(F32), q1T[rows, parity, :, b * S:(b + 1) * S].bitcast(F32)).then_inc(queries_in[b], 16)

                sp.wait_ge(blank, 1)
                place_keys(0, 0, 0)
                place_keys(0, 1, 1)
                sp.wait_ge(misc_done, 3)
                sp.wait_ge(blank, 3)
                place_queries(0, 0)
                place_queries(0, 1)

                def chunk(c):
                    if c.last:
                        return
                    if c.first:
                        sp.wait_ge(scores_full, 4)
                    at_least(sp, shifted_full, c.pair * UNITS)
                    place_keys(1 - c.parity, 0, c.pair * 2 + 2)
                    sp.wait_ge(shifted_full, c.pair * UNITS + 4)
                    place_keys(1 - c.parity, 1, c.pair * 2 + 3)
                    sp.wait_ge(shifted_full, c.pair * UNITS + 6)
                    place_queries(1 - c.parity, 0)
                    sp.wait_ge(shifted_full, c.pair * UNITS + 8)
                    place_queries(1 - c.parity, 1)

                chunks(sp, chunk)

            @block.gpsimd
            def _(pool):
                def place_values(parity, b, batch, used):
                    at_least(pool, values_full, used)
                    pool.tensor_copy(v_wide[:, parity, b, :, 0:DH], m.v1[:, bass.ds(batch, 1), :, 0:DH].rearrange("p a h d -> p (a h) d")).then_inc(v_ready, 1)

                def chunk(c):
                    if not c.last:
                        for b in range(2):
                            place_values(1 - c.parity, b, c.pair * 2 + (2 + b), c.pair * UNITS + (4 * b - 4))

                pool.memset(k_blocks[:].bitcast(F32), 0.0).then_inc(blank, 1)
                pool.memset(v_wide[:], 1.0).then_inc(blank, 1)
                pool.memset(q_blocks[:].bitcast(F32), 0.0).then_inc(blank, 1)
                pool.wait_ge(blank, 2)
                place_values(0, 0, 0, 0)
                place_values(0, 1, 1, 0)
                chunks(pool, chunk)

            @block.tensor
            def _(pe):
                def opened(n):
                    at_least(pe, misc_done, n)

                def transpose_inputs(n, pair):
                    opened(n)
                    pe.wait_ge(xs_ready, pair + 1)
                    for t in range(2):
                        last = pe.transpose(psM[:, t * P:(t + 1) * P], xs[:, t, :], m.ident[:])
                    last.then_inc(misc_full, 1)

                def project_q(n, half):
                    opened(n)
                    for i in range(2):
                        t = 2 * half + i
                        lh, ll = m.wqe[:, 0, t * P:(t + 1) * P], m.wqe[:, 1, t * P:(t + 1) * P]
                        dst = psM[:, 256 * i:256 * i + 256]
                        pe.matmul(dst, lh, xt[:, 0, :], start=True, stop=False)
                        pe.matmul(dst, lh, xt[:, 1, :], start=False, stop=False)
                        last = pe.matmul(dst, ll, xt[:, 0, :], start=False, stop=True)
                    last.then_inc(misc_full, 1)

                def scores(unit, parity, b, t):
                    at_least(pe, max_ready, unit - 1)
                    pe.matmul(psS[:, t % 2, :], q1T[:, parity, t, b * S:(b + 1) * S],
                              k_blocks[:, b, t].rearrange("p j s -> p (j s)"), start=True, stop=True).then_inc(scores_full, 1)

                def transpose_maxima(batch):
                    at_least(pe, shift_ready, batch)
                    pe.wait_ge(parts_ready, batch + 1)
                    pe.matmul(psN[:, 0:S], parts[:, :, :].rearrange("p a h -> p (a h)"), m.ident_b[:],
                              start=True, stop=True).then_inc(shift_full, 1)

                def shifted_scores(c, u):
                    b, t = u // 4, u % 4
                    unit = c.pair * UNITS + u
                    at_least(pe, probs_ready, unit - 1)
                    if t == 0:
                        pe.wait_ge(queries_in[b], c.pair * 64 + 64)
                        pe.wait_ge(shift_ready, c.pair * 2 + (b + 1))
                    pe.matmul(psE[:, t % 2, :], kc[:, c.parity, t, b * S:(b + 1) * S],
                              q_blocks[:, b, t].rearrange("p j s -> p (j s)"), start=True, stop=False)
                    for j in range(4):
                        last = pe.matmul(psE[:, t % 2, j * S:(j + 1) * S], m.select[:, t * 4 + j, :], shift[:, b, :],
                                         start=False, stop=j == 3)
                    last.then_inc(shifted_full, 1)

                def attend(c, local):
                    u = (local - 1) % UNITS
                    b, t = u // 4, u % 4
                    batch = c.pair * 2 + (b if local else -1)
                    parity = c.parity if local else 1 - c.parity
                    pe.wait_ge(probs_ready, c.pair * UNITS + local)
                    if t == 0:
                        at_least(pe, values_copied, batch)
                        pe.wait_ge(v_ready, batch + 1)
                    for j in range(4):
                        last = pe.matmul(psO[32 * j:32 * j + 32, t * S:(t + 1) * S], v_wide[:, parity, b, t * 4 + j, :],
                                         pT[:, t, j * S:(j + 1) * S], start=True, stop=True)
                    last.then_inc(values_full, 1)

                def turn_values(batch):
                    pe.wait_ge(values_copied, batch + 1)
                    at_least(pe, values_read, batch)
                    for t in range(4):
                        last = pe.transpose(psR[:, t * S:(t + 1) * S], oT[:, t * S:(t + 1) * S], m.ident[:])
                    last.then_inc(rows_full, 1)

                def transpose_attended(c, name, batches, parity):
                    opened(c.fill(name))
                    at_least(pe, values_read, batches)
                    for b in range(2):
                        last = pe.transpose(psM[:, b * P:(b + 1) * P], at[:, parity, b, :], m.ident[:])
                    last.then_inc(misc_full, 1)

                def project_out(c, name):
                    opened(c.fill(name))
                    for b in range(2):
                        last = pe.matmul(psM[:, b * P:(b + 1) * P], aT[:, b, :], m.wo1[:], start=True, stop=True)
                    last.then_inc(misc_full, 1)

                transpose_inputs(0, 0)
                project_q(1, 0)
                project_q(2, 1)
                transpose_inputs(3, 1)
                pe.wait_ge(misc_done, 3)
                pe.wait_ge(keys_in[0][0], 80)
                for u in range(AHEAD):
                    scores(u, 0, 0, u)
                transpose_maxima(0)

                def chunk(c):
                    for u in range(UNITS):
                        b, j = u // 4, u % 4
                        shifted_scores(c, u)
                        ahead = not (c.last and b == 1)
                        if ahead:
                            if j == 0:
                                if b == 0:
                                    pe.wait_ge(keys_in[c.parity][1], c.turn * 80 + 80)
                                else:
                                    pe.wait_ge(keys_in[1 - c.parity][0], (c.turn + c.parity) * 80 + 80)
                                if b == 1:
                                    pe.wait_ge(misc_done, c.fill("qb") + 1)
                            for v in (2 * j, 2 * j + 1) if j < 2 else ():
                                scores(c.pair * UNITS + (4 * b + 4 + v), c.parity if b == 0 else 1 - c.parity, 1 - b, v)
                        if not (c.first and u == 0):
                            attend(c, u)
                        if j == 1 and not (c.first and u == 1):
                            turn_values(c.pair * 2 + (b - 1))
                        if ahead and j == 3:
                            transpose_maxima(c.pair * 2 + (b + 1))
                        if u in (0, 1) and not c.last:
                            project_q(c.fill("qa" if u == 0 else "qb"), u)
                        if u == 3 and not c.first:
                            transpose_attended(c, "at", c.pair * 2, 1 - c.parity)
                        if u == 4 and not c.first:
                            project_out(c, "wo")
                        if u == 6 and c.loads_ahead:
                            transpose_inputs(c.fill("xt"), c.pair + 2)

                chunks(pe, chunk)
                end = Chunk(PAIRS - 1, 1, PAIRS // 2 - 1, last=True)
                attend(Chunk(PAIRS, 0, 0), 0)
                turn_values(B - 1)
                transpose_attended(end, "at'", B, 1)
                project_out(end, "wo'")

            @block.scalar
            def _(act):
                def hi_x(n):
                    act.wait_ge(misc_full, n + 1)
                    act.copy(xt[:, 0, :], psM[:, 0:256]).then_inc(hi_ready, 1)

                def hi_q(n, half):
                    act.wait_ge(misc_full, n + 1)
                    for i in range(2):
                        t = 2 * half + i
                        last = act.activation(q1h[:, half, i, :], psM[:, 256 * i:256 * i + 256], ACT.Identity,
                                              scale=m.cols[:, m.mq:m.mq + 1], bias=m.mcols[:, t:t + 1])
                    last.then_inc(hi_ready, 1)

                def copy_shift(batch, b):
                    act.wait_ge(shift_full, batch + 1)
                    at_least(act, shifted_full, batch * 4 - 4)
                    act.copy(shift[:, b, :], psN[:, 0:S]).then_inc(shift_ready, 1)

                def exps(unit, j):
                    act.wait_ge(shifted_full, unit + 1)
                    at_least(act, values_full, unit - 3)
                    act.activation(pT[:, j, :], psE[:, j % 2, :], ACT.Exp).then_inc(probs_ready, 1)

                def copy_values(batch):
                    act.wait_ge(values_full, batch * 4 + 4)
                    at_least(act, rows_full, batch)
                    act.copy(oT[:], psO[:]).then_inc(values_copied, 1)

                hi_x(0)
                hi_q(1, 0)
                hi_q(2, 1)
                hi_x(3)
                copy_shift(0, 0)

                def chunk(c):
                    for u in range(UNITS):
                        b, j = u // 4, u % 4
                        exps(c.pair * UNITS + u, j)
                        if j == 0 and not (c.first and u == 0):
                            copy_values(c.pair * 2 + (b - 1))
                        if j == 3 and not (c.last and b == 1):
                            copy_shift(c.pair * 2 + (b + 1), 1 - b)
                        if u in (0, 1) and not c.last:
                            hi_q(c.fill("qa" if u == 0 else "qb"), u)
                        if u == 6 and c.loads_ahead:
                            hi_x(c.fill("xt"))

                chunks(act, chunk)
                copy_values(B - 1)

            @block.vector
            def _(dve):
                chain = Chain(dve, chained)

                def normalise(pair):
                    for i in range(2):
                        t = pair * 2 + i
                        last = dve.tensor_scalar(xs[:, i, :], m.x[:, bass.ds(t, 1), :].rearrange("p a d -> p (a d)"),
                                                 m.mean_var[:, bass.ds(t, 1), 0], m.rstd[:, bass.ds(t, 1)], ALU.subtract, ALU.mult)
                    last.then_inc(xs_ready, 1)

                def lo_x(n, done):
                    dve.wait_ge(misc_full, n + 1)
                    dve.wait_ge(hi_ready, done)
                    dve.tensor_tensor(xt[:, 1, :], psM[:, 0:256], xt[:, 0, :].bitcast(F32), ALU.subtract).then_inc(misc_done, 1)

                def lo_q(n, half, parity, done):
                    dve.wait_ge(misc_full, n + 1)
                    dve.wait_ge(hi_ready, done)
                    for i in range(2):
                        t = 2 * half + i
                        last = dve.scalar_tensor_tensor(q1T[:, parity, t, :], psM[:, 256 * i:256 * i + 256],
                                                        m.cols[:, m.bq1 + t:m.bq1 + t + 1], q1h[:, half, i, :].bitcast(F32),
                                                        ALU.add, ALU.subtract)
                    last.then_inc(misc_done, 1)

                def row_max(unit, b, j):
                    dve.wait_ge(scores_full, unit + 1)
                    dve.tensor_reduce(nmx[:, b, j, :], psS[:, j % 2, :].rearrange("p (t k) -> p t k", t=G), AX_X, ALU.max,
                                      negate=True).then_inc(max_ready, 1)

                def split_maxima(batch, b):
                    dve.wait_ge(max_ready, batch * 4 + 4)
                    at_least(dve, shift_full, batch)
                    whole = nmx[:, b].rearrange("p t j -> p (t j)")
                    chain.add(dve.tensor_copy(parts[:, 0, :], whole)).wait()
                    chain.add(dve.tensor_tensor(rest[:, 0, :], whole, parts[:, 0, :], ALU.subtract)).wait()
                    chain.add(dve.tensor_copy(parts[:, 1, :], rest[:, 0, :])).wait()
                    dve.tensor_tensor(parts[:, 2, :], rest[:, 0, :], parts[:, 1, :], ALU.subtract).then_inc(parts_ready, 1)

                def normalise_attended(b, batches):
                    dve.wait_ge(rows_full, batches)
                    o = psR[:].rearrange("p (h d) -> p h d", h=H)
                    chain.add(dve.reciprocal(rec[:, b, :], o[:, :, DH])).wait()
                    return o

                def scale_attended(o, parity, b):
                    dve.tensor_tensor(at[:, parity, b, :].rearrange("p (h d) -> p h d", h=H), o[:, :, 0:DH],
                                      rec[:, b, :].rearrange("p (h d) -> p h d", d=1).to_broadcast([P, H, DH]), ALU.mult).then_inc(values_read, 1)

                def copy_attended(n):
                    dve.wait_ge(misc_full, n + 1)
                    dve.tensor_copy(aT[:, :, :], psM[:, 0:256].rearrange("p (b s) -> p b s", b=2)).then_inc(misc_done, 1)

                def residual(n, pair):
                    dve.wait_ge(misc_full, n + 1)
                    dst = m.x[:, bass.ds(pair * 2, 2), :]
                    dve.tensor_tensor(dst, dst, psM[:, 0:256].rearrange("p (b d) -> p b d", b=2), ALU.add).then_inc(misc_done, 1)
                    dve.wait_ge(misc_done, n + 1)
                    chain.add(dve.tensor_tensor(dst, dst, m.bo1_bc[:].rearrange("p (b d) -> p b d", b=1).to_broadcast([P, 2, D]), ALU.add))
                    chain.wait()
                    for t in range(2):
                        last = dve.bn_stats(m.stats[:, bass.ds(pair * 2 + t, 1), :].rearrange("p a s -> p (a s)"),
                                            m.x[:, bass.ds(pair * 2 + t, 1), :].rearrange("p a d -> p (a d)"))
                    chain.add(last)

                normalise(0)
                lo_x(0, 1)
                normalise(1)
                lo_q(1, 0, 0, 2)
                lo_q(2, 1, 0, 3)
                lo_x(3, 4)
                for u in range(AHEAD):
                    row_max(u, 0, u)
                split_maxima(0, 0)

                def chunk(c):
                    for u in range(UNITS):
                        b, j = u // 4, u % 4
                        ahead = not (c.last and b == 1)
                        first_max = c.pair * UNITS + (4 * b + 4)
                        if ahead and j < 2:
                            row_max(first_max + 2 * j, 1 - b, 2 * j)
                            row_max(first_max + 2 * j + 1, 1 - b, 2 * j + 1)
                        if ahead and j == 2:
                            split_maxima(c.pair * 2 + (b + 1), 1 - b)
                        if u in (0, 1) and not c.last:
                            at_least(dve, shifted_full, c.pair * UNITS)
                            name = "qa" if u == 0 else "qb"
                            lo_q(c.fill(name), u, 1 - c.parity, c.halved(name))
                        if j == 2 and not (c.first and u == 2):
                            o = normalise_attended(1 - b, c.pair * 2 + b)
                            scale_attended(o, c.parity if b else 1 - c.parity, 1 - b)
                        if u == 3 and not c.first:
                            copy_attended(c.fill("at"))
                        if u == 4 and not c.first:
                            residual(c.fill("wo"), c.pair - 1)
                        if u == 4 and c.loads_ahead:
                            normalise(c.pair + 2)
                        if u == 6 and c.loads_ahead:
                            lo_x(c.fill("xt"), c.halved("xt"))
                        if c.first and u == 5:
                            late.aggregate()
                            late.guess()
                        if c.first and u == 7:
                            for _ in range(3):
                                late.step()
                        if c.last and u == 5:
                            early.aggregate()
                            early.guess()
                        if c.last and u == 6:
                            for _ in range(3):
                                early.step()

                late, early = RowStatistics(dve, chain, m, 8, B), RowStatistics(dve, chain, m, 0, EARLY)
                chunks(dve, chunk, chain)
                end = Chunk(PAIRS - 1, 1, PAIRS // 2 - 1, last=True)
                o = normalise_attended(1, B)
                scale_attended(o, 1, 1)
                copy_attended(end.fill("at'"))
                residual(end.fill("wo'"), PAIRS - 1)


CHAINED_2 = 20


CAP_FACTOR, TOP = 1.25, 2
RING = 2


def prepare_experts(nc, m, T, lasting):
    D, E = P, T["L1_ffn_router_w"].shape[0]
    IR, IS = T["L1_ffn_rg"].shape[2], T["L1_ffn_sg"].shape[1]
    keep = lambda name, shape, dt=F32: lasting.enter_context(nc.sbuf_tensor(name, shape, dt))
    sem = lambda name: lasting.enter_context(nc.semaphore(name))
    m.E, m.IR, m.IS = E, IR, IS
    m.capacity = max(int(CAP_FACTOR * m.x.shape[1] * P / E), 1)
    m.slots = E * m.capacity
    m.router = keep("router", [E, D])
    m.sd = keep("sd", [P, IS // P, D])
    m.sgu = keep("sgu", [P, 2, 2, IS], F32R)
    m.sgu_raw = keep("sgu_raw", [P, 2, IS])
    m.rgu = keep("rgu", [P, RING, 2, 2, IR], F32R)
    m.rgu_raw = keep("rgu_raw", [P, RING, 2, IR])
    m.rd = keep("rd", [P, RING, IR // P, D])
    m.zeros = keep("zeros", [P, D])
    m.gathered = nc.dram_tensor("gathered", (m.slots, D), F32, kind="Internal").ap()
    m.expert_out = nc.dram_tensor("expert_out", (m.slots + 1, D), F32, kind="Internal").ap()
    m.shared_loaded, m.zeroed, m.zeros_set = sem("shared_loaded"), sem("zeroed"), sem("zeros_set")
    m.raw_loaded = [sem(f"raw_loaded{i}") for i in range(RING)]
    m.rd_loaded = [sem(f"rd_loaded{i}") for i in range(RING)]
    m.shared_split, m.expert_split, m.pool_chained = sem("shared_split"), sem("expert_split"), sem("pool_chained")

    def load_expert(sp, e, slot):
        index = lambda name: T[name][bass.ds(e, 1)].rearrange("a k n -> k (a n)")
        sp.dma_start(m.rgu_raw[:, slot, 0, :], index("L1_ffn_rg")).then_inc(m.raw_loaded[slot], 16)
        sp.dma_start(m.rgu_raw[:, slot, 1, :], index("L1_ffn_ru")).then_inc(m.raw_loaded[slot], 16)

    def load_down(sp, e, slot):
        sp.dma_start(m.rd[:, slot, :, :], T["L1_ffn_rd"][bass.ds(e, 1)].rearrange("a (t p) n -> p (a t) n", p=P)).then_inc(m.rd_loaded[slot], 16)

    def load_experts(block):
        @block.gpsimd
        def _(pool):
            pool.memset(m.zeros[:], 0.0).then_inc(m.zeros_set, 1)
            m.build_select(pool)
            split_experts(pool)

        @block.sync
        def _(sp):
            sp.dma_start(m.sgu_raw[:, 0, :], T["L1_ffn_sg"]).then_inc(m.shared_loaded, 16)
            sp.dma_start(m.sgu_raw[:, 1, :], T["L1_ffn_su"]).then_inc(m.shared_loaded, 16)
            sp.dma_start(m.sd[:], T["L1_ffn_sd"].rearrange("(t p) n -> p t n", p=P)).then_inc(m.shared_loaded, 16)
            sp.dma_start(m.router[:], T["L1_ffn_router_w"]).then_inc(m.shared_loaded, 16)
            for e in range(RING):
                load_expert(sp, e, e)
                load_down(sp, e, e)
            sp.wait_ge(m.zeros_set, 1)
            tiles = m.slots // P
            sp.dma_start(m.gathered.rearrange("(t p) d -> p t d", p=P),
                         m.zeros[:].rearrange("p (t d) -> p t d", t=1).to_broadcast([P, tiles, D])).then_inc(m.zeroed, 16)
            sp.dma_start(m.expert_out[m.slots:m.slots + 1, :], m.zeros[0:1, :]).then_inc(m.zeroed, 16)

    def split(pool, chain, dst, src):
        for i in range(2):
            chain.add(pool.tensor_copy(dst[:, i, 0, :], src[:, i, :]))
        chain.wait()
        pool.tensor_tensor(dst[:, 0, 1, :], src[:, 0, :], dst[:, 0, 0, :].bitcast(F32), ALU.subtract)
        return pool.tensor_tensor(dst[:, 1, 1, :], src[:, 1, :], dst[:, 1, 0, :].bitcast(F32), ALU.subtract)

    def split_experts(pool):
        chain = Chain(pool, m.pool_chained)
        pool.wait_ge(m.shared_loaded, 64)
        split(pool, chain, m.sgu, m.sgu_raw).then_inc(m.shared_split, 1)
        for e in range(RING):
            pool.wait_ge(m.raw_loaded[e], 32)
            split(pool, chain, m.rgu[:, e], m.rgu_raw[:, e]).then_inc(m.expert_split, 1)

    m.load_expert, m.load_down, m.load_experts, m.split, m.split_experts = load_expert, load_down, load_experts, split, split_experts


def mixture(nc, m, T, out):
    B, D = m.x.shape[1], m.x.shape[2]
    E, IR, IS, CAP, SLOTS = m.E, m.IR, m.IS, m.capacity, m.slots
    N = 256
    FS, FE = IS // P, IR // P
    ST = SLOTS // P
    assert SLOTS % P == 0 and CAP <= 512 and CAP % 2 == 0 and RING == 2 and TOP == 2
    SLOT_TILES = [(a, min(P, CAP - a)) for a in range(0, CAP, P)]
    with ExitStack() as ctx:
        sb = lambda name, shape, dt=F32: ctx.enter_context(nc.sbuf_tensor(name, shape, dt))
        sem = lambda name: ctx.enter_context(nc.semaphore(name))
        psum = lambda name, shape: ctx.enter_context(nc.psum_tensor(name, shape, F32))
        u = sb("m_u", [P, B, D])
        uT = sb("m_uT", [P, 2, B * P], F32R)
        xgT_hi = sb("m_xgT_hi", [P, SLOTS], F32R)
        xgT_lo = sb("m_xgT_lo", [P, SLOTS], F32R)
        xg = sb("m_xg", [P, ST, D])
        rwT = sb("m_rwT", [P, 2, E], F32R)
        rms = sb("m_rms", [P, B])
        iota = sb("m_iota", [P, E])
        ones, tri = sb("m_ones", [P, P]), sb("m_tri", [P, P])
        logits = sb("m_logits", [P, B, E])
        index = sb("m_index", [P, B, 8], U32)
        chosen = sb("m_chosen", [P, 2, B])
        one_hot = sb("m_one_hot", [P, 2, B, E])
        mask = sb("m_mask", [P, B, E])
        prefix = sb("m_prefix", [P, 2, B, E])
        place = sb("m_place", [P, 2, B, E])
        others, top = place[:, 0], [sb("m_top", [P, B, 8]), place[:, 1]]
        assert E == 8
        pos = sb("m_pos", [P, 2, B])
        valid = sb("m_valid", [P, 2, B])
        slot = sb("m_slot", [P, 2, B], U32)
        weight = sb("m_weight", [P, 2, B])
        gap = sb("m_gap", [P, 2, B])
        s = sb("m_s", [P, 2, 512])
        a = sb("m_a", [P, 2, FS, N])
        ae = a[:, :, :, :].rearrange("p b f n -> p b (f n)")[:, :, 0:FE * CAP].rearrange("p b (f n) -> p b f n", f=FE)
        eo = sb("m_eo", [P, 2, len(SLOT_TILES), D])
        picked = m.k1T[:].bitcast(F32).rearrange("p g n -> p (g n)")[:, 0:2 * B * D].rearrange("p (c t d) -> p c t d", c=2, d=D)
        psG, psU, psD, psX = psum("m_psG", [P, 2, 512]), psum("m_psU", [P, 2, 512]), psum("m_psD", [P, 2, 512]), psum("m_psX", [P, 2, 512])
        consts, u_ready, x_full, x_done, hi_done = sem("m_consts"), sem("m_u_ready"), sem("m_x_full"), sem("m_x_done"), sem("m_hi_done")
        gap_ready, gap_exp, mask_ready, slot_ready = sem("m_gap_ready"), sem("m_gap_exp"), sem("m_mask_ready"), sem("m_slot_ready")
        scattered, xg_loaded, w_hi = sem("m_scattered"), sem("m_xg_loaded"), sem("m_w_hi")
        gu_full, s_ready, a_ready, down_full, down_read = sem("m_gu_full"), sem("m_s_ready"), sem("m_a_ready"), sem("m_down_full"), sem("m_down_read")
        eo_stored, picked_in = [sem(f"m_eo_stored{b}") for b in range(2)], [sem(f"m_picked{g}") for g in range(4)]
        combined, stored = sem("m_combined"), sem("m_stored")
        chained = sem("m_chained")
        SH_ROUNDS = B * P // N // 4
        EX_ROUNDS = E // 2

        class Section:
            def __init__(self, kind, i, part=0, last=False):
                self.kind, self.i, self.part, self.last = kind, i, part, last
                self.first = kind == "shared" and part == 0 and isinstance(i, int) and i == 0
                self.tiles = FE if kind == "expert" else FS
                if kind == "expert":
                    self.tile0 = i * (2 * FE) + SH_ROUNDS * 2 * FS
                    self.job0 = i * 2 + SH_ROUNDS * 2
                else:
                    self.tile0 = i * (2 * FS) + part * (SH_ROUNDS * 2 * FS + EX_ROUNDS * 2 * FE)
                    self.job0 = i * 2 + part * (SH_ROUNDS * 2 + EX_ROUNDS * 2)
                self.item0 = i * 2 + (part * SH_ROUNDS * 2 if kind == "shared" else 0)

        def sections(engine, body, before_experts=None):
            for i in range(SH_ROUNDS):
                body(Section("shared", i))
            if before_experts:
                before_experts()
            body(Section("expert", 0))
            with engine.Fori(1, EX_ROUNDS - 1) as i:
                body(Section("expert", i))
            body(Section("expert", EX_ROUNDS - 1, last=True))
            for i in range(SH_ROUNDS):
                body(Section("shared", i, 1, last=i == SH_ROUNDS - 1))

        X_ROUTER, X_UT, X_LOGITS, X_PLACE, X_XGT = 0, 1, 5, 6, 7
        XG_FILLS = ST // 4
        COMBINE_AT = (2, 6, 12)
        ROUTER_COUNT = 4
        with nc.Block() as block:
            @block.sync
            def _(sp):
                for b in range(2):
                    m.load_expert(sp, 2 + b, b)
                sp.wait_ge(scattered, 16 * 2 * B)
                sp.dma_start(xg[:], m.gathered.rearrange("(t p) d -> p t d", p=P)).then_inc(xg_loaded, 16)

                def expert_round(i):
                    if not (isinstance(i, int) and i + 2 >= EX_ROUNDS):
                        for b in range(2):
                            sp.wait_ge(m.expert_split, i * 2 + (b + 3))
                            m.load_expert(sp, (i + 2) * 2 + b, b)
                    if not (isinstance(i, int) and i + 1 >= EX_ROUNDS):
                        for b in range(2):
                            sp.wait_ge(down_full, i * 2 + (SH_ROUNDS * 2 + b + 1))
                            m.load_down(sp, (i + 1) * 2 + b, b)
                    for b in range(2):
                        sp.wait_ge(down_read, i * 2 + (SH_ROUNDS * 2 + b + 1))
                        whole, (at, rows) = len(SLOT_TILES) - 1, SLOT_TILES[-1]
                        sp.dma_start(m.expert_out[bass.ds((i * 2 + b) * CAP, at)].rearrange("(t p) d -> p t d", p=P),
                                     eo[:, b, 0:whole, :]).then_inc(eo_stored[b], 16)
                        sp.dma_start(m.expert_out[bass.ds((i * 2 + b) * CAP + at, rows)],
                                     eo[0:rows, b, whole, :]).then_inc(eo_stored[b], 16)

                with sp.Fori(0, EX_ROUNDS - 2) as i:
                    expert_round(i)
                for i in range(EX_ROUNDS - 2, EX_ROUNDS):
                    expert_round(i)
                for g in range(4):
                    sp.wait_ge(combined, g + 1)
                    sp.dma_start(out[4 * g:4 * g + 4].rearrange("b s d -> s b d"), m.x[:, 4 * g:4 * g + 4, :]).then_inc(stored, 16)
                sp.wait_ge(stored, 64)

            @block.gpsimd
            def _(pool):
                pool.memset(ones[:], 1.0).then_inc(consts, 1)
                for e in range(E):
                    last = pool.memset(iota[:, e:e + 1], float(e))
                last.then_inc(consts, 1)
                pool.wait_ge(consts, 1)
                pool.affine_select(out=tri[:], in_=ones[:], compare_op=ALU.is_gt, fill=0.0, base=0,
                                   pattern=[[1, P]], channel_multiplier=-1).then_inc(consts, 1)
                pool.wait_ge(slot_ready, 1)
                pool.wait_ge(m.zeroed, 32)
                for t in range(B):
                    for c in range(TOP):
                        pool.indirect_dma_start(m.gathered, bass.IndirectOffsetOnAxis(ap=slot[:, c, t:t + 1], axis=0),
                                                u[:, t, :], None, bounds_check=SLOTS - 1, oob_is_err=False).then_inc(scattered, 16)
                for b in range(2):
                    pool.wait_ge(eo_stored[b], 32 * EX_ROUNDS)
                for t in range(B):
                    for c in range(TOP):
                        pool.indirect_dma_start(picked[:, c, t, :], None, m.expert_out,
                                                bass.IndirectOffsetOnAxis(ap=slot[:, c, t:t + 1], axis=0)).then_inc(picked_in[t // 4], 16)

            @block.tensor
            def _(pe):
                def product(dst, lh, ll, rh, rl):
                    pe.matmul(dst, lh, rh, start=True, stop=False)
                    pe.matmul(dst, lh, rl, start=False, stop=False)
                    return pe.matmul(dst, ll, rh, start=False, stop=True)

                pe.transpose(psX[:, 0, 0:E], m.router[:], m.ident[0:E, 0:E]).then_inc(x_full, 1)
                for f in range(4):
                    n = X_UT + f
                    at_least(pe, x_done, n - 1)
                    pe.wait_ge(u_ready, f + 1)
                    for t in range(4):
                        last = pe.transpose(psX[:, n % 2, t * P:(t + 1) * P], u[:, 4 * f + t, :], m.ident[:])
                    last.then_inc(x_full, 1)
                pe.wait_ge(x_done, X_LOGITS)
                for t in range(B):
                    part = slice(t * P, (t + 1) * P)
                    at = t * 2 * E
                    pe.matmul(psX[:, X_LOGITS % 2, at:at + 2 * E], uT[:, 0, part], rwT[:, :, :].rearrange("p h e -> p (h e)"),
                              start=True, stop=False)
                    last = pe.matmul(psX[:, X_LOGITS % 2, at:at + E], uT[:, 1, part], rwT[:, 0, :], start=False, stop=True)
                last.then_inc(x_full, 1)
                def count_chosen():
                    pe.wait_ge(mask_ready, 1)
                    pe.wait_ge(consts, 3)
                    chosen_in = mask[:, :, :].rearrange("p b e -> p (b e)")
                    pe.matmul(psX[:, X_PLACE % 2, 0:B * E], tri[:], chosen_in, start=True, stop=True)
                    pe.matmul(psX[:, X_PLACE % 2, B * E:2 * B * E], ones[:], chosen_in, start=True, stop=True).then_inc(x_full, 1)

                def jobs(sec):
                    n = N if sec.kind == "shared" else CAP
                    for b in range(2):
                        if sec.kind == "expert":
                            pe.wait_ge(m.expert_split, sec.item0 + b + 1)
                        for f in range(sec.tiles):
                            k = b * sec.tiles + f
                            tile = sec.tile0 + k
                            at_least(pe, a_ready, tile - 1)
                            w = m.sgu if sec.kind == "shared" else m.rgu[:, b]
                            cols = slice(f * P, (f + 1) * P)
                            at = bass.ds((sec.item0 + b) * n, n)
                            rh, rl = (uT[:, 0, at], uT[:, 1, at]) if sec.kind == "shared" else (xgT_hi[:, at], xgT_lo[:, at])
                            product(psG[:, k % 2, 0:n], w[:, 0, 0, cols], w[:, 0, 1, cols], rh, rl)
                            product(psU[:, k % 2, 0:n], w[:, 1, 0, cols], w[:, 1, 1, cols], rh, rl).then_inc(gu_full, 1)
                            if sec.first and k == ROUTER_COUNT:
                                count_chosen()
                    for b in range(2):
                        pe.wait_ge(a_ready, sec.tile0 + (b + 1) * sec.tiles)
                        at_least(pe, down_read, sec.job0 + (b - 1))
                        if sec.kind == "expert":
                            pe.wait_ge(m.rd_loaded[b], sec.i * 16 + 16)
                        tiles = SLOT_TILES if sec.kind == "expert" else [(c, P) for c in range(0, N, P)]
                        w, act = (m.rd[:, b], ae) if sec.kind == "expert" else (m.sd, a)
                        for c, (at, rows) in enumerate(tiles):
                            for f in range(sec.tiles):
                                last = pe.matmul(psD[0:rows, b, c * P:(c + 1) * P], act[:, b, f, at:at + rows], w[:, f, :],
                                                 start=f == 0, stop=f == sec.tiles - 1)
                        last.then_inc(down_full, 1)

                def transpose_slots():
                    pe.wait_ge(xg_loaded, 16)
                    for f in range(XG_FILLS):
                        n = X_XGT + f
                        pe.wait_ge(x_done, n - 1)
                        for t in range(4):
                            last = pe.transpose(psX[:, n % 2, t * P:(t + 1) * P], xg[:, 4 * f + t, :], m.ident[:])
                        last.then_inc(x_full, 1)
                    pe.wait_ge(x_done, X_XGT + XG_FILLS)

                pe.wait_ge(m.shared_split, 1)
                sections(pe, jobs, transpose_slots)

            @block.scalar
            def _(act):
                def hi(n, dst):
                    act.wait_ge(x_full, n + 1)
                    act.copy(dst, psX[:, n % 2, :]).then_inc(hi_done, 1)

                for f in range(4):
                    hi(X_UT + f, uT[:, 0, f * 512:(f + 1) * 512])

                def jobs(sec):
                    n = N if sec.kind == "shared" else CAP
                    for b in range(2):
                        for f in range(sec.tiles):
                            k = b * sec.tiles + f
                            act.wait_ge(gu_full, sec.tile0 + k + 1)
                            act.activation(s[:, k % 2, 0:n], psG[:, k % 2, 0:n], ACT.Silu).then_inc(s_ready, 1)
                    if sec.kind == "expert" and not sec.last:
                        for b in range(2):
                            act.wait_ge(m.raw_loaded[b], sec.i * 32 + 64)
                            act.copy(m.rgu[:, b, :, 0, :], m.rgu_raw[:, b]).then_inc(w_hi, 1)
                    if sec.kind == "expert":
                        for b in range(2):
                            job = sec.job0 + b
                            act.wait_ge(down_full, job + 1)
                            at_least(act, eo_stored[b], sec.i * 32)
                            whole = len(SLOT_TILES) - 1
                            act.copy(eo[:, b, 0:whole, :], psD[:, b, 0:whole * P].rearrange("p (t d) -> p t d", t=whole))
                            rows = SLOT_TILES[-1][1]
                            ins = act.copy(eo[0:rows, b, whole, :], psD[0:rows, b, whole * P:(whole + 1) * P])
                            ins.then_inc(down_read, 1)

                def slots():
                    act.wait_ge(gap_ready, 1)
                    act.activation(gap[:, 1, :], gap[:, 0, :], ACT.Exp).then_inc(gap_exp, 1)
                    for f in range(XG_FILLS):
                        hi(X_XGT + f, xgT_hi[:, f * 512:(f + 1) * 512])

                sections(act, jobs, slots)

            @block.vector
            def _(dve):
                chain = Chain(dve, chained)
                C = lambda ins: chain.add(ins).wait()
                def normalise_rows(a, z):
                    for t in range(a, z):
                        last = dve.tensor_scalar(u[:, t, :], m.x[:, t, :], m.mean_var[:, t, 0:1], m.rstd[:, t:t + 1], ALU.subtract, ALU.mult)
                        if t % 4 == 3:
                            last.then_inc(u_ready, 1)

                def lo(n, done, dst, hi):
                    dve.wait_ge(hi_done, done)
                    dve.tensor_tensor(dst, psX[:, n % 2, :], hi.bitcast(F32), ALU.subtract).then_inc(x_done, 1)

                def lo_of_inputs(f):
                    part = slice(f * 512, (f + 1) * 512)
                    lo(X_UT + f, f + 1, uT[:, 1, part], uT[:, 0, part])

                late = RowStatistics(dve, chain, m, EARLY, B)
                normalise_rows(0, EARLY)
                dve.wait_ge(x_full, 1)
                C(dve.tensor_copy(rwT[:, 0, :], psX[:, 0, 0:E]))
                dve.tensor_tensor(rwT[:, 1, :], psX[:, 0, 0:E], rwT[:, 0, :].bitcast(F32), ALU.subtract).then_inc(x_done, 1)
                late.aggregate()
                late.guess()
                lo_of_inputs(0)
                late.step()
                lo_of_inputs(1)
                late.step()
                late.step()
                normalise_rows(EARLY, B)
                lo_of_inputs(2)
                lo_of_inputs(3)

                def logits_and_top():
                    C(dve.tensor_tensor(m.mean_var[:, :, 1], m.mean_var[:, :, 1], m.rstd[:], ALU.mult))
                    C(dve.tensor_tensor(m.mean_var[:, :, 1], m.mean_var[:, :, 1], m.rstd[:], ALU.mult))
                    inverse_root(dve, chain, rms[:], m.mean_var[:, :, 1], 1.1920929e-07, m.root_tmp)
                    dve.wait_ge(x_full, X_LOGITS + 1)
                    parts = psX[:, X_LOGITS % 2, :].rearrange("p (b h e) -> p b h e", h=2, e=E)
                    C(dve.tensor_copy(logits[:, :, :], parts[:, 0:B, 0, :]))
                    dve.tensor_tensor(logits[:, :, :], parts[:, 0:B, 1, :], logits[:, :, :], ALU.add).then_inc(x_done, 1)
                    dve.wait_ge(x_done, X_LOGITS + 1)
                    C(dve.tensor_tensor(logits[:, :, :], logits[:, :, :], rms[:].rearrange("p (b e) -> p b e", e=1).to_broadcast([P, B, E]), ALU.mult))
                    for t in range(B):
                        chain.add(dve.max(top[0][:, t, :], logits[:, t, :]))
                    chain.wait()

                def one_hot_of(c):
                    chain.add(dve.tensor_copy(chosen[:, c, :], index[:, :, 0])).wait()
                    if c == 0:
                        dve.wait_ge(consts, 2)
                    chain.add(dve.tensor_tensor(one_hot[:, c], iota[:].rearrange("p (b e) -> p b e", b=1).to_broadcast([P, B, E]),
                                                chosen[:, c, :].rearrange("p (b e) -> p b e", e=1).to_broadcast([P, B, E]), ALU.is_equal))
                    chain.wait()

                def first_choice():
                    for t in range(B):
                        chain.add(dve.max_index(index[:, t, :], top[0][:, t, :], logits[:, t, :]))
                    chain.wait()
                    one_hot_of(0)
                    C(dve.scalar_tensor_tensor(others[:, :, :], one_hot[:, 0], -3e38, logits[:, :, :], ALU.mult, ALU.add))

                def second_choice():
                    for t in range(B):
                        chain.add(dve.max(top[1][:, t, :], others[:, t, :]))
                    chain.wait()
                    for t in range(B):
                        chain.add(dve.max_index(index[:, t, :], top[1][:, t, :], others[:, t, :]))
                    dve.tensor_tensor(gap[:, 0, :], top[1][:, :, 0], top[0][:, :, 0], ALU.subtract).then_inc(gap_ready, 1)
                    chain.wait()

                def choose():
                    one_hot_of(1)
                    dve.tensor_tensor(mask[:, :, :], one_hot[:, 0], one_hot[:, 1], ALU.add).then_inc(mask_ready, 1)

                placed = psX[:, X_PLACE % 2, :]

                def counts_of_batches():
                    dve.wait_ge(x_full, X_PLACE + 1)
                    total = placed[:, B * E:2 * B * E].rearrange("p (b e) -> p b e", e=E)
                    chain.add(dve.memset(prefix[:, 0, 0:1, :], 0.0))
                    C(dve.tensor_copy(prefix[:, 0, 1:B, :], total[:, 0:B - 1, :]))
                    now, step = 0, 1
                    while step < B:
                        chain.add(dve.tensor_copy(prefix[:, 1 - now, 0:step, :], prefix[:, now, 0:step, :]))
                        C(dve.tensor_tensor(prefix[:, 1 - now, step:B, :], prefix[:, now, step:B, :], prefix[:, now, 0:B - step, :], ALU.add))
                        now, step = 1 - now, step * 2
                    return now

                def places(now):
                    within = placed[:, 0:B * E].rearrange("p (b e) -> p b e", e=E)
                    ins = dve.tensor_tensor(prefix[:, 1 - now], within, prefix[:, now], ALU.add)
                    ins.then_inc(x_done, 1)
                    dve.wait_ge(x_done, X_PLACE + 1)
                    for c in range(TOP):
                        chain.add(dve.tensor_tensor(place[:, c], one_hot[:, c], prefix[:, 1 - now], ALU.mult))
                    chain.wait()
                    C(dve.tensor_reduce(pos[:], place[:, :, :, :], AX_X, ALU.add))

                def slots_of_tokens():
                    chain.add(dve.tensor_scalar(valid[:], pos[:], float(CAP), None, ALU.is_lt))
                    C(dve.scalar_tensor_tensor(pos[:], chosen[:], float(CAP), pos[:], ALU.mult, ALU.add))
                    C(dve.scalar_tensor_tensor(pos[:], pos[:], float(-SLOTS), valid[:], ALU.add, ALU.mult))
                    dve.tensor_scalar(slot[:], pos[:], float(SLOTS), None, ALU.add).then_inc(slot_ready, 1)

                def weights():
                    dve.wait_ge(gap_exp, 1)
                    C(dve.tensor_scalar(weight[:, 0, :], gap[:, 1, :], 1.0, None, ALU.add))
                    C(dve.reciprocal(weight[:, 0, :], weight[:, 0, :]))
                    C(dve.tensor_tensor(weight[:, 1, :], gap[:, 1, :], weight[:, 0, :], ALU.mult))

                def combine(t, c):
                    return dve.scalar_tensor_tensor(m.x[:, t, :], picked[:, c, t, :], weight[:, c, t:t + 1],
                                                    m.x[:, t, :], ALU.mult, ALU.add)

                def combine_group(g):
                    dve.wait_ge(picked_in[g], 16 * TOP * 4)
                    dve.wait_ge(down_read, EX_ROUNDS * 2 + (8 if g == 3 else 6))
                    for c in range(TOP):
                        for t in range(4 * g, 4 * g + 4):
                            last = combine(t, c)
                            if c == 0:
                                chain.add(last)
                        if c == 0:
                            chain.wait()
                    last.then_inc(combined, 1)

                def jobs(sec):
                    n = N if sec.kind == "shared" else CAP
                    for b in range(2):
                        for f in range(sec.tiles):
                            k = b * sec.tiles + f
                            if sec.first and k == 0:
                                logits_and_top()
                            if sec.first and k == 1:
                                first_choice()
                            if sec.first and k == 2:
                                second_choice()
                            if sec.first and k == 3:
                                choose()
                            if sec.first and k == ROUTER_COUNT + 1:
                                now = counts_of_batches()
                            if sec.first and k == ROUTER_COUNT + 2:
                                places(now)
                                slots_of_tokens()
                            if sec.kind == "shared" and sec.part == 1 and sec.last and k in COMBINE_AT:
                                g = COMBINE_AT.index(k)
                                combine_group(g)
                            dve.wait_ge(s_ready, sec.tile0 + k + 1)
                            if f == 0:
                                at_least(dve, down_full, sec.job0 + (b - 1))
                            dst = a[:, b, f, :] if sec.kind == "shared" else ae[:, b, f, :]
                            dve.tensor_tensor(dst, s[:, k % 2, 0:n], psU[:, k % 2, 0:n], ALU.mult).then_inc(a_ready, 1)
                    if sec.kind == "expert" and not sec.last:
                        for b in range(2):
                            dve.wait_ge(w_hi, sec.i * 2 + b + 1)
                            dve.tensor_tensor(m.rgu[:, b, :, 1, :], m.rgu_raw[:, b], m.rgu[:, b, :, 0, :].bitcast(F32),
                                              ALU.subtract).then_inc(m.expert_split, 1)
                    if sec.kind == "shared":
                        for b in range(2):
                            dve.wait_ge(down_full, sec.job0 + b + 1)
                            dst = m.x[:, bass.ds((sec.item0 + b) * (N // P), N // P), :]
                            dve.tensor_tensor(dst, dst, psD[:, b, 0:N].rearrange("p (t d) -> p t d", t=N // P), ALU.add).then_inc(down_read, 1)

                def slots():
                    weights()
                    for f in range(XG_FILLS):
                        part = slice(f * 512, (f + 1) * 512)
                        lo(X_XGT + f, 4 + f + 1, xgT_lo[:, part], xgT_hi[:, part])

                sections(dve, jobs, slots)
                combine_group(3)



_INS = ["x", "ctx_1024", "L0_xattn_wq_w", "L0_xattn_wq_b", "L0_xattn_wk_w", "L0_xattn_wk_b", "L0_xattn_wv_w",
        "L0_xattn_wv_b", "L0_xattn_mk", "L0_xattn_mv", "L0_xattn_wo_w", "L0_xattn_wo_b", "L0_ffn_ln_gamma",
        "L0_ffn_ln_beta", "L0_ffn_fc1_q", "L0_ffn_fc1_scales", "L0_ffn_fc1_bias", "L0_ffn_fc2_q", "L0_ffn_fc2_scales",
        "L0_ffn_fc2_bias", "L1_xattn_Wq", "L1_xattn_bq", "L1_xattn_Wkv", "L1_xattn_bkv", "L1_xattn_Wo", "L1_xattn_bo",
        "L1_ffn_router_w", "L1_ffn_rg", "L1_ffn_ru", "L1_ffn_rd", "L1_ffn_sg", "L1_ffn_su", "L1_ffn_sd"]


def kernel(**inputs):
    import numpy as np
    import concourse.bacc as bacc
    from concourse.bass_utils import run_bass_kernel_spmd

    nc = bacc.Bacc("TRN2", target_bir_lowering=False, num_devices=1)
    arrays, tensors = {}, {}
    for name in _INS:
        a = np.ascontiguousarray(inputs[name])
        arrays[f"in_{name}"] = a
        tensors[name] = nc.dram_tensor(f"in_{name}", a.shape, mybir.dt.from_np(a.dtype), kind="ExternalInput").ap()
    out = nc.dram_tensor("out", inputs["x"].shape, F32, kind="ExternalOutput").ap()
    transformer(nc, tensors, out)
    return run_bass_kernel_spmd(nc, [arrays], core_ids=[0]).results[0]["out"]
```
